# Optimizing a Trainium2 kernel written in Bass

```python
import numpy as np
import jax
import jax.numpy as jnp

def _softmax(x, axis=-1):
    return jax.nn.softmax(x, axis=axis)

def _gelu(x):
    return jax.nn.gelu(x, approximate=True)

def _silu(x):
    return jax.nn.silu(x)

def _sigmoid(x):
    return jax.nn.sigmoid(x)

def _layernorm(x, axis=-1, eps=1e-05):
    m = jnp.mean(x, axis=axis, keepdims=True)
    v = jnp.var(x, axis=axis, keepdims=True)
    return (x - m) / jnp.sqrt(v + eps)

def _scatter_add(tgt, idx, src, axis=0):
    return tgt.at[idx].add(src)

def _segment_sum(src, seg, n):
    return jax.ops.segment_sum(src, seg, n)
kernel_name = 'mk_sandwich_d2_jaxref_r8_0930cc'

def setup_inputs(seed: int=0):
    np.random.seed(seed)
    _w = jnp.asarray

    def _L0_attn_setup():
        import jax, jax.numpy as jnp
        import numpy as np
        D_MODEL = 128
        D_STATE = 64
        D_CONV = 4
        EXPAND = 2
        HEADDIM = 64
        NGROUPS = 1
        D_INNER = EXPAND * D_MODEL
        NHEADS = D_INNER // HEADDIM
        CONV_DIM = D_INNER + 2 * NGROUPS * D_STATE
        D_IN_PROJ = 2 * D_INNER + 2 * NGROUPS * D_STATE + NHEADS
        BATCH, SEQLEN = (2, 512)
        CHUNK = 64
        LN_EPS = 1e-05
        RMS_EPS = 1e-05

        def _segsum(a):
            q = a.shape[-1]
            cs = jnp.cumsum(a, axis=-1)
            seg = cs[..., :, None] - cs[..., None, :]
            mask = jnp.tril(jnp.ones((q, q), dtype=bool))
            return jnp.where(mask, seg, -jnp.inf)

        def _ssd(xdt, Adt, Bm, Cm):
            b, l, h, p = xdt.shape
            c = l // CHUNK
            X = xdt.reshape(b, c, CHUNK, h, p)
            A = Adt.reshape(b, c, CHUNK, h).transpose(0, 3, 1, 2)
            Bq = Bm.reshape(b, c, CHUNK, -1)
            Cq = Cm.reshape(b, c, CHUNK, -1)
            A_cum = jnp.cumsum(A, -1)
            Lmat = jnp.exp(_segsum(A))
            Y_diag = jnp.einsum('bcln,bcsn,bhcls,bcshp->bclhp', Cq, Bq, Lmat, X)
            decay_states = jnp.exp(A_cum[..., -1:] - A_cum)
            states = jnp.einsum('bcln,bhcl,bclhp->bchpn', Bq, decay_states, X)
            chunk_decay = jnp.exp(A_cum[..., -1])

            def step(hprev, inp):
                s, dec = inp
                return (dec[..., None, None] * hprev + s, hprev)
            h0 = jnp.zeros((b, h, p, states.shape[-1]), xdt.dtype)
            _, prev = jax.lax.scan(step, h0, (jnp.moveaxis(states, 1, 0), jnp.moveaxis(chunk_decay, 2, 0)))
            prev = jnp.moveaxis(prev, 0, 1)
            Y_off = jnp.einsum('bcln,bchpn,bhcl->bclhp', Cq, prev, jnp.exp(A_cum))
            return (Y_diag + Y_off).reshape(b, l, h, p)
        key = jax.random.key(seed)
        ks = jax.random.split(key, 8)
        dt = jnp.exp(jax.random.uniform(ks[3], (NHEADS,)) * (np.log(0.1) - np.log(0.001)) + np.log(0.001))
        dt_bias = dt + jnp.log(-jnp.expm1(-dt))
        return {'x': jax.random.normal(ks[0], (BATCH, SEQLEN, D_MODEL), jnp.float32), 'ln_w': jnp.ones((D_MODEL,), jnp.float32), 'ln_b': jnp.zeros((D_MODEL,), jnp.float32), 'in_proj_w': 0.02 * jax.random.normal(ks[1], (D_IN_PROJ, D_MODEL), jnp.float32), 'conv_w': 0.2 * jax.random.normal(ks[2], (CONV_DIM, 1, D_CONV), jnp.float32), 'conv_b': jnp.zeros((CONV_DIM,), jnp.float32), 'dt_bias': dt_bias, 'A_log': jnp.log(1.0 + 15.0 * jax.random.uniform(ks[4], (NHEADS,), jnp.float32)), 'D_skip': jnp.ones((NHEADS,), jnp.float32), 'norm_w': jnp.ones((D_INNER,), jnp.float32), 'out_proj_w': 0.02 * jax.random.normal(ks[5], (D_MODEL, D_INNER), jnp.float32)}
    _L0_attn_in = _L0_attn_setup()

    def _L0_ffn_setup():
        import jax, jax.numpy as jnp
        import numpy as np
        DIM = 128
        DEPTH = 2
        HEADS = 8
        DIM_HEAD = 64
        WINDOW = 64
        INNER = HEADS * DIM_HEAD
        HID = int(DIM * 4 * 2 / 3)
        B, N = (2, 1024)
        QK_SCALE = 8.0

        def shift_token(t):
            t1, t2 = jnp.split(t, 2, axis=-1)
            t2 = jnp.pad(t2, ((0, 0), (1, 0), (0, 0)))[:, :-1]
            return jnp.concatenate([t1, t2], axis=-1)

        def l2norm(t):
            return t / jnp.clip(jnp.linalg.norm(t, axis=-1, keepdims=True), 1e-12)

        def rotate_half(x):
            x1, x2 = jnp.split(x, 2, axis=-1)
            return jnp.concatenate([-x2, x1], axis=-1)

        def rotary_xpos(q, k):
            n = q.shape[-2]
            half_idx = jnp.arange(0, DIM_HEAD, 2, dtype=jnp.float32)
            inv_freq = 1.0 / 10000.0 ** (half_idx / DIM_HEAD)
            t = jnp.arange(n, dtype=jnp.float32)
            freqs = t[:, None] * inv_freq[None, :]
            freqs = jnp.concatenate([freqs, freqs], axis=-1)
            base = (half_idx + 0.4 * DIM_HEAD) / (1.4 * DIM_HEAD)
            power = (t - n // 2) / float(WINDOW // 2)
            scale = base[None, :] ** power[:, None]
            scale = jnp.concatenate([scale, scale], axis=-1)
            cos, sin = (jnp.cos(freqs), jnp.sin(freqs))
            q = q * cos * scale + rotate_half(q) * sin * scale
            k = k * cos / scale + rotate_half(k) * sin / scale
            return (q, k)

        def local_attention(q, k, v):
            b, h, n, d = q.shape
            w = n // WINDOW
            bq = q.reshape(b, h, w, WINDOW, d) * QK_SCALE
            bk = k.reshape(b, h, w, WINDOW, d)
            bv = v.reshape(b, h, w, WINDOW, d)

            def look_around(t):
                p = jnp.pad(t, ((0, 0), (0, 0), (1, 0), (0, 0), (0, 0)))
                return jnp.concatenate([p[:, :, :w], p[:, :, 1:]], axis=3)
            bk, bv = (look_around(bk), look_around(bv))
            bt = jnp.arange(n).reshape(w, WINDOW)
            btp = jnp.pad(bt, ((1, 0), (0, 0)), constant_values=-1)
            btk = jnp.concatenate([btp[:w], btp[1:]], axis=1)
            sim = jnp.einsum('bhwid,bhwjd->bhwij', bq, bk)
            i = bt[:, :, None]
            j = btk[:, None, :]
            mask = (i < j) | (i > j + WINDOW) | (j == -1)
            sim = jnp.where(mask, -jnp.finfo(sim.dtype).max, sim)
            attn = jax.nn.softmax(sim, axis=-1)
            out = jnp.einsum('bhwij,bhwjd->bhwid', attn, bv)
            return out.reshape(b, h, n, d)

        def _layer(x, wqkv, qs, ksc, wo, lg, lb, w1, b1, w2, b2):
            b, n, _ = x.shape
            h = shift_token(x)
            qkv = h @ wqkv
            q, k, v = jnp.split(qkv, 3, axis=-1)
            to_heads = lambda t: t.reshape(b, n, HEADS, DIM_HEAD).transpose(0, 2, 1, 3)
            q, k, v = (to_heads(q), to_heads(k), to_heads(v))
            q = l2norm(q) * qs
            k = l2norm(k) * ksc
            q, k = rotary_xpos(q, k)
            o = local_attention(q, k, v)
            o = o.transpose(0, 2, 1, 3).reshape(b, n, INNER)
            x = x + o @ wo
            h = shift_token(x)
            mu = h.mean(-1, keepdims=True)
            var = h.var(-1, keepdims=True)
            h = (h - mu) / jnp.sqrt(var + 1e-05) * lg + lb
            h = h @ w1 + b1
            a, g = jnp.split(h, 2, axis=-1)
            h = a * jax.nn.gelu(g, approximate=False)
            x = x + h @ w2 + b2
            return x
        key = jax.random.key(seed)
        ks = jax.random.split(key, 6)
        return {'x': jax.random.normal(ks[0], (B, N, DIM), jnp.float32), 'wqkv': jax.random.normal(ks[1], (DEPTH, DIM, 3 * INNER), jnp.float32) * 0.02, 'q_scale': jnp.ones((DEPTH, DIM_HEAD), jnp.float32), 'k_scale': jnp.ones((DEPTH, DIM_HEAD), jnp.float32), 'wo': jax.random.normal(ks[2], (DEPTH, INNER, DIM), jnp.float32) * 0.02, 'ln_g': jnp.ones((DEPTH, DIM), jnp.float32), 'ln_b': jnp.zeros((DEPTH, DIM), jnp.float32), 'w1': jax.random.normal(ks[3], (DEPTH, DIM, 2 * HID), jnp.float32) * 0.02, 'b1': jnp.zeros((DEPTH, 2 * HID), jnp.float32), 'w2': jax.random.normal(ks[4], (DEPTH, HID, DIM), jnp.float32) * 0.02, 'b2': jnp.zeros((DEPTH, DIM), jnp.float32)}
    _L0_ffn_in = _L0_ffn_setup()

    def _L1_attn_setup():
        import jax, jax.numpy as jnp
        import numpy as np
        D_MODEL = 128
        D_STATE = 16
        D_CONV = 4
        EXPAND = 2
        D_INNER = D_MODEL * EXPAND

        def soft_clamp(x, lo, hi, sharp):
            c = (hi + lo) / 2.0
            r = (hi - lo) / 2.0
            return jnp.tanh((x - c) / (r + 1e-08) * sharp) / sharp * r + c
        key = jax.random.key(seed)
        ks = jax.random.split(key, 9)
        B, L = (2, 128)
        x = jax.random.normal(ks[0], (B, L, D_MODEL), jnp.float32)
        norm_w = jnp.ones((D_MODEL,), jnp.float32)
        W_in = jax.random.normal(ks[1], (2 * D_INNER, D_MODEL), jnp.float32) * 0.02
        conv_w = jax.random.normal(ks[2], (D_INNER, 1, D_CONV), jnp.float32) * 0.02
        conv_b = jnp.zeros((D_INNER,), jnp.float32)
        W_dt = jax.random.normal(ks[3], (D_INNER, D_INNER), jnp.float32) * 0.02
        b_dt = jnp.full((D_INNER,), -2.0, jnp.float32)
        W_B = jax.random.normal(ks[4], (D_STATE, D_INNER), jnp.float32) * 0.02
        W_C = jax.random.normal(ks[5], (D_STATE, D_INNER), jnp.float32) * 0.02
        A_log = jax.random.normal(ks[6], (D_INNER, D_STATE), jnp.float32) * 0.1
        D_param = jnp.full((D_INNER,), 0.1, jnp.float32)
        W_out = jax.random.normal(ks[7], (D_MODEL, D_INNER), jnp.float32) * 0.02
        residual_scale = jnp.asarray(0.3, jnp.float32)
        return dict(x=x, norm_w=norm_w, W_in=W_in, conv_w=conv_w, conv_b=conv_b, W_dt=W_dt, b_dt=b_dt, W_B=W_B, W_C=W_C, A_log=A_log, D_param=D_param, W_out=W_out, residual_scale=residual_scale)
    _L1_attn_in = _L1_attn_setup()

    def _L1_ffn_setup():
        import jax, jax.numpy as jnp
        import numpy as np
        TOP_K = 2
        key = jax.random.key(seed)
        k1, k2, k3, k4 = jax.random.split(key, 4)
        B, S, D = (2, 256, 128)
        E, W = (8, 128)
        x = jax.random.normal(k1, (B, S, D), dtype=jnp.float32)
        router_w = jax.random.normal(k2, (E, D), dtype=jnp.float32) * 0.02
        w1 = jax.random.normal(k3, (D, E * W), dtype=jnp.float32) * 0.02
        w2 = jax.random.normal(k4, (E * W, D), dtype=jnp.float32) * 0.02
        return {'x': x, 'router_w': router_w, 'w1': w1, 'w2': w2}
    _L1_ffn_in = _L1_ffn_setup()
    _d = {'L0_attn_x': _L0_attn_in['x'], 'L0_attn_ln_w': _L0_attn_in['ln_w'], 'L0_attn_ln_b': _L0_attn_in['ln_b'], 'L0_attn_in_proj_w': _L0_attn_in['in_proj_w'], 'L0_attn_conv_w': _L0_attn_in['conv_w'], 'L0_attn_conv_b': _L0_attn_in['conv_b'], 'L0_attn_dt_bias': _L0_attn_in['dt_bias'], 'L0_attn_A_log': _L0_attn_in['A_log'], 'L0_attn_D_skip': _L0_attn_in['D_skip'], 'L0_attn_norm_w': _L0_attn_in['norm_w'], 'L0_attn_out_proj_w': _L0_attn_in['out_proj_w'], 'L0_ffn_wqkv': _L0_ffn_in['wqkv'], 'L0_ffn_q_scale': _L0_ffn_in['q_scale'], 'L0_ffn_k_scale': _L0_ffn_in['k_scale'], 'L0_ffn_wo': _L0_ffn_in['wo'], 'L0_ffn_ln_g': _L0_ffn_in['ln_g'], 'L0_ffn_ln_b': _L0_ffn_in['ln_b'], 'L0_ffn_w1': _L0_ffn_in['w1'], 'L0_ffn_b1': _L0_ffn_in['b1'], 'L0_ffn_w2': _L0_ffn_in['w2'], 'L0_ffn_b2': _L0_ffn_in['b2'], 'L1_attn_norm_w': _L1_attn_in['norm_w'], 'L1_attn_W_in': _L1_attn_in['W_in'], 'L1_attn_conv_w': _L1_attn_in['conv_w'], 'L1_attn_conv_b': _L1_attn_in['conv_b'], 'L1_attn_W_dt': _L1_attn_in['W_dt'], 'L1_attn_b_dt': _L1_attn_in['b_dt'], 'L1_attn_W_B': _L1_attn_in['W_B'], 'L1_attn_W_C': _L1_attn_in['W_C'], 'L1_attn_A_log': _L1_attn_in['A_log'], 'L1_attn_D_param': _L1_attn_in['D_param'], 'L1_attn_W_out': _L1_attn_in['W_out'], 'L1_attn_residual_scale': _L1_attn_in['residual_scale'], 'L1_ffn_router_w': _L1_ffn_in['router_w'], 'L1_ffn_w1': _L1_ffn_in['w1'], 'L1_ffn_w2': _L1_ffn_in['w2']}
    _x0 = _d['L0_attn_x']
    _d['L0_attn_x'] = jax.random.normal(jax.random.fold_in(jax.random.key(seed), 1), (8, 1024, 128), dtype=_x0.dtype)
    del _x0
    return _d

def reference(L0_attn_x, L0_attn_ln_w, L0_attn_ln_b, L0_attn_in_proj_w, L0_attn_conv_w, L0_attn_conv_b, L0_attn_dt_bias, L0_attn_A_log, L0_attn_D_skip, L0_attn_norm_w, L0_attn_out_proj_w, L0_ffn_wqkv, L0_ffn_q_scale, L0_ffn_k_scale, L0_ffn_wo, L0_ffn_ln_g, L0_ffn_ln_b, L0_ffn_w1, L0_ffn_b1, L0_ffn_w2, L0_ffn_b2, L1_attn_norm_w, L1_attn_W_in, L1_attn_conv_w, L1_attn_conv_b, L1_attn_W_dt, L1_attn_b_dt, L1_attn_W_B, L1_attn_W_C, L1_attn_A_log, L1_attn_D_param, L1_attn_W_out, L1_attn_residual_scale, L1_ffn_router_w, L1_ffn_w1, L1_ffn_w2):

    def _L0_attn_ref(x, ln_w, ln_b, in_proj_w, conv_w, conv_b, dt_bias, A_log, D_skip, norm_w, out_proj_w):
        import jax, jax.numpy as jnp
        import numpy as np
        D_MODEL = 128
        D_STATE = 64
        D_CONV = 4
        EXPAND = 2
        HEADDIM = 64
        NGROUPS = 1
        D_INNER = EXPAND * D_MODEL
        NHEADS = D_INNER // HEADDIM
        CONV_DIM = D_INNER + 2 * NGROUPS * D_STATE
        D_IN_PROJ = 2 * D_INNER + 2 * NGROUPS * D_STATE + NHEADS
        BATCH, SEQLEN = (2, 512)
        CHUNK = 64
        LN_EPS = 1e-05
        RMS_EPS = 1e-05

        def _segsum(a):
            q = a.shape[-1]
            cs = jnp.cumsum(a, axis=-1)
            seg = cs[..., :, None] - cs[..., None, :]
            mask = jnp.tril(jnp.ones((q, q), dtype=bool))
            return jnp.where(mask, seg, -jnp.inf)

        def _ssd(xdt, Adt, Bm, Cm):
            b, l, h, p = xdt.shape
            c = l // CHUNK
            X = xdt.reshape(b, c, CHUNK, h, p)
            A = Adt.reshape(b, c, CHUNK, h).transpose(0, 3, 1, 2)
            Bq = Bm.reshape(b, c, CHUNK, -1)
            Cq = Cm.reshape(b, c, CHUNK, -1)
            A_cum = jnp.cumsum(A, -1)
            Lmat = jnp.exp(_segsum(A))
            Y_diag = jnp.einsum('bcln,bcsn,bhcls,bcshp->bclhp', Cq, Bq, Lmat, X)
            decay_states = jnp.exp(A_cum[..., -1:] - A_cum)
            states = jnp.einsum('bcln,bhcl,bclhp->bchpn', Bq, decay_states, X)
            chunk_decay = jnp.exp(A_cum[..., -1])

            def step(hprev, inp):
                s, dec = inp
                return (dec[..., None, None] * hprev + s, hprev)
            h0 = jnp.zeros((b, h, p, states.shape[-1]), xdt.dtype)
            _, prev = jax.lax.scan(step, h0, (jnp.moveaxis(states, 1, 0), jnp.moveaxis(chunk_decay, 2, 0)))
            prev = jnp.moveaxis(prev, 0, 1)
            Y_off = jnp.einsum('bcln,bchpn,bhcl->bclhp', Cq, prev, jnp.exp(A_cum))
            return (Y_diag + Y_off).reshape(b, l, h, p)
        b, l, _ = x.shape
        mu = jnp.mean(x, -1, keepdims=True)
        var = jnp.mean(jnp.square(x - mu), -1, keepdims=True)
        xn = (x - mu) * jax.lax.rsqrt(var + LN_EPS) * ln_w + ln_b
        zxbcdt = xn @ in_proj_w.T
        z = zxbcdt[..., :D_INNER]
        xBC = zxbcdt[..., D_INNER:D_INNER + CONV_DIM]
        dt = zxbcdt[..., D_INNER + CONV_DIM:]
        xBC_t = jnp.transpose(xBC, (0, 2, 1))
        xBC_c = jax.lax.conv_general_dilated(xBC_t, conv_w, (1,), [(D_CONV - 1, 0)], dimension_numbers=('NCH', 'OIH', 'NCH'), feature_group_count=CONV_DIM)
        xBC = jax.nn.silu(jnp.transpose(xBC_c, (0, 2, 1)) + conv_b)
        xs = xBC[..., :D_INNER].reshape(b, l, NHEADS, HEADDIM)
        Bm = xBC[..., D_INNER:D_INNER + D_STATE]
        Cm = xBC[..., D_INNER + D_STATE:]
        dt = jax.nn.softplus(dt + dt_bias)
        A = -jnp.exp(A_log)
        y = _ssd(xs * dt[..., None], dt * A, Bm, Cm)
        y = y + D_skip[None, None, :, None] * xs
        y = y.reshape(b, l, D_INNER)
        yg = y * jax.nn.silu(z)
        yg = yg * jax.lax.rsqrt(jnp.mean(jnp.square(yg), -1, keepdims=True) + RMS_EPS) * norm_w
        return x + yg @ out_proj_w.T

    def _L0_ffn_ref(x, wqkv, q_scale, k_scale, wo, ln_g, ln_b, w1, b1, w2, b2):
        import jax, jax.numpy as jnp
        import numpy as np
        DIM = 128
        DEPTH = 2
        HEADS = 8
        DIM_HEAD = 64
        WINDOW = 64
        INNER = HEADS * DIM_HEAD
        HID = int(DIM * 4 * 2 / 3)
        B, N = (2, 1024)
        QK_SCALE = 8.0

        def shift_token(t):
            t1, t2 = jnp.split(t, 2, axis=-1)
            t2 = jnp.pad(t2, ((0, 0), (1, 0), (0, 0)))[:, :-1]
            return jnp.concatenate([t1, t2], axis=-1)

        def l2norm(t):
            return t / jnp.clip(jnp.linalg.norm(t, axis=-1, keepdims=True), 1e-12)

        def rotate_half(x):
            x1, x2 = jnp.split(x, 2, axis=-1)
            return jnp.concatenate([-x2, x1], axis=-1)

        def rotary_xpos(q, k):
            n = q.shape[-2]
            half_idx = jnp.arange(0, DIM_HEAD, 2, dtype=jnp.float32)
            inv_freq = 1.0 / 10000.0 ** (half_idx / DIM_HEAD)
            t = jnp.arange(n, dtype=jnp.float32)
            freqs = t[:, None] * inv_freq[None, :]
            freqs = jnp.concatenate([freqs, freqs], axis=-1)
            base = (half_idx + 0.4 * DIM_HEAD) / (1.4 * DIM_HEAD)
            power = (t - n // 2) / float(WINDOW // 2)
            scale = base[None, :] ** power[:, None]
            scale = jnp.concatenate([scale, scale], axis=-1)
            cos, sin = (jnp.cos(freqs), jnp.sin(freqs))
            q = q * cos * scale + rotate_half(q) * sin * scale
            k = k * cos / scale + rotate_half(k) * sin / scale
            return (q, k)

        def local_attention(q, k, v):
            b, h, n, d = q.shape
            w = n // WINDOW
            bq = q.reshape(b, h, w, WINDOW, d) * QK_SCALE
            bk = k.reshape(b, h, w, WINDOW, d)
            bv = v.reshape(b, h, w, WINDOW, d)

            def look_around(t):
                p = jnp.pad(t, ((0, 0), (0, 0), (1, 0), (0, 0), (0, 0)))
                return jnp.concatenate([p[:, :, :w], p[:, :, 1:]], axis=3)
            bk, bv = (look_around(bk), look_around(bv))
            bt = jnp.arange(n).reshape(w, WINDOW)
            btp = jnp.pad(bt, ((1, 0), (0, 0)), constant_values=-1)
            btk = jnp.concatenate([btp[:w], btp[1:]], axis=1)
            sim = jnp.einsum('bhwid,bhwjd->bhwij', bq, bk)
            i = bt[:, :, None]
            j = btk[:, None, :]
            mask = (i < j) | (i > j + WINDOW) | (j == -1)
            sim = jnp.where(mask, -jnp.finfo(sim.dtype).max, sim)
            attn = jax.nn.softmax(sim, axis=-1)
            out = jnp.einsum('bhwij,bhwjd->bhwid', attn, bv)
            return out.reshape(b, h, n, d)

        def _layer(x, wqkv, qs, ksc, wo, lg, lb, w1, b1, w2, b2):
            b, n, _ = x.shape
            h = shift_token(x)
            qkv = h @ wqkv
            q, k, v = jnp.split(qkv, 3, axis=-1)
            to_heads = lambda t: t.reshape(b, n, HEADS, DIM_HEAD).transpose(0, 2, 1, 3)
            q, k, v = (to_heads(q), to_heads(k), to_heads(v))
            q = l2norm(q) * qs
            k = l2norm(k) * ksc
            q, k = rotary_xpos(q, k)
            o = local_attention(q, k, v)
            o = o.transpose(0, 2, 1, 3).reshape(b, n, INNER)
            x = x + o @ wo
            h = shift_token(x)
            mu = h.mean(-1, keepdims=True)
            var = h.var(-1, keepdims=True)
            h = (h - mu) / jnp.sqrt(var + 1e-05) * lg + lb
            h = h @ w1 + b1
            a, g = jnp.split(h, 2, axis=-1)
            h = a * jax.nn.gelu(g, approximate=False)
            x = x + h @ w2 + b2
            return x
        for l in range(DEPTH):
            x = _layer(x, wqkv[l], q_scale[l], k_scale[l], wo[l], ln_g[l], ln_b[l], w1[l], b1[l], w2[l], b2[l])
        return x

    def _L1_attn_ref(x, norm_w, W_in, conv_w, conv_b, W_dt, b_dt, W_B, W_C, A_log, D_param, W_out, residual_scale):
        import jax, jax.numpy as jnp
        import numpy as np
        D_MODEL = 128
        D_STATE = 16
        D_CONV = 4
        EXPAND = 2
        D_INNER = D_MODEL * EXPAND

        def soft_clamp(x, lo, hi, sharp):
            c = (hi + lo) / 2.0
            r = (hi - lo) / 2.0
            return jnp.tanh((x - c) / (r + 1e-08) * sharp) / sharp * r + c
        B, L, _ = x.shape
        var = jnp.mean(x * x, axis=-1, keepdims=True)
        xn = x * jax.lax.rsqrt(var + 1e-06) * norm_w
        proj = xn @ W_in.T
        x_branch, gate = (proj[..., :D_INNER], proj[..., D_INNER:])
        xc = jax.lax.conv_general_dilated(jnp.swapaxes(x_branch, 1, 2), conv_w, (1,), [(D_CONV - 1, 0)], dimension_numbers=('NCH', 'OIH', 'NCH'), feature_group_count=D_INNER)
        xc = xc + conv_b[None, :, None]
        xc = jnp.swapaxes(xc, 1, 2)
        xc = xc * jax.nn.sigmoid(xc)
        dt = soft_clamp(jax.nn.softplus(xc @ W_dt.T + b_dt), 0.001, 0.1, 0.5)
        Bp = xc @ W_B.T
        Cp = xc @ W_C.T
        A = -jnp.exp(soft_clamp(A_log, -5.0, 5.0, 0.5))
        dt_A = soft_clamp(dt[..., None] * A[None, None], -8.0, 8.0, 0.5)
        dA = jnp.exp(dt_A)
        dB = dt[..., None] * Bp[:, :, None, :]
        h0 = jnp.zeros((B, D_INNER, D_STATE), jnp.float32)

        def step(h, inp):
            dA_t, dB_t, x_t, C_t, t = inp
            h = h * dA_t + dB_t * x_t[:, :, None]
            nrm = jnp.sqrt(jnp.sum(h * h, axis=(1, 2), keepdims=True))
            fac = jnp.minimum(20.0 / (nrm + 1e-08), 1.0)
            h = jnp.where(t % 10 == 0, h * fac, h)
            y = jnp.einsum('bdn,bn->bd', h, C_t) + D_param * x_t
            return (h, y)
        xs = (jnp.swapaxes(dA, 0, 1), jnp.swapaxes(dB, 0, 1), jnp.swapaxes(xc, 0, 1), jnp.swapaxes(Cp, 0, 1), jnp.arange(L))
        _, ys = jax.lax.scan(step, h0, xs)
        x_ssm = jnp.swapaxes(ys, 0, 1)
        x_out = x_ssm * (gate * jax.nn.sigmoid(gate)) @ W_out.T
        scale = jax.nn.sigmoid(residual_scale) * 0.5
        return x + scale * x_out

    def _L1_ffn_ref(x, router_w, w1, w2):
        import jax, jax.numpy as jnp
        import numpy as np
        TOP_K = 2
        B, S, D = x.shape
        E = router_w.shape[0]
        W = w1.shape[1] // E
        T = B * S
        xf = x.reshape(T, D)
        router_logits = jnp.einsum('td,ed->te', xf, router_w)
        router_probs = jax.nn.sigmoid(router_logits.astype(jnp.float32))
        top_w, sel = jax.lax.top_k(router_probs, TOP_K)
        top_w = top_w / (top_w.sum(axis=-1, keepdims=True) + 1e-20)
        top_w = top_w.astype(x.dtype)
        W1e = w1.reshape(D, E, W).transpose(1, 0, 2)
        W2e = w2.reshape(E, W, D)
        h = jnp.einsum('td,edw->etw', xf, W1e)
        a = jnp.square(jax.nn.relu(h))
        y = jnp.einsum('etw,ewd->etd', a, W2e)
        cw = jnp.zeros((T, E), dtype=x.dtype).at[jnp.arange(T)[:, None], sel].set(top_w)
        out = jnp.einsum('etd,te->td', y, cw)
        return out.reshape(B, S, D)
    x = L0_attn_x
    x = x + _layernorm(_L0_attn_ref(_layernorm(x, axis=-1), L0_attn_ln_w, L0_attn_ln_b, L0_attn_in_proj_w, L0_attn_conv_w, L0_attn_conv_b, L0_attn_dt_bias, L0_attn_A_log, L0_attn_D_skip, L0_attn_norm_w, L0_attn_out_proj_w), axis=-1)
    x = x + _layernorm(_L0_ffn_ref(_layernorm(x, axis=-1), L0_ffn_wqkv, L0_ffn_q_scale, L0_ffn_k_scale, L0_ffn_wo, L0_ffn_ln_g, L0_ffn_ln_b, L0_ffn_w1, L0_ffn_b1, L0_ffn_w2, L0_ffn_b2), axis=-1)
    x = x + _layernorm(_L1_attn_ref(_layernorm(x, axis=-1), L1_attn_norm_w, L1_attn_W_in, L1_attn_conv_w, L1_attn_conv_b, L1_attn_W_dt, L1_attn_b_dt, L1_attn_W_B, L1_attn_W_C, L1_attn_A_log, L1_attn_D_param, L1_attn_W_out, L1_attn_residual_scale), axis=-1)
    x = x + _layernorm(_L1_ffn_ref(_layernorm(x, axis=-1), L1_ffn_router_w, L1_ffn_w1, L1_ffn_w2), axis=-1)
    return x

_drawn_inputs = setup_inputs


def setup_inputs(seed=0):
    import zlib

    import numpy as np

    out = dict(_drawn_inputs(seed))
    spreads = {'L0_attn_ln_w': (1.0, 0.2),
     'L0_attn_ln_b': (0.0, 0.1),
     'L0_attn_conv_b': (0.0, 0.1),
     'L0_attn_D_skip': (1.0, 0.2),
     'L0_attn_norm_w': (1.0, 0.2),
     'L0_ffn_q_scale': (1.0, 0.6),
     'L0_ffn_k_scale': (1.0, 0.6),
     'L0_ffn_ln_g': (1.0, 0.6),
     'L0_ffn_ln_b': (0.0, 0.8),
     'L0_ffn_b1': (0.0, 0.541),
     'L0_ffn_b2': (0.0, 0.1),
     'L1_attn_norm_w': (1.0, 0.6),
     'L1_attn_conv_b': (0.0, 0.8),
     'L1_attn_b_dt': (-2.0, 0.6),
     'L1_attn_D_param': (0.10000000149011612, 0.6)}
    factors = {'L0_attn_dt_bias': 8.0,
     'L0_attn_A_log': 8.0,
     'L0_ffn_w1': 3.136,
     'L0_ffn_w2': 3.378,
     'L1_attn_W_in': 8.0,
     'L1_attn_conv_w': 8.0,
     'L1_attn_W_dt': 8.0,
     'L1_attn_W_B': 8.0,
     'L1_attn_W_C': 8.0,
     'L1_attn_A_log': 8.0,
     'L1_attn_W_out': 8.0}
    for name, (base, spread) in spreads.items():
        noise = np.random.default_rng([zlib.crc32(name.encode()), seed]).standard_normal(out[name].shape)
        drawn = base * np.exp(spread * noise) if base else spread * noise
        out[name] = jnp.asarray(drawn.astype(out[name].dtype))
    for name, factor in factors.items():
        out[name] = (out[name] * factor).astype(out[name].dtype)
    return out
```

```python
from contextlib import ExitStack

import concourse.bass as bass
from concourse import mybir

F32 = mybir.dt.float32
BF16 = mybir.dt.bfloat16
U32 = mybir.dt.uint32
ALU = mybir.AluOpType
ACT = mybir.ActivationFunctionType
AX_X = mybir.AxisListType.X
AX_XY = mybir.AxisListType.XY

P = 128
D = 128
B = 8
L = 1024
C = L // P
MASKED = -1.0e30


class Steps:

    def __init__(self, nc, name, per):
        self.sem, self.name, self.per, self.n = nc.alloc_semaphore(name), name, per, 0

    def mark(self, ins):
        ins.then_inc(self.sem, 1)
        self.n += 1
        return self.n

    def need(self, eng, turn, n):
        eng.wait_ge(self.sem, turn * self.per + (1 + n))

    def before(self, eng, turn, back, n):
        eng.wait_ge(self.sem, turn * self.per + (1 + n - back * self.per))

    def close(self):
        assert self.n == self.per, (self.name, self.n, self.per)
        self.n = 0


def wide(ap, at, shape):
    return ap.unsqueeze(at).to_broadcast(shape)




def mamba2_layer(nc, x_in, x_out, w, const):
    H, HD, NS, DI = 4, 64, 64, 256
    TAPS = 4
    XB = DI + NS
    with ExitStack() as ctx:
        def sb(name, shape, dt=F32):
            return ctx.enter_context(nc.sbuf_tensor("a_" + name, shape, dt))

        def steps(name, per):
            return Steps(nc, "a_" + name, per)

        bank = [ctx.enter_context(nc.psum_tensor(f"a_bank{n}", [P, 512], F32)) for n in range(8)]
        w_in = sb("w_in", [D, 2 * DI + 2 * NS + H])
        taps = sb("taps", [P, TAPS, DI + 2 * NS])
        w_zdt = sb("w_zdt", [D, DI + H])
        w_conv = sb("w_conv", [D, TAPS, DI + 2 * NS])
        conv_b_row = sb("conv_b_row", [1, XB])
        conv_b_col = sb("conv_b_col", [NS, 2])
        ln_wb = sb("ln_wb", [D, 2])
        dt_bias = sb("dt_bias", [P, H])
        a_neg = sb("a_neg", [P, H])
        d_skip = sb("d_skip", [P, H])
        norm_w = sb("norm_w", [P, 2])
        w_out = sb("w_out", [P, 2, D])
        ident = sb("ident", [P, P])
        ident_b = sb("ident_b", [P, P], BF16)
        upper = sb("upper", [P, P])
        mask = sb("mask", [P, P], BF16)
        ones = sb("ones", [P, P])
        minus_half = sb("minus_half", [P, C])
        xt = sb("xt", [P, 2, C, D])
        xn0 = sb("xn0", [P, C, D])
        xn = sb("xn", [P, C, D])
        stat = sb("stat", [P, C, 6])
        mean = sb("mean", [P, C])
        apart = sb("apart", [P, C])
        var = sb("var", [P, C])
        rstd = sb("rstd", [P, C])
        xnT = sb("xnT", [D, TAPS - 1 + L])
        bT = sb("bT", [NS, L])
        cT = sb("cT", [NS, L])
        xsb = sb("xsb", [P, C, XB])
        zs = sb("zs", [P, C, DI])
        dt_raw = sb("dt_raw", [P, C, H])
        dt_abs = sb("dt_abs", [P, C, H])
        dt_exp = sb("dt_exp", [P, C, H])
        dt = sb("dt", [P, C, H])
        adt = sb("adt", [P, C, H])
        cs_neg = sb("cs_neg", [P, C, H])
        rest = sb("rest", [P, C, H])
        e_cs = sb("e_cs", [P, C, H])
        e_tot = sb("e_tot", [P, C, H])
        e_rest = sb("e_rest", [P, C, H])
        decay = sb("decay", [P, 2, H, P])
        gated = sb("gated", [P, 2, H, P])
        xdt = sb("xdt", [P, C, H, HD])
        xdec = sb("xdec", [P, C, H, HD])
        xskip = sb("xskip", [P, C, H, HD])
        state = sb("state", [NS, 2, H, HD])
        y1 = sb("y1", [P, H, HD])
        y2 = sb("y2", [P, H, HD])
        yg = sb("yg", [P, C, DI])
        sq = sb("sq", [P, DI])
        ssum = sb("ssum", [P, C])
        ygT = sb("ygT", [P, 2, 2, P])
        ot = sb("ot", [P, C, D])
        yo = sb("yo", [P, C, D])

        loaded_w = nc.alloc_semaphore("a_loaded_w")
        loaded = nc.alloc_semaphore("a_loaded")
        stored = nc.alloc_semaphore("a_stored")
        pool_own = nc.alloc_semaphore("a_pool_own")
        a_exp = nc.alloc_semaphore("a_exp")
        ready_w = nc.alloc_semaphore("a_ready_w")
        vec = steps("vec", 47)
        var_ready = steps("var_ready", 4)
        xn_ready = steps("xn_ready", C)
        dt_abs_ready = steps("dt_abs_ready", 1)
        dt_ready = steps("dt_ready", 1)
        cs_ready = steps("cs_ready", 1)
        gated_ready = steps("gated_ready", C)
        state_ready = steps("state_ready", C)
        yg_ready = steps("yg_ready", C)
        out_sum = steps("out_sum", C)
        out_ready = steps("out_ready", C)
        act_own = steps("act_own", 1)
        xnT_ready = steps("xnT_ready", 2)
        bcT_ready = steps("bcT_ready", 4)
        xsb_ready = steps("xsb_ready", C)
        dt_log_ready = steps("dt_log_ready", 1)
        decays_ready = steps("decays_ready", 1)
        decay_ready = steps("decay_ready", C)
        ss_ready = steps("ss_ready", C)
        ygT_ready = steps("ygT_ready", C)
        t_xn = steps("t_xn", 2)
        mm_bc = steps("mm_bc", 4)
        mm_xz = steps("mm_xz", C)
        mm_cs = steps("mm_cs", 1)
        mm_decay = steps("mm_decay", C)
        mm_scores = steps("mm_scores", C)
        mm_y = steps("mm_y", C)
        t_yg = steps("t_yg", C)
        mm_out = steps("mm_out", C)
        rstd_ready = steps("rstd_ready", 4)
        xdt_ready = steps("xdt_ready", C)
        xdec_ready = steps("xdec_ready", C)
        xskip_ready = steps("xskip_ready", C)

        x_rows = x_in.rearrange("b (c p) d -> b p c d", p=P)
        o_rows = x_out.rearrange("b (c p) d -> b p c d", p=P)
        loads = [(w_in, w["in_projT"]), (taps, w["conv_w"].partition_broadcast(P)),
                 (conv_b_row, w["conv_b"][0:1, 0:XB]), (conv_b_col, w["conv_b_cols"]),
                 (ln_wb, w["ln_wb"]), (dt_bias, w["dt_bias"].partition_broadcast(P)),
                 (a_neg, w["A_log"].partition_broadcast(P)),
                 (d_skip, w["D_skip"].partition_broadcast(P)), (norm_w, w["norm_w"]),
                 (w_out, w["out_projT"].rearrange("(k p) n -> p k n", p=P)),
                 (ident, const["ident"]), (upper, const["upper"]), (mask, const["mask_upper"])]
        W_LOADED = 16 * len(loads)
        block = ctx.enter_context(nc.Block())

        @block.sync
        def _(sp):
            for to, of in loads:
                sp.dma_start(to[:], of).then_inc(loaded_w, 16)

            sp.sem_inc(stored, 1)
            sp.dma_start(xt[:, 0], x_rows[0]).then_inc(loaded, 16)
            with sp.Fori(0, B - 1) as seq:
                xn_ready.need(sp, seq, 1)
                sp.dma_start(xt[:, bass.ds((seq + 1) % 2, 1)].squeeze(1),
                             x_rows[bass.ds(seq + 1, 1)].squeeze(0)).then_inc(loaded, 16)
                out_ready.need(sp, seq, C)
                sp.dma_start(o_rows[bass.ds(seq, 1)].squeeze(0), yo[:]).then_inc(stored, 16)
            out_ready.need(sp, B - 1, C)
            sp.dma_start(o_rows[B - 1], yo[:]).then_inc(stored, 16)
            sp.wait_ge(stored, 16 * B + 1)

        @block.gpsimd
        def _(pool):
            for s in (rstd_ready, xdt_ready, xdec_ready, xskip_ready):
                pool.sem_inc(s.sem, 1)
            pool.memset(minus_half[:], -0.5).then_inc(pool_own, 1)
            pool.wait_ge(pool_own, 1)
            with pool.Fori(0, B) as seq:
                def inverse_root(n):
                    var_ready.need(pool, seq, n)
                    rstd_ready.mark(pool.tensor_tensor(rstd[:], var[:], minus_half[:], ALU.pow))

                inverse_root(1)
                inverse_root(2)
                dt_ready.need(pool, seq, 1)
                for c in range(C):
                    xsb_ready.need(pool, seq, c + 1)
                    xs = xsb[:, c, 0:DI].rearrange("p (h e) -> p h e", h=H)
                    xdt_ready.mark(pool.tensor_tensor(
                        xdt[:, c], xs, wide(dt[:, c], 2, [P, H, HD]), ALU.mult))
                    xskip_ready.mark(pool.tensor_tensor(
                        xskip[:, c], xs, wide(d_skip[:], 2, [P, H, HD]), ALU.mult))
                decays_ready.need(pool, seq, 1)
                for c in range(C):
                    xdt_ready.need(pool, seq, c + 1)
                    xdec_ready.mark(pool.tensor_tensor(
                        xdec[:, c], xdt[:, c], wide(e_rest[:, c], 2, [P, H, HD]), ALU.mult))
                inverse_root(3)
                inverse_root(4)
            for s in (rstd_ready, xdt_ready, xdec_ready, xskip_ready):
                s.close()

        @block.scalar
        def _(act):
            for s in (act_own, xnT_ready, bcT_ready, xsb_ready, dt_log_ready,
                      decays_ready, decay_ready, ss_ready, ygT_ready):
                act.sem_inc(s.sem, 1)
            act.wait_ge(loaded_w, W_LOADED)
            act.activation(a_neg[:], a_neg[:], ACT.Exp).then_inc(a_exp, 1)
            with act.Fori(0, B) as seq:
                for g in range(2):
                    t_xn.need(act, seq, g + 1)
                    xnT_ready.mark(act.activation(
                        xnT[:, TAPS - 1 + 512 * g:TAPS - 1 + 512 * (g + 1)], bank[g][:], ACT.Identity,
                        bias=ln_wb[:, 1:2], scale=ln_wb[:, 0:1]))
                for g in range(2):
                    for k, to in enumerate((bT, cT)):
                        mm_bc.need(act, seq, 2 * g + k + 1)
                        bcT_ready.mark(act.activation(
                            to[:, 512 * g:512 * (g + 1)], bank[2 + 2 * g + k][0:NS, :], ACT.Silu,
                            bias=conv_b_col[:, k:k + 1]))
                for c in range(C):
                    mm_xz.need(act, seq, c + 1)
                    act.activation(dt_raw[:, c], bank[c % 2][:, DI:DI + H], ACT.Copy)
                    act.activation(zs[:, c], bank[c % 2][:, 0:DI], ACT.Silu)
                    xsb_ready.mark(act.activation(xsb[:, c], bank[6 + c % 2][:, 0:XB], ACT.Silu))
                dt_abs_ready.need(act, seq, 1)
                n = act_own.mark(act.activation(dt_exp[:], dt_abs[:], ACT.Exp, scale=-1.0))
                act_own.need(act, seq, n)
                dt_log_ready.mark(act.activation(dt_exp[:], dt_exp[:], ACT.Ln, bias=1.0))
                cs_ready.need(act, seq, 1)
                act.activation(e_cs[:], bank[2][:, 0:C * H].rearrange("p (c h) -> p c h", h=H), ACT.Exp)
                act.activation(e_tot[:], bank[2][:, C * H:2 * C * H].rearrange("p (c h) -> p c h", h=H), ACT.Exp)
                decays_ready.mark(act.activation(e_rest[:], rest[:], ACT.Exp))
                for c in range(C):
                    mm_decay.need(act, seq, c + 1)
                    if c >= 2:
                        gated_ready.need(act, seq, c - 1)
                    for h in range(H):
                        ins = act.activation(decay[:, c % 2, h], bank[3 + c % 2][:, h * P:(h + 1) * P],
                                             ACT.Exp, bias=cs_neg[:, c, h:h + 1])
                    decay_ready.mark(ins)
                for c in range(C):
                    yg_ready.need(act, seq, c + 1)
                    if c >= 1:
                        ss_ready.need(act, seq, c)
                    ss_ready.mark(act.activation(sq[:], yg[:, c], ACT.Square, accum_out=ssum[:, c:c + 1]))
                for c in range(C):
                    t_yg.need(act, seq, c + 1)
                    if c >= 2:
                        mm_out.need(act, seq, c - 1)
                    for k in range(2):
                        ins = act.activation(ygT[:, c % 2, k], bank[3 + c % 2][:, k * P:(k + 1) * P],
                                             ACT.Identity, bias=0.0, scale=norm_w[:, k:k + 1])
                    ygT_ready.mark(ins)
            for s in (act_own, xnT_ready, bcT_ready, xsb_ready, dt_log_ready,
                      decays_ready, decay_ready, ss_ready, ygT_ready):
                s.close()

        @block.tensor
        def _(pe):
            for s in (t_xn, mm_bc, mm_xz, mm_cs, mm_decay, mm_scores, mm_y, t_yg, mm_out):
                pe.sem_inc(s.sem, 1)
            pe.wait_ge(loaded_w, W_LOADED)
            pe.wait_ge(ready_w, 5)
            with pe.Fori(0, B) as seq:
                for g in range(2):
                    for q in range(4):
                        xn_ready.need(pe, seq, 4 * g + q + 1)
                        ins = pe.transpose(bank[g][:, q * P:(q + 1) * P], xn[:, 4 * g + q], ident[:])
                    t_xn.mark(ins)
                for g in range(2):
                    xnT_ready.need(pe, seq, g + 1)
                    for k in range(2):
                        for j in range(TAPS):
                            ins = pe.matmul(bank[2 + 2 * g + k][0:NS, :], w_conv[:, j, DI + k * NS:DI + (k + 1) * NS],
                                            xnT[:, 512 * g + j:512 * (g + 1) + j], start=(j == 0), stop=(j == TAPS - 1))
                        mm_bc.mark(ins)
                for c in range(C):
                    if c >= 2:
                        xsb_ready.need(pe, seq, c - 1)
                    for j in range(TAPS):
                        pe.matmul(bank[6 + c % 2][:, 0:XB], xnT[:, c * P + j:(c + 1) * P + j], w_conv[:, j, 0:XB],
                                  start=(j == 0), stop=False)
                    pe.matmul(bank[6 + c % 2][:, 0:XB], ones[0:1, :], conv_b_row[0:1, :], start=False, stop=True)
                    mm_xz.mark(pe.matmul(bank[c % 2][:, 0:DI + H], xnT[:, c * P + TAPS - 1:(c + 1) * P + TAPS - 1],
                                         w_zdt[:], start=True, stop=True))
                dt_ready.need(pe, seq, 1)
                bcT_ready.need(pe, seq, 4)
                flat = adt[:].rearrange("p c h -> p (c h)")
                pe.matmul(bank[2][:, 0:C * H], upper[:], flat, start=True, stop=True)
                mm_cs.mark(pe.matmul(bank[2][:, C * H:2 * C * H], ones[:], flat, start=True, stop=True))
                for c in range(C + 1):
                    if c < C:
                        if c >= 2:
                            decay_ready.need(pe, seq, c - 1)
                        pe.matmul(bank[3 + c % 2][:], ident_b[:], wide(mask[:], 1, [P, H, P]), start=True, stop=False)
                        for h in range(H):
                            ins = pe.matmul(bank[3 + c % 2][:, h * P:(h + 1) * P], adt[:, c, h:h + 1].to_broadcast([P, P]),
                                            upper[:], start=False, stop=(h == H - 1))
                        mm_decay.mark(ins)
                        if c >= 2:
                            gated_ready.need(pe, seq, c - 1)
                        mm_scores.mark(pe.matmul(bank[5 + c % 2][:, 0:P], bT[:, c * P:(c + 1) * P], cT[:, c * P:(c + 1) * P],
                                                 start=True, stop=True))
                    if c >= 1:
                        d = c - 1
                        gated_ready.need(pe, seq, d + 1)
                        xdec_ready.need(pe, seq, d + 1)
                        state_ready.need(pe, seq, d)
                        if d >= 2:
                            yg_ready.need(pe, seq, d - 1)
                        elif d == 0:
                            xsb_ready.need(pe, seq, C)
                        to = bank[(7, 0)[d % 2]]
                        for h in range(H):
                            pe.matmul(to[:, h * HD:(h + 1) * HD], gated[:, d % 2, h], xdt[:, d, h], start=True, stop=True)
                        pe.matmul(to[:, DI:2 * DI], cT[:, d * P:(d + 1) * P], state[:, d % 2].rearrange("p h e -> p (h e)"),
                                  start=True, stop=True)
                        mm_y.mark(pe.matmul(bank[(1, 2)[d % 2]][0:NS, 0:DI], xsb[:, d, DI:XB],
                                            xdec[:, d].rearrange("p h e -> p (h e)"), start=True, stop=True))
                for c in range(C + 1):
                    if c < C:
                        yg_ready.need(pe, seq, c + 1)
                        if c >= 2:
                            ygT_ready.need(pe, seq, c - 1)
                        else:
                            decay_ready.need(pe, seq, C)
                        for k in range(2):
                            ins = pe.transpose(bank[3 + c % 2][:, k * P:(k + 1) * P], yg[:, c, k * P:(k + 1) * P], ident[:])
                        t_yg.mark(ins)
                    if c >= 1:
                        ygT_ready.need(pe, seq, c)
                        if c >= 3:
                            out_sum.need(pe, seq, c - 2)
                        else:
                            gated_ready.need(pe, seq, C)
                        for k in range(2):
                            ins = pe.matmul(bank[5 + (c - 1) % 2][:, 0:D], ygT[:, (c - 1) % 2, k], w_out[:, k], start=(k == 0), stop=(k == 1))
                        mm_out.mark(ins)
            for s in (t_xn, mm_bc, mm_xz, mm_cs, mm_decay, mm_scores, mm_y, t_yg, mm_out):
                s.close()

        @block.vector
        def _(dve):
            for s in (vec, var_ready, xn_ready, dt_abs_ready, dt_ready, cs_ready, gated_ready,
                      state_ready, yg_ready, out_sum, out_ready):
                dve.sem_inc(s.sem, 1)
            dve.sem_inc(ready_w, 1)
            dve.wait_ge(loaded_w, W_LOADED)
            for j in range(TAPS):
                ins = dve.tensor_tensor(w_conv[:, j], w_in[:, DI:2 * DI + 2 * NS], taps[:, j], ALU.mult)
            ins.then_inc(ready_w, 1)
            dve.tensor_copy(w_zdt[:, 0:DI], w_in[:, 0:DI])
            dve.tensor_copy(w_zdt[:, DI:DI + H], w_in[:, 2 * DI + 2 * NS:]).then_inc(ready_w, 1)
            dve.memset(xnT[:, 0:TAPS - 1], 0.0)
            dve.memset(ones[:], 1.0)
            dve.tensor_copy(ident_b[:], ident[:]).then_inc(ready_w, 1)
            dve.wait_ge(a_exp, 1)
            dve.tensor_scalar(a_neg[:], a_neg[:], -1.0, None, ALU.mult).then_inc(ready_w, 1)
            dve.wait_ge(ready_w, 5)
            with dve.Fori(0, B) as seq:
                def own(ins):
                    vec.need(dve, seq, vec.mark(ins))

                rounds = [0]

                def normalise(to, of, eps, done=None, ready=None):
                    for c in range(C):
                        if ready:
                            ready(c)
                        ins = dve.bn_stats(stat[:, c], of(c))
                    own(ins)
                    dve.tensor_tensor(mean[:], stat[:, :, 1], stat[:, :, 4], ALU.add)
                    dve.tensor_tensor(apart[:], stat[:, :, 1], stat[:, :, 4], ALU.subtract)
                    own(dve.scalar_tensor_tensor(var[:], stat[:, :, 2], D * eps, stat[:, :, 5], ALU.add, ALU.add))
                    dve.tensor_scalar(mean[:], mean[:], 0.5, None, ALU.mult)
                    own(dve.scalar_tensor_tensor(apart[:], apart[:], 0.25, apart[:], ALU.mult, ALU.mult))
                    var_ready.mark(dve.scalar_tensor_tensor(var[:], var[:], 1.0 / D, apart[:], ALU.mult, ALU.add))
                    rounds[0] += 1
                    rstd_ready.need(dve, seq, rounds[0])
                    for c in range(C):
                        ins = dve.tensor_scalar(to[:, c], of(c), mean[:, c:c + 1], rstd[:, c:c + 1], ALU.subtract, ALU.mult)
                        if done:
                            done.mark(ins)
                    return ins

                dve.wait_ge(loaded, seq * 16 + 16)
                half = seq % 2
                own(normalise(xn0, lambda c: xt[:, bass.ds(half, 1), c].squeeze(1), 1e-5))
                normalise(xn, lambda c: xn0[:, c], 1e-5, done=xn_ready)
                xsb_ready.need(dve, seq, C)
                own(dve.tensor_tensor(dt_raw[:], dt_raw[:], wide(dt_bias[:], 1, [P, C, H]), ALU.add))
                dt_abs_ready.mark(dve.scalar_tensor_tensor(dt_abs[:], dt_raw[:], -1.0, dt_raw[:], ALU.mult, ALU.max))
                dt_log_ready.need(dve, seq, 1)
                own(dve.scalar_tensor_tensor(dt[:], dt_raw[:], 0.0, dt_exp[:], ALU.max, ALU.add))
                dt_ready.mark(dve.tensor_tensor(adt[:], dt[:], wide(a_neg[:], 1, [P, C, H]), ALU.mult))
                mm_cs.need(dve, seq, 1)
                cs = bank[2][:, 0:C * H].rearrange("p (c h) -> p c h", h=H)
                tot = bank[2][:, C * H:2 * C * H].rearrange("p (c h) -> p c h", h=H)
                own(dve.tensor_scalar(cs_neg[:], cs, -1.0, None, ALU.mult))
                own(dve.memset(state[:, 0], 0.0))
                cs_ready.mark(dve.tensor_tensor(rest[:], tot, cs_neg[:], ALU.add))
                decays_ready.need(dve, seq, 1)
                for c in range(C + 1):
                    if c < C:
                        decay_ready.need(dve, seq, c + 1)
                        mm_scores.need(dve, seq, c + 1)
                        if c >= 2:
                            mm_y.need(dve, seq, c - 1)
                        gated_ready.mark(dve.tensor_tensor(gated[:, c % 2], decay[:, c % 2],
                                                           wide(bank[5 + c % 2][:, 0:P], 1, [P, H, P]), ALU.mult))
                    if c >= 1:
                        d = c - 1
                        to = bank[(7, 0)[d % 2]]
                        mm_y.need(dve, seq, d + 1)
                        yg_ready.need(dve, seq, d)
                        own(dve.tensor_tensor(y1[:], to[:, DI:2 * DI].rearrange("p (h e) -> p h e", h=H),
                                              wide(e_cs[:, d], 2, [P, H, HD]), ALU.mult))
                        nxt = state[:, (d + 1) % 2]
                        own(dve.tensor_tensor(nxt, state[:, d % 2], wide(e_tot[0:NS, d], 2, [NS, H, HD]), ALU.mult))
                        own(dve.tensor_tensor(y2[:], to[:, 0:DI].rearrange("p (h e) -> p h e", h=H), y1[:], ALU.add))
                        state_ready.mark(dve.tensor_tensor(
                            nxt, bank[(1, 2)[d % 2]][0:NS, 0:DI].rearrange("p (h e) -> p h e", h=H), nxt, ALU.add))
                        xskip_ready.need(dve, seq, d + 1)
                        own(dve.tensor_tensor(y1[:], y2[:], xskip[:, d], ALU.add))
                        yg_ready.mark(dve.tensor_tensor(yg[:, d], y1[:].rearrange("p h e -> p (h e)"), zs[:, d], ALU.mult))
                        state_ready.need(dve, seq, d + 1)
                ss_ready.need(dve, seq, C)
                var_ready.mark(dve.tensor_scalar(var[:], ssum[:], 1.0 / DI, 1e-5, ALU.mult, ALU.add))
                rounds[0] += 1
                rstd_ready.need(dve, seq, rounds[0])
                for c in range(C):
                    mm_out.need(dve, seq, c + 1)
                    out_sum.mark(dve.scalar_tensor_tensor(ot[:, c], bank[5 + c % 2][:, 0:D], rstd[:, c:c + 1], xn0[:, c],
                                                          ALU.mult, ALU.add))
                out_sum.need(dve, seq, C)
                own(normalise(xn, lambda c: ot[:, c], 1e-5))
                dve.wait_ge(stored, seq * 16 + 1)
                for c in range(C):
                    out_ready.mark(dve.tensor_tensor(yo[:, c], xn[:, c], xt[:, bass.ds(half, 1), c].squeeze(1), ALU.add))
            for s in (vec, var_ready, xn_ready, dt_abs_ready, dt_ready, cs_ready, gated_ready,
                      state_ready, yg_ready, out_sum, out_ready):
                s.close()


def attention_layer(nc, x_in, x_out, w, const):
    DEPTH, H, HD, WIN = 2, 8, 64, 64
    INNER = H * HD
    HID = D * 4 * 2 // 3
    PAIRS = H // 2
    VW = HD + 1
    HALF = HD // 2
    UNITS = 2 * C
    HID_TILES = [(0, P), (P, P), (2 * P, HID - 2 * P)]
    with ExitStack() as ctx:
        def sb(name, shape, dt=F32):
            return ctx.enter_context(nc.sbuf_tensor("b_" + name, shape, dt))

        def steps(name, per):
            return Steps(nc, "b_" + name, per)

        bank = [ctx.enter_context(nc.psum_tensor(f"b_bank{n}", [P, 512], F32)) for n in range(8)]
        w_qkv = sb("w_qkv", [D, DEPTH, 3, INNER])
        w_o = sb("w_o", [P, DEPTH, PAIRS, D])
        w1 = sb("w1", [D, DEPTH, 2, HID])
        b1 = sb("b1", [1, DEPTH, 2, HID])
        w2 = sb("w2", [P, DEPTH, 3, D])
        b2 = sb("b2", [1, DEPTH, D])
        ln_gb = sb("ln_gb", [D, DEPTH, 2])
        ln_now = sb("ln_now", [D, 2])
        scales = sb("scales", [P, DEPTH, 4, HD])
        tab = sb("tab", [P, DEPTH, 4, C, HD])
        tab_now = sb("tab_now", [P, 4, C, HD])
        ident = sb("ident", [P, P])
        ident_b = sb("ident_b", [P, P], BF16)
        masks = sb("masks", [P, 2, P], BF16)
        ones = sb("ones", [1, P])
        minus_half = sb("minus_half", [P, 2 * H])
        xt = sb("xt", [P, 2, C, D])
        xr = sb("xr", [P, C, D])
        stat = sb("stat", [P, C, 6])
        mean = sb("mean", [P, C])
        apart = sb("apart", [P, C])
        var = sb("var", [P, C])
        rstd = sb("rstd", [P, C])
        hT = sb("hT", [D, L + 1])
        q_raw = sb("q_raw", [P, 2, H, HD])
        k_raw = sb("k_raw", [P, 2, H, HD])
        square = sb("square", [P, 2, 2, H, HD])
        ss = sb("ss", [P, 2, 2, H])
        inv = sb("inv", [P, 2, 2, H])
        q_cos = sb("q_cos", [P, H, HD])
        q_sin = sb("q_sin", [P, H, HD])
        k_cos = sb("k_cos", [P, H, HD])
        k_sin = sb("k_sin", [P, H, HD])
        q_rot = sb("q_rot", [P, 2, H, HD])
        k_rot = sb("k_rot", [P, 2, H, HD])
        qT = sb("qT", [P, C, PAIRS, P])
        rotary = qT[:].rearrange("p c j t -> p (c j t)")[:, 0:4 * C * HD].rearrange("p (a c e) -> p a c e", a=4, c=C)
        kT = sb("kT", [P, PAIRS, 2 * C + 1, WIN])
        v_own = sb("v_own", [P, C, H, VW])
        v_mix = sb("v_mix", [P, C + 1, H, VW])
        shifted_s = sb("shifted_s", [P, 2, PAIRS, P])
        probs = sb("probs", [P, 2, PAIRS, P])
        row_max = sb("row_max", [P, 2, PAIRS])
        probsT = sb("probsT", [P, 2, PAIRS, P])
        inv_sum = sb("inv_sum", [P, 2, PAIRS])
        o_rows = sb("o_rows", [P, 2, PAIRS, 2, HD])
        oT = sb("oT", [P, 2, PAIRS, P])
        sh = sb("sh", [P, C, D])
        hn = sb("hn", [P, C, D])
        hnT = hT[:, 1:L + 1]
        flat = square[:].rearrange("p a b h e -> p (a b h e)")
        gelu = flat[:, 0:2 * HID].rearrange("p (a n) -> p a n", a=2)
        prod = flat[:, 2 * HID:4 * HID].rearrange("p (a n) -> p a n", a=2)
        prodT = sb("prodT", [P, 2, 3, P])

        loaded_w = nc.alloc_semaphore("b_loaded_w")
        loaded = nc.alloc_semaphore("b_loaded")
        stored = nc.alloc_semaphore("b_stored")
        shifted = nc.alloc_semaphore("b_shifted")
        pool_own = nc.alloc_semaphore("b_pool_own")
        ready_w = nc.alloc_semaphore("b_ready_w")
        seq_own = steps("seq_own", 8)
        seq_var = steps("seq_var", 2)
        out_ready = steps("out_ready", C)
        seq_seen = steps("seq_seen", 1)
        vec = steps("vec", 60)
        block_ready = steps("block_ready", 1)
        ss_ready = steps("ss_ready", C)
        q_ready = steps("q_ready", C)
        max_ready = steps("max_ready", UNITS)
        o_ready = steps("o_ready", UNITS)
        mid_ready = steps("mid_ready", C)
        var_ready = steps("var_ready", 1)
        hn_ready = steps("hn_ready", C)
        prod_ready = steps("prod_ready", C)
        end_ready = steps("end_ready", C)
        hT_ready = steps("hT_ready", 2)
        qk_ready = steps("qk_ready", C)
        v_ready = steps("v_ready", C)
        qkT_ready = steps("qkT_ready", C)
        exp_ready = steps("exp_ready", UNITS)
        probsT_ready = steps("probsT_ready", UNITS)
        oT_ready = steps("oT_ready", C)
        hnT_ready = steps("hnT_ready", 2)
        gelu_ready = steps("gelu_ready", C)
        prodT_ready = steps("prodT_ready", C)
        t_x = steps("t_x", 2)
        mm_qkv = steps("mm_qkv", C)
        t_qk = steps("t_qk", C)
        mm_s = steps("mm_s", UNITS)
        t_p = steps("t_p", UNITS)
        mm_pv = steps("mm_pv", UNITS)
        t_o = steps("t_o", C)
        mm_o = steps("mm_o", C)
        t_h = steps("t_h", 2)
        mm_1 = steps("mm_1", C)
        t_prod = steps("t_prod", C)
        mm_2 = steps("mm_2", C)
        seq_rstd = steps("seq_rstd", 2)
        inv_ready = steps("inv_ready", C)
        k_ready = steps("k_ready", C)
        rstd_ready = steps("rstd_ready", 1)
        pool_vec = steps("pool_vec", 2 * C)

        x_rows = x_in.rearrange("b (c p) d -> b p c d", p=P)
        y_rows = x_out.rearrange("b (c p) d -> b p c d", p=P)
        loads = [(w_qkv[:], w["wqkv"].rearrange("l d (j n) -> d l j n", j=3)),
                 (w_o[:], w["wo"].rearrange("l (k p) n -> p l k n", p=P)),
                 (w1[:], w["w1"].rearrange("l d (j n) -> d l j n", j=2)),
                 (b1[:], w["b1"].rearrange("(o l) (j n) -> o l j n", j=2, o=1)),
                 (w2[:, :, 0], w["w2"][:, 0:P].rearrange("l p n -> p l n")),
                 (w2[:, :, 1], w["w2"][:, P:2 * P].rearrange("l p n -> p l n")),
                 (w2[0:HID - 2 * P, :, 2], w["w2"][:, 2 * P:HID].rearrange("l p n -> p l n")),
                 (b2[:], w["b2"].rearrange("(o l) n -> o l n", o=1)),
                 (ln_gb[:], w["ln_gb"]), (scales[:], w["qk_scales"].partition_broadcast(P)),
                 (rotary, const["rotary"]), (ident[:], const["ident"]), (masks[:], const["window_masks"])]
        W_LOADED = 16 * len(loads)
        block = ctx.enter_context(nc.Block())

        @block.sync
        def _(sp):
            for to, of in loads:
                sp.dma_start(to, of).then_inc(loaded_w, 16)
            sp.sem_inc(stored, 1)
            sp.dma_start(xt[:, 0], x_rows[0]).then_inc(loaded, 16)

            def blocks(seq):
                with sp.Fori(0, DEPTH) as depth:
                    turn = seq * DEPTH + depth
                    mid_ready.need(sp, turn, C)
                    sp.dma_start(sh[1:P, :, HD:D], xr[0:P - 1, :, HD:D]).then_inc(shifted, 16)
                    sp.dma_start(sh[0:1, 1:C, HD:D], xr[P - 1:P, 0:C - 1, HD:D]).then_inc(shifted, 16)

            with sp.Fori(0, B - 1) as seq:
                seq_seen.need(sp, seq, 1)
                sp.dma_start(xt[:, bass.ds((seq + 1) % 2, 1)].squeeze(1),
                             x_rows[bass.ds(seq + 1, 1)].squeeze(0)).then_inc(loaded, 16)
                blocks(seq)
                out_ready.need(sp, seq, C)
                sp.dma_start(y_rows[bass.ds(seq, 1)].squeeze(0), hn[:]).then_inc(stored, 16)
            blocks(B - 1)
            out_ready.need(sp, B - 1, C)
            sp.dma_start(y_rows[B - 1], hn[:]).then_inc(stored, 16)
            sp.wait_ge(stored, 16 * B + 1)

        @block.gpsimd
        def _(pool):
            marks = (seq_rstd, inv_ready, k_ready, rstd_ready, pool_vec)
            for s in marks:
                pool.sem_inc(s.sem, 1)
            pool.memset(minus_half[:], -0.5).then_inc(pool_own, 1)
            pool.wait_ge(pool_own, 1)
            with pool.Fori(0, B) as seq:
                seq_var.need(pool, seq, 1)
                seq_rstd.mark(pool.tensor_tensor(rstd[:], var[:], minus_half[:, 0:C], ALU.pow))
                with pool.Fori(0, DEPTH) as depth:
                    turn = seq * DEPTH + depth
                    for c in range(C):
                        ss_ready.need(pool, turn, c + 1)
                        if c >= 2:
                            q_ready.need(pool, turn, c - 1)
                        inv_ready.mark(pool.tensor_tensor(
                            inv[:, c % 2].rearrange("p a h -> p (a h)"), ss[:, c % 2].rearrange("p a h -> p (a h)"),
                            minus_half[:], ALU.pow))
                        k = k_raw[:, c % 2]
                        if c >= 1:
                            k_ready.need(pool, turn, c)
                        pool.tensor_tensor(k_cos[:], k, wide(tab_now[:, 2, c], 1, [P, H, HD]), ALU.mult)
                        pool.tensor_tensor(k_sin[:, :, 0:HALF], k[:, :, HALF:HD],
                                           wide(tab_now[:, 3, c, 0:HALF], 1, [P, H, HALF]), ALU.mult)
                        n = pool_vec.mark(pool.tensor_tensor(k_sin[:, :, HALF:HD], k[:, :, 0:HALF],
                                                             wide(tab_now[:, 3, c, HALF:HD], 1, [P, H, HALF]), ALU.mult))
                        pool_vec.need(pool, turn, n)
                        n = pool_vec.mark(pool.tensor_tensor(k_sin[:], k_cos[:], k_sin[:], ALU.add))
                        pool_vec.need(pool, turn, n)
                        inv_ready.need(pool, turn, c + 1)
                        if c >= 2:
                            t_qk.need(pool, turn, c - 1)
                        k_ready.mark(pool.tensor_tensor(
                            k_rot[:, c % 2], k_sin[:], wide(inv[:, c % 2, 1], 2, [P, H, HD]), ALU.mult))
                    var_ready.need(pool, turn, 1)
                    rstd_ready.mark(pool.tensor_tensor(rstd[:], var[:], minus_half[:, 0:C], ALU.pow))
                seq_var.need(pool, seq, 2)
                seq_rstd.mark(pool.tensor_tensor(rstd[:], var[:], minus_half[:, 0:C], ALU.pow))
            for s in marks:
                s.close()

        @block.scalar
        def _(act):
            marks = (hT_ready, qk_ready, v_ready, qkT_ready, exp_ready, probsT_ready, oT_ready, hnT_ready,
                     gelu_ready, prodT_ready)
            for s in marks:
                act.sem_inc(s.sem, 1)
            act.wait_ge(ready_w, 3)
            with act.Fori(0, B) as seq:
                with act.Fori(0, DEPTH) as depth:
                    turn = seq * DEPTH + depth
                    for g in range(2):
                        t_x.need(act, turn, g + 1)
                        act.activation(hT[0:HD, 512 * g:512 * (g + 1)], bank[g][0:HD, :], ACT.Copy)
                        hT_ready.mark(act.activation(hT[HD:D, 512 * g + 1:512 * (g + 1) + 1], bank[g][HD:D, :], ACT.Copy))

                    def transposed(c):
                        t_qk.need(act, turn, c + 1)
                        act.activation(qT[:, c], bank[6][:].rearrange("p (j t) -> p j t", j=PAIRS), ACT.Copy)
                        qkT_ready.mark(act.activation(
                            kT[:, :, 2 * c + 1:2 * c + 3], bank[7][:].rearrange("p (j w t) -> p j w t", j=PAIRS, w=2), ACT.Copy))

                    for c in range(C):
                        q, k, v = (bank[3 * (c % 2) + j][:].rearrange("p (h e) -> p h e", h=H) for j in range(3))
                        mm_qkv.need(act, turn, c + 1)
                        if c >= 2:
                            q_ready.need(act, turn, c - 1)
                            k_ready.need(act, turn, c - 1)
                        act.activation(square[:, c % 2, 0], q, ACT.Square)
                        act.activation(square[:, c % 2, 1], k, ACT.Square)
                        act.activation(q_raw[:, c % 2], q, ACT.Copy)
                        qk_ready.mark(act.activation(k_raw[:, c % 2], k, ACT.Copy))
                        act.activation(v_own[:, c, :, 0:HD], v, ACT.Copy)
                        act.activation(v_mix[0:WIN, c, :, 0:HD], v[0:WIN], ACT.Copy)
                        v_ready.mark(act.activation(v_mix[WIN:P, c + 1, :, 0:HD], v[WIN:P], ACT.Copy))
                        if c >= 1:
                            transposed(c - 1)
                    transposed(C - 1)

                    def copy_probs(u):
                        t_p.need(act, turn, u + 1)
                        if u >= 2:
                            mm_pv.need(act, turn, u - 1)
                        probsT_ready.mark(act.activation(
                            probsT[:, u % 2], bank[2 + u % 2][:].rearrange("p (j t) -> p j t", j=PAIRS), ACT.Copy))

                    def copy_o(c):
                        t_o.need(act, turn, c + 1)
                        if c >= 2:
                            mm_o.need(act, turn, c - 1)
                        oT_ready.mark(act.activation(oT[:, c % 2], bank[6][:].rearrange("p (j t) -> p j t", j=PAIRS), ACT.Copy))

                    for u in range(UNITS + 3):
                        if u < UNITS:
                            max_ready.need(act, turn, u + 1)
                            if u >= 2:
                                t_p.need(act, turn, u - 1)
                            exp_ready.mark(act.activation(probs[:, u % 2], shifted_s[:, u % 2], ACT.Exp))
                        if 1 <= u <= UNITS:
                            copy_probs(u - 1)
                        if u >= 4 and u % 2 == 0:
                            copy_o(u // 2 - 2)
                    for g in range(2):
                        t_h.need(act, turn, g + 1)
                        hnT_ready.mark(act.activation(hnT[:, 512 * g:512 * (g + 1)], bank[4 + g][:], ACT.Identity,
                                                      bias=ln_now[:, 1:2], scale=ln_now[:, 0:1]))
                    for c in range(C + 1):
                        if c < C:
                            mm_1.need(act, turn, c + 1)
                            if c >= 2:
                                prod_ready.need(act, turn, c - 1)
                            gelu_ready.mark(act.activation(gelu[:, c % 2], bank[2 + c % 2][:, 0:HID], ACT.Gelu))
                        if c >= 1:
                            d = c - 1
                            t_prod.need(act, turn, d + 1)
                            if d >= 2:
                                mm_2.need(act, turn, d - 1)
                            act.activation(prodT[:, d % 2, 0:2], bank[4 + d % 2][:, 0:2 * P].rearrange("p (j t) -> p j t", j=2), ACT.Copy)
                            prodT_ready.mark(act.activation(prodT[0:HID - 2 * P, d % 2, 2], bank[4 + d % 2][0:HID - 2 * P, 2 * P:3 * P], ACT.Copy))
            for s in marks:
                s.close()

        @block.tensor
        def _(pe):
            marks = (t_x, mm_qkv, t_qk, mm_s, t_p, mm_pv, t_o, mm_o, t_h, mm_1, t_prod, mm_2)
            for s in marks:
                pe.sem_inc(s.sem, 1)
            pe.wait_ge(loaded_w, W_LOADED)
            pe.wait_ge(ready_w, 3)
            with pe.Fori(0, B) as seq:
                with pe.Fori(0, DEPTH) as depth:
                    turn = seq * DEPTH + depth
                    block_ready.need(pe, turn, 1)
                    for g in range(2):
                        for j in range(4):
                            ins = pe.transpose(bank[g][:, j * P:(j + 1) * P], xr[:, 4 * g + j], ident[:])
                        t_x.mark(ins)
                    hT_ready.need(pe, turn, 2)

                    def transpose_qk(c):
                        if c >= 1:
                            qkT_ready.need(pe, turn, c)
                        q_ready.need(pe, turn, c + 1)
                        for j in range(PAIRS):
                            pe.transpose(bank[6][:, j * P:(j + 1) * P],
                                         q_rot[:, c % 2, 2 * j:2 * j + 2].rearrange("p h e -> p (h e)"), ident[:])
                        k_ready.need(pe, turn, c + 1)
                        for j in range(PAIRS):
                            ins = pe.transpose(bank[7][:, j * P:(j + 1) * P],
                                               k_rot[:, c % 2, 2 * j:2 * j + 2].rearrange("p h e -> p (h e)"), ident[:])
                        t_qk.mark(ins)

                    for c in range(C):
                        if c >= 2:
                            v_ready.need(pe, turn, c - 1)
                        for j in range(3):
                            ins = pe.matmul(bank[3 * (c % 2) + j][:], hT[:, c * P:(c + 1) * P],
                                            w_qkv[:, bass.ds(depth, 1), j].squeeze(1), start=True, stop=True)
                        mm_qkv.mark(ins)
                        if c >= 1:
                            transpose_qk(c - 1)
                    transpose_qk(C - 1)

                    def scores(u):
                        c, par = divmod(u, 2)
                        to = bank[u % 2]
                        if u >= 2:
                            max_ready.need(pe, turn, u - 1)
                        else:
                            v_ready.need(pe, turn, C)
                            qkT_ready.need(pe, turn, C)
                        pe.matmul(to[:], ident_b[:], wide(masks[:, min(c, 1)], 1, [P, PAIRS, P]), start=True, stop=False)
                        rows = slice(par * HD, (par + 1) * HD)
                        for j in range(PAIRS):
                            cols = slice(j * P, (j + 1) * P)
                            pe.matmul(to[0:WIN, j * P:j * P + WIN], qT[rows, c, j, 0:WIN], kT[rows, j, 2 * c + 1],
                                      start=False, stop=False)
                            pe.matmul(to[0:WIN, j * P + WIN:(j + 1) * P], qT[rows, c, j, 0:WIN], kT[rows, j, 2 * c],
                                      start=False, stop=(j == PAIRS - 1))
                            ins = pe.matmul(to[WIN:P, cols], qT[rows, c, j, WIN:P],
                                            kT[rows, j, 2 * c + 1:2 * c + 3].rearrange("p w t -> p (w t)"),
                                            start=False, stop=(j == PAIRS - 1))
                        mm_s.mark(ins)

                    def transpose_probs(u):
                        exp_ready.need(pe, turn, u + 1)
                        if u >= 2:
                            probsT_ready.need(pe, turn, u - 1)
                        for j in range(PAIRS):
                            ins = pe.transpose(bank[2 + u % 2][:, j * P:(j + 1) * P], probs[:, u % 2, j], ident[:])
                        t_p.mark(ins)

                    def values(u):
                        c, par = divmod(u, 2)
                        probsT_ready.need(pe, turn, u + 1)
                        if u >= 2:
                            o_ready.need(pe, turn, u - 1)
                        for j in range(PAIRS):
                            h = 2 * j + par
                            pe.matmul(bank[4 + u % 2][0:WIN, j * VW:(j + 1) * VW], probsT[:, u % 2, j, 0:WIN], v_mix[:, c, h],
                                      start=True, stop=True)
                            ins = pe.matmul(bank[4 + u % 2][WIN:P, j * VW:(j + 1) * VW], probsT[:, u % 2, j, WIN:P], v_own[:, c, h],
                                            start=True, stop=True)
                        mm_pv.mark(ins)

                    def transpose_o(c):
                        o_ready.need(pe, turn, 2 * c + 2)
                        if c >= 1:
                            oT_ready.need(pe, turn, c)
                        for j in range(PAIRS):
                            ins = pe.transpose(bank[6][:, j * P:(j + 1) * P], o_rows[:, c % 2, j].rearrange("p a e -> p (a e)"), ident[:])
                        t_o.mark(ins)

                    def project(c):
                        oT_ready.need(pe, turn, c + 1)
                        if c >= 1:
                            mid_ready.need(pe, turn, c)
                        for j in range(PAIRS):
                            ins = pe.matmul(bank[7][:, 0:D], oT[:, c % 2, j], w_o[:, bass.ds(depth, 1), j].squeeze(1),
                                            start=(j == 0), stop=(j == PAIRS - 1))
                        mm_o.mark(ins)

                    for u in range(UNITS + 5):
                        if u < UNITS:
                            scores(u)
                        if 1 <= u <= UNITS:
                            transpose_probs(u - 1)
                        if 2 <= u <= UNITS + 1:
                            values(u - 2)
                        if u >= 4 and u % 2 == 0 and u // 2 - 2 < C:
                            transpose_o(u // 2 - 2)
                        if u >= 5 and u % 2 == 1 and (u - 5) // 2 < C:
                            project((u - 5) // 2)

                    for g in range(2):
                        for j in range(4):
                            hn_ready.need(pe, turn, 4 * g + j + 1)
                            ins = pe.transpose(bank[4 + g][:, j * P:(j + 1) * P], hn[:, 4 * g + j], ident[:])
                        t_h.mark(ins)

                    def up(c):
                        if c >= 2:
                            prod_ready.need(pe, turn, c - 1)
                        hnT_ready.need(pe, turn, c // 4 + 1)
                        for j in range(2):
                            to = bank[2 * j + c % 2][:, 0:HID]
                            pe.matmul(to, hnT[:, c * P:(c + 1) * P], w1[:, bass.ds(depth, 1), j].squeeze(1), start=True, stop=False)
                            ins = pe.matmul(to, ones[:], b1[:, bass.ds(depth, 1), j].squeeze(1), start=False, stop=True)
                        mm_1.mark(ins)

                    def transpose_prod(c):
                        prod_ready.need(pe, turn, c + 1)
                        if c >= 2:
                            prodT_ready.need(pe, turn, c - 1)
                        else:
                            hnT_ready.need(pe, turn, 2)
                        for j, (a, n) in enumerate(HID_TILES):
                            ins = pe.transpose(bank[4 + c % 2][0:n, j * P:(j + 1) * P], prod[:, c % 2, a:a + n], ident[:])
                        t_prod.mark(ins)

                    def down(c):
                        prodT_ready.need(pe, turn, c + 1)
                        if c >= 2:
                            end_ready.need(pe, turn, c - 1)
                        to = bank[6 + c % 2][:, 0:D]
                        for j, (a, n) in enumerate(HID_TILES):
                            pe.matmul(to, prodT[0:n, c % 2, j], w2[0:n, bass.ds(depth, 1), j].squeeze(1), start=(j == 0), stop=False)
                        mm_2.mark(pe.matmul(to, ones[:], b2[:, bass.ds(depth, 1)].squeeze(1), start=False, stop=True))

                    for c in range(C + 2):
                        if c < C:
                            up(c)
                        if 1 <= c <= C:
                            transpose_prod(c - 1)
                        if c >= 2:
                            down(c - 2)
            for s in marks:
                s.close()

        @block.vector
        def _(dve):
            marks = (seq_own, seq_var, out_ready, seq_seen, vec, block_ready, ss_ready, q_ready, max_ready,
                     o_ready, mid_ready, var_ready, hn_ready, prod_ready, end_ready)
            for s in marks:
                dve.sem_inc(s.sem, 1)
            dve.wait_ge(loaded_w, W_LOADED)
            dve.tensor_copy(ident_b[:], ident[:])
            dve.memset(ones[:], 1.0)
            dve.memset(hT[HD:D, 0:1], 0.0)
            dve.memset(kT[:, :, 0], 0.0)
            dve.memset(v_own[:, :, :, HD:VW], 1.0)
            dve.memset(v_mix[:, :, :, HD:VW], 1.0)
            dve.memset(v_mix[WIN:P, 0, :, 0:HD], 0.0)
            dve.memset(sh[0:1, 0, HD:D], 0.0).then_inc(ready_w, 1)
            for l in range(DEPTH):
                for j in range(4):
                    ins = dve.tensor_tensor(tab[:, l, j], rotary[:, j], wide(scales[:, l, j], 1, [P, C, HD]), ALU.mult)
            ins.then_inc(ready_w, 1)
            dve.wait_ge(ready_w, 2)
            dve.tensor_scalar(tab[:, :, 0:2], tab[:, :, 0:2], 8.0, None, ALU.mult).then_inc(ready_w, 1)
            dve.wait_ge(ready_w, 3)
            with dve.Fori(0, B) as seq:
                def normalise(own, to, of, eps, var_mark, inverted, done=None):
                    for c in range(C):
                        ins = dve.bn_stats(stat[:, c], of(c))
                    own(ins)
                    dve.tensor_tensor(mean[:], stat[:, :, 1], stat[:, :, 4], ALU.add)
                    dve.tensor_tensor(apart[:], stat[:, :, 1], stat[:, :, 4], ALU.subtract)
                    own(dve.scalar_tensor_tensor(var[:], stat[:, :, 2], D * eps, stat[:, :, 5], ALU.add, ALU.add))
                    dve.tensor_scalar(mean[:], mean[:], 0.5, None, ALU.mult)
                    own(dve.scalar_tensor_tensor(apart[:], apart[:], 0.25, apart[:], ALU.mult, ALU.mult))
                    var_mark(dve.scalar_tensor_tensor(var[:], var[:], 1.0 / D, apart[:], ALU.mult, ALU.add))
                    inverted()
                    for c in range(C):
                        ins = dve.tensor_scalar(to[:, c], of(c), mean[:, c:c + 1], rstd[:, c:c + 1], ALU.subtract, ALU.mult)
                        if done:
                            done.mark(ins)
                    return ins

                def own_seq(ins):
                    seq_own.need(dve, seq, seq_own.mark(ins))

                dve.wait_ge(loaded, seq * 16 + 16)
                dve.wait_ge(stored, seq * 16 + 1)
                half = seq % 2
                own_seq(normalise(own_seq, xr, lambda c: xt[:, bass.ds(half, 1), c].squeeze(1), 1e-5,
                                  seq_var.mark, lambda: seq_rstd.need(dve, seq, 1)))
                seq_seen.mark(dve.memset(apart[:], 0.0))
                with dve.Fori(0, DEPTH) as depth:
                    turn = seq * DEPTH + depth

                    def own(ins):
                        vec.need(dve, turn, vec.mark(ins))

                    dve.tensor_copy(ln_now[:], ln_gb[:, bass.ds(depth, 1)].squeeze(1))
                    block_ready.mark(dve.tensor_copy(tab_now[:], tab[:, bass.ds(depth, 1)].squeeze(1)))
                    block_ready.need(dve, turn, 1)

                    def rotate_q(c):
                        q = q_raw[:, c % 2]
                        dve.tensor_tensor(q_cos[:], q, wide(tab_now[:, 0, c], 1, [P, H, HD]), ALU.mult)
                        dve.tensor_tensor(q_sin[:, :, 0:HALF], q[:, :, HALF:HD],
                                          wide(tab_now[:, 1, c, 0:HALF], 1, [P, H, HALF]), ALU.mult)
                        own(dve.tensor_tensor(q_sin[:, :, HALF:HD], q[:, :, 0:HALF],
                                              wide(tab_now[:, 1, c, HALF:HD], 1, [P, H, HALF]), ALU.mult))
                        own(dve.tensor_tensor(q_sin[:], q_cos[:], q_sin[:], ALU.add))
                        inv_ready.need(dve, turn, c + 1)
                        if c >= 2:
                            t_qk.need(dve, turn, c - 1)
                        q_ready.mark(dve.tensor_tensor(q_rot[:, c % 2], q_sin[:], wide(inv[:, c % 2, 0], 2, [P, H, HD]), ALU.mult))
                        q_ready.need(dve, turn, c + 1)

                    for c in range(C):
                        qk_ready.need(dve, turn, c + 1)
                        own(dve.tensor_reduce(ss[:, c % 2], square[:, c % 2], AX_X, ALU.add))
                        ss_ready.mark(dve.tensor_scalar(ss[:, c % 2], ss[:, c % 2], 1e-24, None, ALU.max))
                        if c >= 1:
                            rotate_q(c - 1)
                    rotate_q(C - 1)

                    def row_shift(u):
                        of = bank[u % 2][:].rearrange("p (j t) -> p j t", j=PAIRS)
                        mm_s.need(dve, turn, u + 1)
                        if u >= 2:
                            exp_ready.need(dve, turn, u - 1)
                        own(dve.tensor_reduce(row_max[:, u % 2], of, AX_X, ALU.max))
                        max_ready.mark(dve.tensor_tensor(shifted_s[:, u % 2], of, wide(row_max[:, u % 2], 2, [P, PAIRS, P]), ALU.subtract))

                    def divide(u):
                        c, par = divmod(u, 2)
                        of = bank[4 + u % 2][:, 0:PAIRS * VW].rearrange("p (j t) -> p j t", j=PAIRS)
                        mm_pv.need(dve, turn, u + 1)
                        if c >= 2:
                            t_o.need(dve, turn, c - 1)
                        own(dve.reciprocal(inv_sum[:, u % 2], of[:, :, HD]))
                        o_ready.mark(dve.tensor_tensor(o_rows[:, c % 2, :, par], of[:, :, 0:HD], wide(inv_sum[:, u % 2], 2, [P, PAIRS, HD]), ALU.mult))

                    def add_o(c):
                        mm_o.need(dve, turn, c + 1)
                        mid_ready.mark(dve.tensor_tensor(xr[:, c], bank[7][:, 0:D], xr[:, c], ALU.add))

                    for u in range(UNITS + 5):
                        if u < UNITS:
                            row_shift(u)
                        if 2 <= u <= UNITS + 1:
                            divide(u - 2)
                        if u >= 5 and u % 2 == 1 and (u - 5) // 2 < C:
                            add_o((u - 5) // 2)
                    mid_ready.need(dve, turn, C)
                    dve.tensor_copy(sh[:, :, 0:HD], xr[:, :, 0:HD])
                    dve.wait_ge(shifted, turn * 32 + 32)
                    own(dve.memset(apart[:], 0.0))
                    normalise(own, hn, lambda c: sh[:, c], 1e-5, var_ready.mark,
                              lambda: rstd_ready.need(dve, turn, 1), done=hn_ready)
                    for c in range(C + 2):
                        if c < C:
                            gelu_ready.need(dve, turn, c + 1)
                            if c >= 2:
                                t_prod.need(dve, turn, c - 1)
                            prod_ready.mark(dve.tensor_tensor(prod[:, c % 2], bank[c % 2][:, 0:HID], gelu[:, c % 2], ALU.mult))
                        if c >= 2:
                            d = c - 2
                            mm_2.need(dve, turn, d + 1)
                            end_ready.mark(dve.tensor_tensor(xr[:, d], bank[6 + d % 2][:, 0:D], xr[:, d], ALU.add))
                    end_ready.need(dve, turn, C)
                own_seq(normalise(own_seq, hn, lambda c: xr[:, c], 1e-5, seq_var.mark, lambda: seq_rstd.need(dve, seq, 2)))
                for c in range(C):
                    out_ready.mark(dve.tensor_tensor(hn[:, c], hn[:, c], xt[:, bass.ds(half, 1), c].squeeze(1), ALU.add))
            for s in marks:
                s.close()


SEG = 10
BLK = 2 * SEG
PAD = SEG - 1
BLOCKS = -(-(L + PAD) // BLK)
T_ALL = BLOCKS * BLK
TAPS1 = 4
LEAD = TAPS1 - 1 + 1


def scan_layer_rows(nc, x_in, rows_out, xnT, w, const):
    with ExitStack() as ctx:
        def sb(name, shape, dt=F32):
            return ctx.enter_context(nc.sbuf_tensor("c0_" + name, shape, dt))

        def steps(name, per):
            return Steps(nc, "c0_" + name, per)

        bank = [ctx.enter_context(nc.psum_tensor(f"c0_bank{n}", [P, 512], F32)) for n in range(2)]
        ident = sb("ident", [P, P])
        norm_w = sb("norm_w", [P, 1])
        minus_half = sb("minus_half", [P, C])
        xt = sb("xt", [P, 2, C, D])
        xn0 = sb("xn0", [P, C, D])
        xn = sb("xn", [P, C, D])
        sq = sb("sq", [P, C, D])
        stat = sb("stat", [P, C, 6])
        mean = sb("mean", [P, C])
        apart = sb("apart", [P, C])
        var = sb("var", [P, C])
        rstd = sb("rstd", [P, C])
        ssum = sb("ssum", [P, C])
        loaded_w = nc.alloc_semaphore("c0_loaded_w")
        loaded = nc.alloc_semaphore("c0_loaded")
        stored = nc.alloc_semaphore("c0_stored")
        pool_own = nc.alloc_semaphore("c0_pool_own")
        zeroed = nc.alloc_semaphore("c0_zeroed")
        vec = steps("vec", 4)
        var_ready = steps("var_ready", 2)
        xn0_ready = steps("xn0_ready", C)
        xn_ready = steps("xn_ready", C)
        ss_ready = steps("ss_ready", C)
        xnT_ready = steps("xnT_ready", 2)
        t_xn = steps("t_xn", 2)
        rstd_ready = steps("rstd_ready", 2)
        x_rows = x_in.rearrange("b (c p) d -> b p c d", p=P)
        o_rows = rows_out.rearrange("b (c p) d -> b p c d", p=P)
        loads = [(ident, const["ident"]), (norm_w, w["norm_w"])]
        W_LOADED = 16 * len(loads)
        block = ctx.enter_context(nc.Block())

        @block.sync
        def _(sp):
            for to, of in loads:
                sp.dma_start(to[:], of).then_inc(loaded_w, 16)
            sp.sem_inc(stored, 1)
            sp.dma_start(xt[:, 0], x_rows[0]).then_inc(loaded, 16)
            with sp.Fori(0, B - 1) as seq:
                xn0_ready.need(sp, seq, 1)
                sp.dma_start(xt[:, bass.ds((seq + 1) % 2, 1)].squeeze(1),
                             x_rows[bass.ds(seq + 1, 1)].squeeze(0)).then_inc(loaded, 16)
                xn0_ready.need(sp, seq, C)
                sp.dma_start(o_rows[bass.ds(seq, 1)].squeeze(0), xn0[:]).then_inc(stored, 16)
            xn0_ready.need(sp, B - 1, C)
            sp.dma_start(o_rows[B - 1], xn0[:]).then_inc(stored, 16)
            sp.wait_ge(stored, 16 * B + 1)

        @block.gpsimd
        def _(pool):
            pool.sem_inc(rstd_ready.sem, 1)
            pool.memset(minus_half[:], -0.5).then_inc(pool_own, 1)
            pool.wait_ge(pool_own, 1)
            with pool.Fori(0, B) as seq:
                for n in (1, 2):
                    var_ready.need(pool, seq, n)
                    rstd_ready.mark(pool.tensor_tensor(rstd[:], var[:], minus_half[:], ALU.pow))
            rstd_ready.close()

        @block.scalar
        def _(act):
            act.sem_inc(ss_ready.sem, 1)
            with act.Fori(0, B) as seq:
                for c in range(C):
                    xn0_ready.need(act, seq, c + 1)
                    ss_ready.mark(act.activation(sq[:, c], xn0[:, c], ACT.Square, accum_out=ssum[:, c:c + 1]))
            ss_ready.close()

        @block.tensor
        def _(pe):
            pe.sem_inc(t_xn.sem, 1)
            pe.wait_ge(loaded_w, W_LOADED)
            with pe.Fori(0, B) as seq:
                for g in range(2):
                    for q in range(4):
                        xn_ready.need(pe, seq, 4 * g + q + 1)
                        ins = pe.transpose(bank[g][:, q * P:(q + 1) * P], xn[:, 4 * g + q], ident[:])
                    t_xn.mark(ins)
            t_xn.close()

        @block.vector
        def _(dve):
            marks = (vec, var_ready, xn0_ready, xn_ready, xnT_ready)
            for s in marks:
                dve.sem_inc(s.sem, 1)
            dve.memset(xnT[:], 0.0).then_inc(zeroed, 1)
            dve.wait_ge(zeroed, 1)
            dve.wait_ge(loaded_w, W_LOADED)
            with dve.Fori(0, B) as seq:
                def own(ins):
                    vec.need(dve, seq, vec.mark(ins))

                dve.wait_ge(loaded, seq * 16 + 16)
                half = seq % 2
                for c in range(C):
                    ins = dve.bn_stats(stat[:, c], xt[:, bass.ds(half, 1), c].squeeze(1))
                own(ins)
                dve.tensor_tensor(mean[:], stat[:, :, 1], stat[:, :, 4], ALU.add)
                dve.tensor_tensor(apart[:], stat[:, :, 1], stat[:, :, 4], ALU.subtract)
                own(dve.scalar_tensor_tensor(var[:], stat[:, :, 2], D * 1e-5, stat[:, :, 5], ALU.add, ALU.add))
                dve.tensor_scalar(mean[:], mean[:], 0.5, None, ALU.mult)
                own(dve.scalar_tensor_tensor(apart[:], apart[:], 0.25, apart[:], ALU.mult, ALU.mult))
                var_ready.mark(dve.scalar_tensor_tensor(var[:], var[:], 1.0 / D, apart[:], ALU.mult, ALU.add))
                rstd_ready.need(dve, seq, 1)
                dve.wait_ge(stored, seq * 16 + 1)
                for c in range(C):
                    xn0_ready.mark(dve.tensor_scalar(xn0[:, c], xt[:, bass.ds(half, 1), c].squeeze(1), mean[:, c:c + 1],
                                                     rstd[:, c:c + 1], ALU.subtract, ALU.mult))
                ss_ready.need(dve, seq, C)
                var_ready.mark(dve.tensor_scalar(var[:], ssum[:], 1.0 / D, 1e-6, ALU.mult, ALU.add))
                rstd_ready.need(dve, seq, 2)
                for c in range(C):
                    xn_ready.mark(dve.tensor_scalar(xn[:, c], xn0[:, c], rstd[:, c:c + 1], None, ALU.mult))
                for g in range(2):
                    t_xn.need(dve, seq, g + 1)
                    xnT_ready.mark(dve.tensor_scalar(
                        xnT[:, bass.ds(seq, 1), LEAD + PAD + 512 * g:LEAD + PAD + 512 * (g + 1)].squeeze(1),
                        bank[g][:], norm_w[:, 0:1], None, ALU.mult))
                own(dve.memset(apart[:], 0.0))
            for s in marks:
                s.close()


def scan_layer_blocks(nc, xnT, spread, out_rows, w, const):
    NS, K = 16, 2
    ROWS = K * B * NS
    GRP = B // 2
    DT_MID, DT_RAD = (0.1 + 0.001) / 2.0, (0.1 - 0.001) / 2.0
    with ExitStack() as ctx:
        def sb(name, shape, dt=F32):
            return ctx.enter_context(nc.sbuf_tensor("c1_" + name, shape, dt))

        def steps(name, per):
            return Steps(nc, "c1_" + name, per)

        bank = [ctx.enter_context(nc.psum_tensor(f"c1_bank{n}", [P, 512], F32)) for n in range(8)]
        w_x = sb("w_x", [D, K, P])
        w_gate = sb("w_gate", [D, K, P])
        taps = sb("taps", [P, TAPS1, K, P])
        w_conv = sb("w_conv", [D, TAPS1, K, P])
        w_dt = sb("w_dt", [P, K, K, P])
        w_bc = sb("w_bc", [P, K, 2, NS])
        w_out = sb("w_out", [P, K, D])
        conv_b = sb("conv_b", [P, K])
        b_dt = sb("b_dt", [P, K])
        a_log = sb("a_log", [P, K, NS])
        a_scale = sb("a_scale", [P, K, NS])
        d_col = sb("d_col", [P, K])
        d_diag = sb("d_diag", [P, K, P])
        ident = sb("ident", [P, P])
        ones = sb("ones", [P, P])
        dt_shift = sb("dt_shift", [P, 1])
        half_pow = sb("half_pow", [P, B])
        xc = sb("xc", [P, 2, K, B, 1 + BLK])
        sg = sb("sg", [P, 2, K, B, BLK])
        dabs = sb("dabs", [P, K, B, BLK])
        drel = sb("drel", [P, K, B, BLK])
        dt = sb("dt", [P, 2, K, B, BLK])
        dtx = sb("dtx", [P, 2, K, B, BLK])
        bc = sb("bc", [NS, 2, B, 2, SEG])
        rep = sb("rep", [P, 2, 2, B, 2, NS, SEG])
        decay = sb("decay", [P, 2, 2, ROWS, 1 + SEG])
        state = sb("state", [P, 2, 2, ROWS, 1 + SEG])
        sq = sb("sq", [P, K, B, NS])
        ssq = sb("ssq", [P, B])
        ssum = sb("ssum", [P, B])
        norm = sb("norm", [P, B])
        fac = sb("fac", [P, B])
        yg = sb("yg", [P, K, B, BLK])
        rows = sb("rows", [GRP * BLK, 2, D])

        loaded_w = nc.alloc_semaphore("c1_loaded_w")
        ready_w = nc.alloc_semaphore("c1_ready_w")
        a_ready = nc.alloc_semaphore("c1_a_ready")
        pool_own = nc.alloc_semaphore("c1_pool_own")
        spread_out = nc.alloc_semaphore("c1_spread_out")
        spread_in = [nc.alloc_semaphore(f"c1_spread_in{k}") for k in range(2)]
        stored = nc.alloc_semaphore("c1_stored")
        mm_x = steps("mm_x", 1)
        mm_dt = steps("mm_dt", 1)
        mm_norm = steps("mm_norm", 2)
        mm_y = steps("mm_y", 1)
        mm_out = steps("mm_out", 1)
        act_own = steps("act_own", 3)
        xc_ready = steps("xc_ready", 1)
        bc_ready = steps("bc_ready", 1)
        plus_ready = steps("plus_ready", 1)
        tanh_ready = steps("tanh_ready", 1)
        decay_ready = steps("decay_ready", 2)
        rows_ready = steps("rows_ready", 1)
        vec = steps("vec", 11)
        sp_ready = steps("sp_ready", 1)
        dt_ready = steps("dt_ready", 1)
        scan_ready = steps("scan_ready", 2)
        ssq_ready = steps("ssq_ready", 2)
        ssum_ready = steps("ssum_ready", 2)
        carried = steps("carried", 2)
        yg_ready = steps("yg_ready", 1)
        norm_ready = steps("norm_ready", 2)
        hc_ready = steps("hc_ready", 2)

        loads = [(w_x, w["W_xT"]), (w_gate, w["W_gateT"]), (taps, w["conv_w"].partition_broadcast(P)),
                 (w_dt, w["W_dtT"]), (w_bc, w["W_bcT"]), (w_out, w["W_outT"]), (conv_b, w["conv_b"]), (b_dt, w["b_dt"]),
                 (a_log, w["A_log"]), (d_col, w["D_col"]), (ident, const["ident"])]
        W_LOADED = 16 * len(loads)
        block = ctx.enter_context(nc.Block())

        def turns(eng, front, scan):
            front(0, 0)
            scan(0, 0, True, False)
            with eng.Fori(0, BLOCKS // 2 - 1) as pair:
                for j in (1, 2):
                    scan(pair * 2 + j, j % 2, False, False)
            scan(BLOCKS - 1, 1, False, True)

        @block.sync
        def _(sp):
            for to, of in loads:
                sp.dma_start(to[:], of).then_inc(loaded_w, 16)
            sp.sem_inc(stored, 1)
            sp.sem_inc(spread_out, 1)

            def front(blk, k):
                bc_ready.need(sp, blk, 1)
                for j in range(2):
                    sp.dma_start(spread[bass.ds(blk, 1), j].squeeze(0).rearrange("x n t -> n x t"),
                                 bc[:, j].rearrange("n b s t -> n (b s) t")).then_inc(spread_out, 16)
                sp.wait_ge(spread_out, blk * 32 + 33)
                if k or not isinstance(blk, int):
                    hc_ready.before(sp, blk, 2, 2)
                sp.dma_start(rep[:, k].rearrange("p j b s n t -> p (j b s n t)"),
                             spread[bass.ds(blk, 1)].squeeze(0).rearrange("j x n t -> (j x n t)").partition_broadcast(P)
                             ).then_inc(spread_in[k], 16)

            def store(blk):
                rows_ready.need(sp, blk, 1)
                for g in range(2):
                    sp.dma_start(out_rows[g * GRP:(g + 1) * GRP, bass.ds(blk * BLK, BLK)], rows[:, g]).then_inc(stored, 16)

            def scan(blk, k, first, last):
                if not last:
                    front(blk + 1, 1 - k)
                if not first:
                    store(blk - 1)

            turns(sp, front, scan)
            store(BLOCKS - 1)
            sp.wait_ge(stored, BLOCKS * 32 + 1)

        @block.gpsimd
        def _(pool):
            marks = (norm_ready, hc_ready)
            for s in marks:
                pool.sem_inc(s.sem, 1)
            pool.memset(half_pow[:], 0.5).then_inc(pool_own, 1)
            pool.wait_ge(pool_own, 1)

            def scan(blk, k, first, last):
                for seg in range(2):
                    ssum_ready.need(pool, blk, seg + 1)
                    norm_ready.mark(pool.tensor_tensor(norm[:], ssum[:], half_pow[:], ALU.pow))
                    for q in range(K):
                        h = state[:, k, seg, q * B * NS:(q + 1) * B * NS, 0:SEG].rearrange("p (b n) t -> p b n t", b=B)
                        ins = pool.tensor_tensor(h, h, rep[:, k, 1, :, seg], ALU.mult)
                    hc_ready.mark(ins)
                for s in marks:
                    s.close()

            turns(pool, lambda blk, k: None, scan)

        @block.scalar
        def _(act):
            marks = (act_own, xc_ready, bc_ready, plus_ready, tanh_ready, decay_ready)
            for s in marks + (rows_ready,):
                act.sem_inc(s.sem, 1)
            act.wait_ge(loaded_w, W_LOADED)
            act.activation(a_log[:], a_log[:], ACT.Tanh, scale=0.5 / (5.0 + 1e-8)).then_inc(a_ready, 1)
            act.wait_ge(a_ready, 1)
            act.activation(a_log[:], a_log[:], ACT.Exp, scale=10.0).then_inc(a_ready, 1)
            act.wait_ge(ready_w, 4)

            def front(blk, k):
                later = k or not isinstance(blk, int)
                mm_x.need(act, blk, 1)
                if later:
                    mm_y.before(act, blk, 2, 1)
                    yg_ready.before(act, blk, 2, 1)
                for q in range(K):
                    act.activation(xc[:, k, q], bank[0][:, q * B * (1 + BLK):(q + 1) * B * (1 + BLK)].rearrange("p (b t) -> p b t", b=B),
                                   ACT.Silu, bias=conv_b[:, q:q + 1])
                xc_ready.mark(act.activation(sg[:, k], bank[1][:, 0:K * B * BLK].rearrange("p (q b t) -> p q b t", q=K, b=B), ACT.Silu))
                mm_dt.need(act, blk, 1)
                act.wait_ge(spread_out, blk * 32 + 1)
                act.activation(bc[:, 0], bank[3][0:NS, 0:B * BLK].rearrange("n (b s t) -> n b s t", b=B, s=2), ACT.Copy)
                bc_ready.mark(act.activation(bc[:, 1], bank[3][0:NS, 256:256 + B * BLK].rearrange("n (b s t) -> n b s t", b=B, s=2), ACT.Copy))
                sp_ready.need(act, blk, 0)
                for q in range(K):
                    v = bank[2][:, q * B * BLK:(q + 1) * B * BLK].rearrange("p (b t) -> p b t", b=B)
                    act.activation(drel[:, q], v, ACT.Relu, bias=b_dt[:, q:q + 1])
                    ins = act.activation(dabs[:, q], v, ACT.Abs, bias=b_dt[:, q:q + 1])
                act_own.need(act, blk, act_own.mark(ins))
                act_own.need(act, blk, act_own.mark(act.activation(dabs[:], dabs[:], ACT.Exp, scale=-1.0)))
                plus_ready.mark(act.activation(dabs[:], dabs[:], ACT.Ln, bias=1.0))
                sp_ready.need(act, blk, 1)
                tanh_ready.mark(act.activation(dabs[:], drel[:], ACT.Tanh, scale=0.5 / (DT_RAD + 1e-8),
                                               bias=dt_shift[:, 0:1]))
                dt_ready.need(act, blk, 1)
                if later:
                    scan_ready.before(act, blk, 2, 2)
                d6 = decay[:, k].rearrange("p s (q b n) t -> p s q b n t", q=K, b=B)
                for q in range(K):
                    for n in range(NS):
                        ins = act.activation(d6[:, :, q, :, n, 1:1 + SEG], dt[:, k, q].rearrange("p b (s t) -> p s b t", s=2),
                                             ACT.Tanh, scale=a_scale[:, q, n:n + 1])
                act_own.need(act, blk, act_own.mark(ins))
                for seg in range(2):
                    part = decay[:, k, seg, :, 1:1 + SEG]
                    decay_ready.mark(act.activation(part, part, ACT.Exp, scale=16.0))
                for s in marks:
                    s.close()

            def out(blk):
                mm_out.need(act, blk, 1)
                act.wait_ge(stored, blk * 32 + 1)
                rows_ready.mark(act.activation(rows[:], bank[6][0:GRP * BLK, 0:2 * D].rearrange("p (g n) -> p g n", g=2), ACT.Copy))
                rows_ready.close()

            def scan(blk, k, first, last):
                if not last:
                    front(blk + 1, 1 - k)
                if not first:
                    out(blk - 1)

            turns(act, front, scan)
            out(BLOCKS - 1)

        @block.tensor
        def _(pe):
            marks = (mm_x, mm_dt, mm_norm, mm_y, mm_out)
            for s in marks:
                pe.sem_inc(s.sem, 1)
            pe.wait_ge(loaded_w, W_LOADED)
            pe.wait_ge(ready_w, 4)

            def project(blk, k):
                for q in range(K):
                    for j in range(TAPS1):
                        pe.matmul(bank[0][:, q * B * (1 + BLK):(q + 1) * B * (1 + BLK)], w_conv[:, j, q],
                                  xnT[:, :, bass.ds(blk * BLK + j, 1 + BLK)], start=(j == 0), stop=(j == TAPS1 - 1))
                for q in range(K):
                    ins = pe.matmul(bank[1][:, q * B * BLK:(q + 1) * B * BLK], w_gate[:, q],
                                    xnT[:, :, bass.ds(blk * BLK + LEAD - 1, BLK)], start=True, stop=True)
                mm_x.mark(ins)
                mm_x.close()

            def inner(blk, k):
                xc_ready.need(pe, blk, 1)
                for m in range(K):
                    for q in range(K):
                        pe.matmul(bank[2][:, m * B * BLK:(m + 1) * B * BLK], w_dt[:, q, m], xc[:, k, q, :, 1:1 + BLK],
                                  start=(q == 0), stop=(q == K - 1))
                for j in range(2):
                    for q in range(K):
                        ins = pe.matmul(bank[3][0:NS, j * 256:j * 256 + B * BLK], w_bc[:, q, j], xc[:, k, q, :, 1 - j:1 - j + BLK],
                                        start=(q == 0), stop=(q == K - 1))
                mm_dt.mark(ins)
                mm_dt.close()

            def front(blk, k):
                project(blk, k)
                inner(blk, k)

            def norms(blk, seg):
                ssq_ready.need(pe, blk, seg + 1)
                mm_norm.mark(pe.matmul(bank[4][:, 0:B], ones[:], ssq[:], start=True, stop=True))

            def outputs(blk, k):
                hc_ready.need(pe, blk, 2)
                yg_ready.need(pe, blk, 0)
                s6 = state[:, k].rearrange("p s (q b n) t -> p q n b s t", q=K, b=B)
                for q in range(K):
                    to = bank[5][:, q * B * BLK:(q + 1) * B * BLK]
                    for n in range(NS):
                        pe.matmul(to, ident[:], s6[:, q, n, :, :, 0:SEG], start=(n == 0), stop=False)
                    ins = pe.matmul(to, d_diag[:, q], xc[:, k, q, :, 0:BLK], start=False, stop=True)
                mm_y.mark(ins)
                mm_y.close()

            def project_out(blk):
                yg_ready.need(pe, blk, 1)
                rows_ready.need(pe, blk, 0)
                for g in range(2):
                    for q in range(K):
                        ins = pe.matmul(bank[6][0:GRP * BLK, g * D:(g + 1) * D],
                                        yg[:, q, g * GRP:(g + 1) * GRP].rearrange("p b t -> p (b t)"), w_out[:, q],
                                        start=(q == 0), stop=(q == K - 1))
                mm_out.mark(ins)
                mm_out.close()

            def scan(blk, k, first, last):
                if not last:
                    project(blk + 1, 1 - k)
                norms(blk, 0)
                if not first:
                    outputs(blk - 1, 1 - k)
                if not last:
                    inner(blk + 1, 1 - k)
                norms(blk, 1)
                mm_norm.close()
                if not first:
                    project_out(blk - 1)

            turns(pe, front, scan)
            outputs(BLOCKS - 1, 1)
            project_out(BLOCKS - 1)

        @block.vector
        def _(dve):
            marks = (sp_ready, dt_ready, scan_ready, ssq_ready, ssum_ready, carried, yg_ready)
            for s in marks + (vec,):
                dve.sem_inc(s.sem, 1)
            dve.wait_ge(loaded_w, W_LOADED)
            for j in range(TAPS1):
                dve.tensor_tensor(w_conv[:, j], w_x[:], taps[:, j], ALU.mult)
            dve.memset(ones[:], 1.0)
            dve.memset(dt_shift[:], -DT_MID * 0.5 / (DT_RAD + 1e-8))
            for q in range(K):
                ins = dve.tensor_scalar(d_diag[:, q], ident[:], d_col[:, q:q + 1], None, ALU.mult)
            ins.then_inc(ready_w, 1)
            dve.wait_ge(a_ready, 2)
            dve.tensor_scalar(a_scale[:], a_log[:], -0.5 / (8.0 + 1e-8), None, ALU.mult).then_inc(ready_w, 1)
            for k in range(2):
                ins = dve.memset(decay[:, k, :, :, 0:1], 0.0)
            ins.then_inc(ready_w, 1)
            dve.memset(state[:, 0, 0, :, 0:1], 0.0).then_inc(ready_w, 1)
            dve.wait_ge(ready_w, 4)

            def step_size(blk, k):
                tanh_ready.need(dve, blk, 1)
                dt_ready.mark(dve.tensor_scalar(dt[:, k], dabs[:], 2.0 * DT_RAD, DT_MID, ALU.mult, ALU.add))
                dt_ready.need(dve, blk, 1)
                own(dve.tensor_tensor(dtx[:, k], dt[:, k], xc[:, k, :, :, 1:1 + BLK], ALU.mult))

            def inputs(blk, k, seg):
                for q in range(K):
                    to = state[:, k, seg, q * B * NS:(q + 1) * B * NS, 1:1 + SEG].rearrange("p (b n) t -> p b n t", b=B)
                    ins = dve.tensor_tensor(to, rep[:, k, 0, :, seg],
                                            wide(dtx[:, k, q, :, seg * SEG:(seg + 1) * SEG], 2, [P, B, NS, SEG]), ALU.mult)
                own(ins)

            def softplus(blk):
                plus_ready.need(dve, blk, 1)
                sp_ready.mark(dve.tensor_tensor(drel[:], drel[:], dabs[:], ALU.add))

            at = [0]

            def own(ins):
                vec.need(dve, at[0], vec.mark(ins))

            def front(blk, k):
                softplus(blk)
                tanh_ready.need(dve, blk, 1)
                dt_ready.mark(dve.tensor_scalar(dt[:, k], dabs[:], 2.0 * DT_RAD, DT_MID, ALU.mult, ALU.add))
                dt_ready.need(dve, blk, 1)
                dve.tensor_tensor(dtx[:, k], dt[:, k], xc[:, k, :, :, 1:1 + BLK], ALU.mult).then_inc(ready_w, 1)
                dve.wait_ge(ready_w, 5)
                dve.memset(dtx[:, k, :, :, 0:PAD], 0.0).then_inc(ready_w, 1)
                dve.wait_ge(ready_w, 6)
                dve.wait_ge(spread_in[k], 16)
                for q in range(K):
                    to = state[:, k, 0, q * B * NS:(q + 1) * B * NS, 1:1 + SEG].rearrange("p (b n) t -> p b n t", b=B)
                    ins = dve.tensor_tensor(to, rep[:, k, 0, :, 0], wide(dtx[:, k, q, :, 0:SEG], 2, [P, B, NS, SEG]), ALU.mult)
                ins.then_inc(ready_w, 1)
                dve.wait_ge(ready_w, 7)
                sp_ready.close()
                dt_ready.close()

            def segment(blk, k, seg):
                decay_ready.need(dve, blk, seg + 1)
                h = state[:, k, seg].rearrange("p r t -> p (r t)")
                scan_ready.mark(dve.tensor_tensor_scan(h, decay[:, k, seg].rearrange("p r t -> p (r t)"), h, 0.0, ALU.mult, ALU.add))
                scan_ready.need(dve, blk, seg + 1)
                last = state[:, k, seg, :, SEG:SEG + 1].rearrange("p (q b n) t -> p q b (n t)", q=K, b=B)
                own(dve.tensor_tensor(sq[:], last, last, ALU.mult))
                ssq_ready.mark(dve.tensor_reduce(ssq[:], sq[:].rearrange("p q b n -> p b q n"), AX_XY, ALU.add))

            def carry(blk, k, seg):
                mm_norm.need(dve, blk, seg + 1)
                ssum_ready.mark(dve.tensor_copy(ssum[:], bank[4][:, 0:B]))
                norm_ready.need(dve, blk, seg + 1)
                own(dve.tensor_scalar(fac[:], norm[:], 1e-8, None, ALU.add))
                own(dve.reciprocal(fac[:], fac[:]))
                own(dve.tensor_scalar(fac[:], fac[:], 20.0, 1.0, ALU.mult, ALU.min))
                to = state[:, k, 1] if seg == 0 else state[:, 1 - k, 0]
                last = state[:, k, seg, :, SEG:SEG + 1].rearrange("p (q b n) t -> p q b (n t)", q=K, b=B)
                carried.mark(dve.tensor_tensor(to[:, :, 0:1].rearrange("p (q b n) t -> p q b (n t)", q=K, b=B), last,
                                               fac[:].unsqueeze(1).unsqueeze(3).to_broadcast([P, K, B, NS]), ALU.mult))
                carried.need(dve, blk, seg + 1)

            def gate(blk, k):
                mm_y.need(dve, blk, 1)
                mm_out.need(dve, blk, 0)
                yg_ready.mark(dve.tensor_tensor(yg[:], bank[5][:, 0:K * B * BLK].rearrange("p (q b t) -> p q b t", q=K, b=B),
                                                sg[:, k], ALU.mult))
                yg_ready.close()

            def scan(blk, k, first, last):
                at[0] = blk
                segment(blk, k, 0)
                inputs(blk, k, 1)
                carry(blk, k, 0)
                segment(blk, k, 1)
                if not first:
                    gate(blk - 1, 1 - k)
                if not last:
                    softplus(blk + 1)
                if not last:
                    carry(blk, k, 1)
                    step_size(blk + 1, 1 - k)
                    dve.wait_ge(spread_in[1 - k], (blk + 1 - (1 - k)) * 8 + 16)
                    inputs(blk + 1, 1 - k, 0)
                    for s in (vec, sp_ready, dt_ready, scan_ready, ssq_ready, ssum_ready, carried):
                        s.close()
                else:
                    mm_norm.need(dve, blk, 2)
                    ssum_ready.mark(dve.tensor_copy(ssum[:], bank[4][:, 0:B]))
                    gate(blk, k)

            turns(dve, front, scan)


def scan_layer_end(nc, x_in, rows_in, out_rows, x_out, w, const):
    with ExitStack() as ctx:
        def sb(name, shape, dt=F32):
            return ctx.enter_context(nc.sbuf_tensor("c2_" + name, shape, dt))

        def steps(name, per):
            return Steps(nc, "c2_" + name, per)

        res = sb("res", [P, 1])
        minus_half = sb("minus_half", [P, C])
        xt = sb("xt", [P, 3, C, D])
        os = sb("os", [P, C, D])
        on = sb("on", [P, C, D])
        stat = sb("stat", [P, C, 6])
        mean = sb("mean", [P, C])
        apart = sb("apart", [P, C])
        var = sb("var", [P, C])
        rstd = sb("rstd", [P, C])
        loaded_w = nc.alloc_semaphore("c2_loaded_w")
        loaded = nc.alloc_semaphore("c2_loaded")
        stored = nc.alloc_semaphore("c2_stored")
        own_w = nc.alloc_semaphore("c2_own_w")
        own_w2 = nc.alloc_semaphore("c2_own_w2")
        pool_own = nc.alloc_semaphore("c2_pool_own")
        vec = steps("vec", 6)
        var_ready = steps("var_ready", 1)
        out_ready = steps("out_ready", C)
        rstd_ready = steps("rstd_ready", 1)
        views = [x_in.rearrange("b (c p) d -> b p c d", p=P), rows_in.rearrange("b (c p) d -> b p c d", p=P),
                 out_rows[:, SEG:SEG + L].rearrange("b (c p) d -> b p c d", p=P)]
        o_rows = x_out.rearrange("b (c p) d -> b p c d", p=P)
        block = ctx.enter_context(nc.Block())

        @block.sync
        def _(sp):
            sp.dma_start(res[:], w["residual_scale"].partition_broadcast(P)).then_inc(loaded_w, 16)
            sp.sem_inc(stored, 1)
            for j in range(3):
                sp.dma_start(xt[:, j], views[j][0]).then_inc(loaded, 16)
            with sp.Fori(0, B - 1) as seq:
                out_ready.need(sp, seq, C)
                sp.dma_start(o_rows[bass.ds(seq, 1)].squeeze(0), on[:]).then_inc(stored, 16)
                for j in range(3):
                    sp.dma_start(xt[:, j], views[j][bass.ds(seq + 1, 1)].squeeze(0)).then_inc(loaded, 16)
            out_ready.need(sp, B - 1, C)
            sp.dma_start(o_rows[B - 1], on[:]).then_inc(stored, 16)
            sp.wait_ge(stored, 16 * B + 1)

        @block.gpsimd
        def _(pool):
            pool.sem_inc(rstd_ready.sem, 1)
            pool.memset(minus_half[:], -0.5).then_inc(pool_own, 1)
            pool.wait_ge(pool_own, 1)
            with pool.Fori(0, B) as seq:
                var_ready.need(pool, seq, 1)
                rstd_ready.mark(pool.tensor_tensor(rstd[:], var[:], minus_half[:], ALU.pow))
            rstd_ready.close()

        @block.scalar
        def _(act):
            act.wait_ge(loaded_w, 16)
            act.activation(res[:], res[:], ACT.Sigmoid).then_inc(own_w, 1)

        @block.vector
        def _(dve):
            marks = (vec, var_ready, out_ready)
            for s in marks:
                dve.sem_inc(s.sem, 1)
            dve.wait_ge(own_w, 1)
            dve.tensor_scalar(res[:], res[:], 0.5, None, ALU.mult).then_inc(own_w2, 1)
            dve.wait_ge(own_w2, 1)
            with dve.Fori(0, B) as seq:
                def own(ins):
                    vec.need(dve, seq, vec.mark(ins))

                dve.wait_ge(loaded, seq * 48 + 48)
                own(dve.scalar_tensor_tensor(os[:], xt[:, 2], res[:, 0:1], xt[:, 1], ALU.mult, ALU.add))
                for c in range(C):
                    ins = dve.bn_stats(stat[:, c], os[:, c])
                own(ins)
                dve.tensor_tensor(mean[:], stat[:, :, 1], stat[:, :, 4], ALU.add)
                dve.tensor_tensor(apart[:], stat[:, :, 1], stat[:, :, 4], ALU.subtract)
                own(dve.scalar_tensor_tensor(var[:], stat[:, :, 2], D * 1e-5, stat[:, :, 5], ALU.add, ALU.add))
                dve.tensor_scalar(mean[:], mean[:], 0.5, None, ALU.mult)
                own(dve.scalar_tensor_tensor(apart[:], apart[:], 0.25, apart[:], ALU.mult, ALU.mult))
                var_ready.mark(dve.scalar_tensor_tensor(var[:], var[:], 1.0 / D, apart[:], ALU.mult, ALU.add))
                rstd_ready.need(dve, seq, 1)
                for c in range(C):
                    ins = dve.tensor_scalar(os[:, c], os[:, c], mean[:, c:c + 1], rstd[:, c:c + 1], ALU.subtract, ALU.mult)
                own(ins)
                dve.wait_ge(stored, seq * 16 + 1)
                for c in range(C):
                    out_ready.mark(dve.tensor_tensor(on[:, c], os[:, c], xt[:, 0, c], ALU.add))
                own(dve.memset(apart[:], 0.0))
            for s in marks:
                s.close()


def scan_layer(nc, x_in, rows, spread, out_rows, x_out, w, const):
    with ExitStack() as ctx:
        xnT = ctx.enter_context(nc.sbuf_tensor("c_xnT", [D, B, LEAD + T_ALL], F32))
        scan_layer_rows(nc, x_in, rows, xnT, w, const)
        scan_layer_blocks(nc, xnT, spread, out_rows, w, const)
    scan_layer_end(nc, x_in, rows, out_rows, x_out, w, const)


def expert_layer(nc, x_in, x_out, w, const):
    E, W = 8, 128
    with ExitStack() as ctx:
        def sb(name, shape, dt=F32):
            return ctx.enter_context(nc.sbuf_tensor("d_" + name, shape, dt))

        def steps(name, per):
            return Steps(nc, "d_" + name, per)

        bank = [ctx.enter_context(nc.psum_tensor(f"d_bank{n}", [P, 512], F32)) for n in range(8)]
        w1 = sb("w1", [D, E, W])
        w2 = sb("w2", [W, E, D])
        router = sb("router", [D, E])
        ident = sb("ident", [P, P])
        number = sb("number", [P, E])
        minus_half = sb("minus_half", [P, C])
        xt = sb("xt", [P, 2, C, D])
        xn0 = sb("xn0", [P, C, D])
        xn = sb("xn", [P, C, D])
        stat = sb("stat", [P, C, 6])
        mean = sb("mean", [P, C])
        apart = sb("apart", [P, C])
        var = sb("var", [P, C])
        rstd = sb("rstd", [P, C])
        xnT = sb("xnT", [D, L])
        probs = sb("probs", [P, C, E])
        top = sb("top", [P, C, E])
        top_at = sb("top_at", [P, C, E], U32)
        top_no = sb("top_no", [P, C, 2])
        total = sb("total", [P, C])
        share = sb("share", [P, C, 2])
        picked = sb("picked", [P, 2, C, E])
        gate = sb("gate", [P, C, E])
        relu = sb("relu", [W, 2, 512])
        hid = sb("hid", [W, 2, E, 512])
        acc = sb("acc", [P, C, D])
        yo = sb("yo", [P, C, D])

        loaded_w = nc.alloc_semaphore("d_loaded_w")
        loaded = nc.alloc_semaphore("d_loaded")
        stored = nc.alloc_semaphore("d_stored")
        pool_own = nc.alloc_semaphore("d_pool_own")
        vec = steps("vec", 71)
        var_ready = steps("var_ready", 2)
        xn_ready = steps("xn_ready", C)
        y_read = steps("y_read", C)
        out_ready = steps("out_ready", C)
        xnT_ready = steps("xnT_ready", 2)
        probs_ready = steps("probs_ready", 1)
        relu_ready = steps("relu_ready", 2 * E)
        t_xn = steps("t_xn", 2)
        mm_router = steps("mm_router", 1)
        mm_hid = steps("mm_hid", 2 * E)
        mm_y = steps("mm_y", C)
        rstd_ready = steps("rstd_ready", 2)
        hid_ready = steps("hid_ready", 2 * E)

        x_rows = x_in.rearrange("b (c p) d -> b p c d", p=P)
        o_rows = x_out.rearrange("b (c p) d -> b p c d", p=P)
        loads = [(w1, w["w1"].rearrange("d (e n) -> d e n", e=E)),
                 (w2, w["w2"].rearrange("(e n) d -> n e d", e=E)),
                 (router, w["routerT"]), (ident, const["ident"]),
                 (number, const["expert_no"].partition_broadcast(P))]
        W_LOADED = 16 * len(loads)
        block = ctx.enter_context(nc.Block())

        @block.sync
        def _(sp):
            for to, of in loads:
                sp.dma_start(to[:], of).then_inc(loaded_w, 16)
            sp.sem_inc(stored, 1)
            sp.dma_start(xt[:, 0], x_rows[0]).then_inc(loaded, 16)
            with sp.Fori(0, B - 1) as seq:
                xn_ready.need(sp, seq, 1)
                sp.dma_start(xt[:, bass.ds((seq + 1) % 2, 1)].squeeze(1),
                             x_rows[bass.ds(seq + 1, 1)].squeeze(0)).then_inc(loaded, 16)
                out_ready.need(sp, seq, C)
                sp.dma_start(o_rows[bass.ds(seq, 1)].squeeze(0), yo[:]).then_inc(stored, 16)
            out_ready.need(sp, B - 1, C)
            sp.dma_start(o_rows[B - 1], yo[:]).then_inc(stored, 16)
            sp.wait_ge(stored, 16 * B + 1)

        @block.gpsimd
        def _(pool):
            for s in (rstd_ready, hid_ready):
                pool.sem_inc(s.sem, 1)
            pool.memset(minus_half[:], -0.5).then_inc(pool_own, 1)
            pool.wait_ge(pool_own, 1)
            with pool.Fori(0, B) as seq:
                def inverse_root(n):
                    var_ready.need(pool, seq, n)
                    rstd_ready.mark(pool.tensor_tensor(rstd[:], var[:], minus_half[:], ALU.pow))

                inverse_root(1)
                for n in range(2 * E):
                    g, e = divmod(n, E)
                    relu_ready.need(pool, seq, n + 1)
                    hid_ready.mark(pool.tensor_tensor(hid[:, g, e], relu[:, n % 2], relu[:, n % 2], ALU.mult))
                inverse_root(2)
            for s in (rstd_ready, hid_ready):
                s.close()

        @block.scalar
        def _(act):
            own = (xnT_ready, probs_ready, relu_ready)
            for s in own:
                act.sem_inc(s.sem, 1)
            with act.Fori(0, B) as seq:
                for g in range(2):
                    t_xn.need(act, seq, g + 1)
                    xnT_ready.mark(act.activation(xnT[:, 512 * g:512 * (g + 1)], bank[g][:], ACT.Copy))
                mm_router.need(act, seq, 1)
                probs_ready.mark(act.activation(probs[:], bank[2][:, 0:C * E].rearrange("p (c e) -> p c e", e=E),
                                                ACT.Sigmoid))
                for n in range(2 * E):
                    mm_hid.need(act, seq, n + 1)
                    if n >= 2:
                        hid_ready.need(act, seq, n - 1)
                    relu_ready.mark(act.activation(relu[:, n % 2], bank[n % 2][:], ACT.Relu))
            for s in own:
                s.close()

        @block.tensor
        def _(pe):
            own = (t_xn, mm_router, mm_hid, mm_y)
            for s in own:
                pe.sem_inc(s.sem, 1)
            pe.wait_ge(loaded_w, W_LOADED)
            with pe.Fori(0, B) as seq:
                for g in range(2):
                    for q in range(4):
                        xn_ready.need(pe, seq, 4 * g + q + 1)
                        ins = pe.transpose(bank[g][:, q * P:(q + 1) * P], xn0[:, 4 * g + q], ident[:])
                    t_xn.mark(ins)
                xnT_ready.need(pe, seq, 2)
                for c in range(C):
                    ins = pe.matmul(bank[2][:, c * E:(c + 1) * E], xnT[:, c * P:(c + 1) * P], router[:], start=True, stop=True)
                mm_router.mark(ins)

                def hidden(n):
                    g, e = divmod(n, E)
                    if n >= 2:
                        relu_ready.need(pe, seq, n - 1)
                    mm_hid.mark(pe.matmul(bank[n % 2][:], w1[:, e], xnT[:, 512 * g:512 * (g + 1)], start=True, stop=True))

                def experts_out(c):
                    if c % 4 == 0:
                        hid_ready.need(pe, seq, E * (c // 4 + 1))
                    if c >= 2:
                        y_read.need(pe, seq, c - 1)
                    for e in range(E):
                        ins = pe.matmul(bank[3 + 2 * (c % 2) + e // 4][:, (e % 4) * D:(e % 4 + 1) * D],
                                        hid[:, c // 4, e, (c % 4) * P:(c % 4 + 1) * P], w2[:, e], start=True, stop=True)
                    mm_y.mark(ins)

                for n in range(E):
                    hidden(n)
                for c in range(4):
                    hidden(E + 2 * c)
                    hidden(E + 2 * c + 1)
                    experts_out(c)
                for c in range(4, C):
                    experts_out(c)
            for s in own:
                s.close()

        @block.vector
        def _(dve):
            marks = (vec, var_ready, xn_ready, y_read, out_ready)
            for s in marks:
                dve.sem_inc(s.sem, 1)
            dve.wait_ge(loaded_w, W_LOADED)
            with dve.Fori(0, B) as seq:
                def own(ins):
                    vec.need(dve, seq, vec.mark(ins))

                rounds = [0]

                def normalise(to, of, eps, done=None):
                    for c in range(C):
                        ins = dve.bn_stats(stat[:, c], of(c))
                    own(ins)
                    dve.tensor_tensor(mean[:], stat[:, :, 1], stat[:, :, 4], ALU.add)
                    dve.tensor_tensor(apart[:], stat[:, :, 1], stat[:, :, 4], ALU.subtract)
                    own(dve.scalar_tensor_tensor(var[:], stat[:, :, 2], D * eps, stat[:, :, 5], ALU.add, ALU.add))
                    dve.tensor_scalar(mean[:], mean[:], 0.5, None, ALU.mult)
                    own(dve.scalar_tensor_tensor(apart[:], apart[:], 0.25, apart[:], ALU.mult, ALU.mult))
                    var_ready.mark(dve.scalar_tensor_tensor(var[:], var[:], 1.0 / D, apart[:], ALU.mult, ALU.add))
                    rounds[0] += 1
                    rstd_ready.need(dve, seq, rounds[0])
                    for c in range(C):
                        ins = dve.tensor_scalar(to[:, c], of(c), mean[:, c:c + 1], rstd[:, c:c + 1], ALU.subtract, ALU.mult)
                        if done:
                            done.mark(ins)
                    return ins

                dve.wait_ge(loaded, seq * 16 + 16)
                half = seq % 2
                normalise(xn0, lambda c: xt[:, bass.ds(half, 1), c].squeeze(1), 1e-5, done=xn_ready)
                probs_ready.need(dve, seq, 1)
                dve.memset(gate[:], 0.0)
                for c in range(C):
                    ins = dve.max(top[:, c], probs[:, c])
                own(ins)
                dve.memset(total[:], 0.0)
                for c in range(C):
                    ins = dve.max_index(top_at[:, c], top[:, c], probs[:, c])
                own(ins)
                own(dve.scalar_tensor_tensor(total[:], top[:, :, 0], 1e-20, top[:, :, 1], ALU.add, ALU.add))
                dve.tensor_copy(top_no[:], top_at[:, :, 0:2])
                own(dve.reciprocal(total[:], total[:]))
                own(dve.tensor_tensor(share[:], top[:, :, 0:2], wide(total[:], 2, [P, C, 2]), ALU.mult))
                for k in range(2):
                    ins = dve.tensor_tensor(picked[:, k], wide(number[:], 1, [P, C, E]),
                                            top_no[:, :, k:k + 1].to_broadcast([P, C, E]), ALU.is_equal)
                own(ins)
                for k in range(2):
                    ins = dve.tensor_tensor(picked[:, k], picked[:, k], share[:, :, k:k + 1].to_broadcast([P, C, E]), ALU.mult)
                own(ins)
                own(dve.tensor_tensor(gate[:], picked[:, 0], picked[:, 1], ALU.add))
                for c in range(C):
                    mm_y.need(dve, seq, c + 1)
                    for e in range(E):
                        of = bank[3 + 2 * (c % 2) + e // 4][:, (e % 4) * D:(e % 4 + 1) * D]
                        if e == 0:
                            own(dve.tensor_scalar(acc[:, c], of, gate[:, c, e:e + 1], None, ALU.mult))
                        else:
                            ins = dve.scalar_tensor_tensor(acc[:, c], of, gate[:, c, e:e + 1], acc[:, c], ALU.mult, ALU.add)
                            if e < E - 1:
                                own(ins)
                    y_read.mark(ins)
                y_read.need(dve, seq, C)
                own(normalise(xn, lambda c: acc[:, c], 1e-5))
                dve.wait_ge(stored, seq * 16 + 1)
                for c in range(C):
                    out_ready.mark(dve.tensor_tensor(yo[:, c], xn[:, c], xt[:, bass.ds(half, 1), c].squeeze(1), ALU.add))
            for s in marks:
                s.close()



def sandwich(nc, inputs, y):
    def scratch(name, shape):
        return nc.dram_tensor(name, shape, F32, kind="Internal").ap()

    def weights(prefix):
        return {n[len(prefix):]: ap for n, ap in inputs.items() if n.startswith(prefix)}

    after_mamba2, after_attention, after_scan = (scratch(n, [B, L, D]) for n in ("after_mamba2", "after_attention", "after_scan"))
    const = weights("const_")
    with nc.cleanup_on_exit():
        mamba2_layer(nc, inputs["x"], after_mamba2, weights("mamba2_"), const)
    with nc.cleanup_on_exit():
        attention_layer(nc, after_mamba2, after_attention, weights("attention_"), const)
    with nc.cleanup_on_exit():
        scan_layer(nc, after_attention, scratch("scan_rows", [B, L, D]), scratch("scan_spread", [BLOCKS, 2, 2 * B, 16, SEG]),
                   scratch("scan_out", [B, T_ALL, D]), after_scan, weights("scan_"), const)
    expert_layer(nc, after_scan, y, weights("expert_"), const)



def rotary_tables():
    import numpy as np
    n, window, width = L, 64, 64
    half = np.arange(0, width, 2, dtype=np.float32)
    inv_freq = (1 / np.float32(10000) ** (half / np.float32(width))).astype(np.float32)
    t = np.arange(n, dtype=np.float32)
    freqs = (t[:, None] * inv_freq).astype(np.float32).astype(np.float64)
    base = ((half + np.float32(0.4 * width)) / np.float32(1.4 * width)).astype(np.float32)
    scale = base.astype(np.float64) ** ((t - n // 2) / (window // 2))[:, None]
    freqs, scale = np.concatenate([freqs, freqs], 1), np.concatenate([scale, scale], 1)
    sign = np.repeat([-1.0, 1.0], width // 2)
    cos, sin = np.cos(freqs), np.sin(freqs) * sign
    tables = np.stack([cos * scale, sin * scale, cos / scale, sin / scale])
    return tables.reshape(4, C, P, width).transpose(2, 0, 1, 3).astype(np.float32)


def window_masks():
    import numpy as np
    i, j = np.arange(64)[:, None], np.arange(64)[None]
    own, before = j <= i, j >= i
    later = np.block([[own, before], [before, own]])
    first = later.copy()
    first[:64, 64:] = False
    return np.where(np.stack([first, later], 1), 0, MASKED).astype(mybir.dt.np(BF16))


def layout(given):
    import numpy as np

    def halves(v):
        return v.reshape(2, P).T

    m, a, s, e = ({n[len(p):]: v for n, v in given.items() if n.startswith(p)}
                  for p in ("L0_attn_", "L0_ffn_", "L1_attn_", "L1_ffn_"))
    upper = np.triu(np.ones((P, P), np.float32))

    def swapped(v):
        return np.concatenate([v[:, 32:], v[:, :32]], 1)

    w_in = s["W_in"].T
    out = {
        "x": m["x"],
        "const_ident": np.eye(P, dtype=np.float32),
        "const_upper": upper,
        "const_mask_upper": ((1 - upper) * MASKED).astype(mybir.dt.np(BF16)),
        "const_rotary": rotary_tables(),
        "const_window_masks": window_masks(),
        "const_expert_no": np.arange(8, dtype=np.float32),
        "mamba2_in_projT": m["in_proj_w"].T,
        "mamba2_conv_w": m["conv_w"][:, 0, :].T,
        "mamba2_conv_b": m["conv_b"].reshape(1, -1),
        "mamba2_conv_b_cols": m["conv_b"][256:].reshape(2, 64).T,
        "mamba2_ln_wb": np.stack([m["ln_w"], m["ln_b"]], 1),
        "mamba2_dt_bias": m["dt_bias"],
        "mamba2_A_log": m["A_log"],
        "mamba2_D_skip": m["D_skip"],
        "mamba2_norm_w": halves(m["norm_w"]),
        "mamba2_out_projT": m["out_proj_w"].T,
        "attention_wqkv": a["wqkv"],
        "attention_wo": a["wo"],
        "attention_w1": a["w1"],
        "attention_b1": a["b1"],
        "attention_w2": a["w2"],
        "attention_b2": a["b2"],
        "attention_ln_gb": np.stack([a["ln_g"], a["ln_b"]], -1).transpose(1, 0, 2),
        "attention_qk_scales": np.stack([a["q_scale"], swapped(a["q_scale"]), a["k_scale"], swapped(a["k_scale"])], 1),
        "scan_norm_w": s["norm_w"][:, None],
        "scan_W_xT": w_in[:, :256].reshape(P, 2, P),
        "scan_W_gateT": w_in[:, 256:].reshape(P, 2, P),
        "scan_conv_w": s["conv_w"][:, 0, :].T.reshape(4, 2, P),
        "scan_conv_b": halves(s["conv_b"]),
        "scan_b_dt": halves(s["b_dt"]),
        "scan_W_dtT": s["W_dt"].T.reshape(2, P, 2, P).transpose(1, 0, 2, 3),
        "scan_W_bcT": np.stack([s["W_B"].T.reshape(2, P, 16), s["W_C"].T.reshape(2, P, 16)], 2).transpose(1, 0, 2, 3),
        "scan_A_log": s["A_log"].reshape(2, P, 16).transpose(1, 0, 2),
        "scan_D_col": halves(s["D_param"]),
        "scan_W_outT": s["W_out"].T.reshape(2, P, P).transpose(1, 0, 2),
        "scan_residual_scale": s["residual_scale"].reshape(1),
        "expert_w1": e["w1"],
        "expert_w2": e["w2"],
        "expert_routerT": e["router_w"].T,
    }
    return {n: np.ascontiguousarray(v) for n, v in out.items()}


def kernel(**inputs):
    import concourse.bacc as bacc
    import numpy as np
    from concourse.bass_utils import run_bass_kernel_spmd

    nc = bacc.Bacc("TRN2", target_bir_lowering=False, num_devices=1)
    arrays = layout({n: np.asarray(v) for n, v in inputs.items()})
    aps = {n: nc.dram_tensor("in_" + n, v.shape, mybir.dt.from_np(v.dtype), kind="ExternalInput").ap() for n, v in arrays.items()}
    y = nc.dram_tensor("out_y", [B, L, D], F32, kind="ExternalOutput").ap()
    sandwich(nc, aps, y)
    got = run_bass_kernel_spmd(nc, [{"in_" + n: v for n, v in arrays.items()}], core_ids=[0])
    return got.results[0]["out_y"]
```

```python
from contextlib import ExitStack

import concourse.bass as bass
from concourse import mybir

F32 = mybir.dt.float32
BF16 = mybir.dt.bfloat16
U32 = mybir.dt.uint32
ALU = mybir.AluOpType
ACT = mybir.ActivationFunctionType
AX_X = mybir.AxisListType.X
AX_XY = mybir.AxisListType.XY

P = 128
D = 128
B = 8
L = 1024
C = L // P
MASKED = -1.0e30


class Steps:

    def __init__(self, nc, name, per):
        self.sem, self.name, self.per, self.n = nc.alloc_semaphore(name), name, per, 0

    def mark(self, ins):
        ins.then_inc(self.sem, 1)
        self.n += 1
        return self.n

    def need(self, eng, turn, n):
        eng.wait_ge(self.sem, turn * self.per + (1 + n))

    def before(self, eng, turn, back, n):
        eng.wait_ge(self.sem, turn * self.per + (1 + n - back * self.per))

    def close(self):
        assert self.n == self.per, (self.name, self.n, self.per)
        self.n = 0


def wide(ap, at, shape):
    return ap.unsqueeze(at).to_broadcast(shape)




def mamba2_layer(nc, x_in, x_out, w, const):
    H, HD, NS, DI = 4, 64, 64, 256
    TAPS = 4
    XB = DI + NS
    with ExitStack() as ctx:
        def sb(name, shape, dt=F32):
            return ctx.enter_context(nc.sbuf_tensor("a_" + name, shape, dt))

        def steps(name, per):
            return Steps(nc, "a_" + name, per)

        bank = [ctx.enter_context(nc.psum_tensor(f"a_bank{n}", [P, 512], F32)) for n in range(8)]
        w_in = sb("w_in", [D, 2 * DI + 2 * NS + H])
        taps = sb("taps", [P, TAPS, DI + 2 * NS])
        w_zdt = sb("w_zdt", [D, DI + H])
        w_conv = sb("w_conv", [D, TAPS, DI + 2 * NS])
        conv_b_row = sb("conv_b_row", [1, XB])
        conv_b_col = sb("conv_b_col", [NS, 2])
        ln_wb = sb("ln_wb", [D, 2])
        dt_bias = sb("dt_bias", [P, H])
        a_neg = sb("a_neg", [P, H])
        d_skip = sb("d_skip", [P, H])
        norm_w = sb("norm_w", [P, 2])
        w_out = sb("w_out", [P, 2, D])
        ident = sb("ident", [P, P])
        ident_b = sb("ident_b", [P, P], BF16)
        upper = sb("upper", [P, P])
        mask = sb("mask", [P, P], BF16)
        ones = sb("ones", [P, P])
        minus_half = sb("minus_half", [P, C])
        xt = sb("xt", [P, 2, C, D])
        xn0 = sb("xn0", [P, C, D])
        xn = sb("xn", [P, C, D])
        stat = sb("stat", [P, C, 6])
        mean = sb("mean", [P, C])
        apart = sb("apart", [P, C])
        var = sb("var", [P, C])
        rstd = sb("rstd", [P, C])
        xnT = sb("xnT", [D, TAPS - 1 + L])
        bT = sb("bT", [NS, L])
        cT = sb("cT", [NS, L])
        xsb = sb("xsb", [P, C, XB])
        zs = sb("zs", [P, C, DI])
        dt_raw = sb("dt_raw", [P, C, H])
        dt_abs = sb("dt_abs", [P, C, H])
        dt_exp = sb("dt_exp", [P, C, H])
        dt = sb("dt", [P, C, H])
        adt = sb("adt", [P, C, H])
        cs_neg = sb("cs_neg", [P, C, H])
        rest = sb("rest", [P, C, H])
        e_cs = sb("e_cs", [P, C, H])
        e_tot = sb("e_tot", [P, C, H])
        e_rest = sb("e_rest", [P, C, H])
        decay = sb("decay", [P, 2, H, P])
        gated = sb("gated", [P, 2, H, P])
        xdt = sb("xdt", [P, C, H, HD])
        xdec = sb("xdec", [P, C, H, HD])
        xskip = sb("xskip", [P, C, H, HD])
        state = sb("state", [NS, 2, H, HD])
        y1 = sb("y1", [P, H, HD])
        y2 = sb("y2", [P, H, HD])
        yg = sb("yg", [P, C, DI])
        sq = sb("sq", [P, DI])
        ssum = sb("ssum", [P, C])
        ygT = sb("ygT", [P, 2, 2, P])
        ot = sb("ot", [P, C, D])
        yo = sb("yo", [P, C, D])

        loaded_w = nc.alloc_semaphore("a_loaded_w")
        loaded = nc.alloc_semaphore("a_loaded")
        stored = nc.alloc_semaphore("a_stored")
        pool_own = nc.alloc_semaphore("a_pool_own")
        a_exp = nc.alloc_semaphore("a_exp")
        ready_w = nc.alloc_semaphore("a_ready_w")
        vec = steps("vec", 47)
        var_ready = steps("var_ready", 4)
        xn_ready = steps("xn_ready", C)
        dt_abs_ready = steps("dt_abs_ready", 1)
        dt_ready = steps("dt_ready", 1)
        cs_ready = steps("cs_ready", 1)
        gated_ready = steps("gated_ready", C)
        state_ready = steps("state_ready", C)
        yg_ready = steps("yg_ready", C)
        out_sum = steps("out_sum", C)
        out_ready = steps("out_ready", C)
        act_own = steps("act_own", 1)
        xnT_ready = steps("xnT_ready", 2)
        bcT_ready = steps("bcT_ready", 4)
        xsb_ready = steps("xsb_ready", C)
        dt_log_ready = steps("dt_log_ready", 1)
        decays_ready = steps("decays_ready", 1)
        decay_ready = steps("decay_ready", C)
        ss_ready = steps("ss_ready", C)
        ygT_ready = steps("ygT_ready", C)
        t_xn = steps("t_xn", 2)
        mm_bc = steps("mm_bc", 4)
        mm_xz = steps("mm_xz", C)
        mm_cs = steps("mm_cs", 1)
        mm_decay = steps("mm_decay", C)
        mm_scores = steps("mm_scores", C)
        mm_y = steps("mm_y", C)
        t_yg = steps("t_yg", C)
        mm_out = steps("mm_out", C)
        rstd_ready = steps("rstd_ready", 4)
        xdt_ready = steps("xdt_ready", C)
        xdec_ready = steps("xdec_ready", C)
        xskip_ready = steps("xskip_ready", C)

        x_rows = x_in.rearrange("b (c p) d -> b p c d", p=P)
        o_rows = x_out.rearrange("b (c p) d -> b p c d", p=P)
        loads = [(w_in, w["in_projT"]), (taps, w["conv_w"].partition_broadcast(P)),
                 (conv_b_row, w["conv_b"][0:1, 0:XB]), (conv_b_col, w["conv_b_cols"]),
                 (ln_wb, w["ln_wb"]), (dt_bias, w["dt_bias"].partition_broadcast(P)),
                 (a_neg, w["A_log"].partition_broadcast(P)),
                 (d_skip, w["D_skip"].partition_broadcast(P)), (norm_w, w["norm_w"]),
                 (w_out, w["out_projT"].rearrange("(k p) n -> p k n", p=P)),
                 (ident, const["ident"]), (upper, const["upper"]), (mask, const["mask_upper"])]
        W_LOADED = 16 * len(loads)
        block = ctx.enter_context(nc.Block())

        @block.sync
        def _(sp):
            for to, of in loads:
                sp.dma_start(to[:], of).then_inc(loaded_w, 16)

            sp.sem_inc(stored, 1)
            sp.dma_start(xt[:, 0], x_rows[0]).then_inc(loaded, 16)
            with sp.Fori(0, B - 1) as seq:
                xn_ready.need(sp, seq, 1)
                sp.dma_start(xt[:, bass.ds((seq + 1) % 2, 1)].squeeze(1),
                             x_rows[bass.ds(seq + 1, 1)].squeeze(0)).then_inc(loaded, 16)
                out_ready.need(sp, seq, C)
                sp.dma_start(o_rows[bass.ds(seq, 1)].squeeze(0), yo[:]).then_inc(stored, 16)
            out_ready.need(sp, B - 1, C)
            sp.dma_start(o_rows[B - 1], yo[:]).then_inc(stored, 16)
            sp.wait_ge(stored, 16 * B + 1)

        @block.gpsimd
        def _(pool):
            for s in (rstd_ready, xdt_ready, xdec_ready, xskip_ready):
                pool.sem_inc(s.sem, 1)
            pool.memset(minus_half[:], -0.5).then_inc(pool_own, 1)
            pool.wait_ge(pool_own, 1)
            with pool.Fori(0, B) as seq:
                def inverse_root(n):
                    var_ready.need(pool, seq, n)
                    rstd_ready.mark(pool.tensor_tensor(rstd[:], var[:], minus_half[:], ALU.pow))

                inverse_root(1)
                inverse_root(2)
                dt_ready.need(pool, seq, 1)
                for c in range(C):
                    xsb_ready.need(pool, seq, c + 1)
                    xs = xsb[:, c, 0:DI].rearrange("p (h e) -> p h e", h=H)
                    xdt_ready.mark(pool.tensor_tensor(
                        xdt[:, c], xs, wide(dt[:, c], 2, [P, H, HD]), ALU.mult))
                    xskip_ready.mark(pool.tensor_tensor(
                        xskip[:, c], xs, wide(d_skip[:], 2, [P, H, HD]), ALU.mult))
                decays_ready.need(pool, seq, 1)
                for c in range(C):
                    xdt_ready.need(pool, seq, c + 1)
                    xdec_ready.mark(pool.tensor_tensor(
                        xdec[:, c], xdt[:, c], wide(e_rest[:, c], 2, [P, H, HD]), ALU.mult))
                inverse_root(3)
                inverse_root(4)
            for s in (rstd_ready, xdt_ready, xdec_ready, xskip_ready):
                s.close()

        @block.scalar
        def _(act):
            for s in (act_own, xnT_ready, bcT_ready, xsb_ready, dt_log_ready,
                      decays_ready, decay_ready, ss_ready, ygT_ready):
                act.sem_inc(s.sem, 1)
            act.wait_ge(loaded_w, W_LOADED)
            act.activation(a_neg[:], a_neg[:], ACT.Exp).then_inc(a_exp, 1)
            with act.Fori(0, B) as seq:
                for g in range(2):
                    t_xn.need(act, seq, g + 1)
                    xnT_ready.mark(act.activation(
                        xnT[:, TAPS - 1 + 512 * g:TAPS - 1 + 512 * (g + 1)], bank[g][:], ACT.Identity,
                        bias=ln_wb[:, 1:2], scale=ln_wb[:, 0:1]))
                for g in range(2):
                    for k, to in enumerate((bT, cT)):
                        mm_bc.need(act, seq, 2 * g + k + 1)
                        bcT_ready.mark(act.activation(
                            to[:, 512 * g:512 * (g + 1)], bank[2 + 2 * g + k][0:NS, :], ACT.Silu,
                            bias=conv_b_col[:, k:k + 1]))
                for c in range(C):
                    mm_xz.need(act, seq, c + 1)
                    act.activation(dt_raw[:, c], bank[c % 2][:, DI:DI + H], ACT.Copy)
                    act.activation(zs[:, c], bank[c % 2][:, 0:DI], ACT.Silu)
                    xsb_ready.mark(act.activation(xsb[:, c], bank[6 + c % 2][:, 0:XB], ACT.Silu))
                dt_abs_ready.need(act, seq, 1)
                n = act_own.mark(act.activation(dt_exp[:], dt_abs[:], ACT.Exp, scale=-1.0))
                act_own.need(act, seq, n)
                dt_log_ready.mark(act.activation(dt_exp[:], dt_exp[:], ACT.Ln, bias=1.0))
                cs_ready.need(act, seq, 1)
                act.activation(e_cs[:], bank[2][:, 0:C * H].rearrange("p (c h) -> p c h", h=H), ACT.Exp)
                act.activation(e_tot[:], bank[2][:, C * H:2 * C * H].rearrange("p (c h) -> p c h", h=H), ACT.Exp)
                decays_ready.mark(act.activation(e_rest[:], rest[:], ACT.Exp))
                for c in range(C):
                    mm_decay.need(act, seq, c + 1)
                    if c >= 2:
                        gated_ready.need(act, seq, c - 1)
                    for h in range(H):
                        ins = act.activation(decay[:, c % 2, h], bank[3 + c % 2][:, h * P:(h + 1) * P],
                                             ACT.Exp, bias=cs_neg[:, c, h:h + 1])
                    decay_ready.mark(ins)
                for c in range(C):
                    yg_ready.need(act, seq, c + 1)
                    if c >= 1:
                        ss_ready.need(act, seq, c)
                    ss_ready.mark(act.activation(sq[:], yg[:, c], ACT.Square, accum_out=ssum[:, c:c + 1]))
                for c in range(C):
                    t_yg.need(act, seq, c + 1)
                    if c >= 2:
                        mm_out.need(act, seq, c - 1)
                    for k in range(2):
                        ins = act.activation(ygT[:, c % 2, k], bank[3 + c % 2][:, k * P:(k + 1) * P],
                                             ACT.Identity, bias=0.0, scale=norm_w[:, k:k + 1])
                    ygT_ready.mark(ins)
            for s in (act_own, xnT_ready, bcT_ready, xsb_ready, dt_log_ready,
                      decays_ready, decay_ready, ss_ready, ygT_ready):
                s.close()

        @block.tensor
        def _(pe):
            for s in (t_xn, mm_bc, mm_xz, mm_cs, mm_decay, mm_scores, mm_y, t_yg, mm_out):
                pe.sem_inc(s.sem, 1)
            pe.wait_ge(loaded_w, W_LOADED)
            pe.wait_ge(ready_w, 5)
            with pe.Fori(0, B) as seq:
                for g in range(2):
                    for q in range(4):
                        xn_ready.need(pe, seq, 4 * g + q + 1)
                        ins = pe.transpose(bank[g][:, q * P:(q + 1) * P], xn[:, 4 * g + q], ident[:])
                    t_xn.mark(ins)
                for g in range(2):
                    xnT_ready.need(pe, seq, g + 1)
                    for k in range(2):
                        for j in range(TAPS):
                            ins = pe.matmul(bank[2 + 2 * g + k][0:NS, :], w_conv[:, j, DI + k * NS:DI + (k + 1) * NS],
                                            xnT[:, 512 * g + j:512 * (g + 1) + j], start=(j == 0), stop=(j == TAPS - 1))
                        mm_bc.mark(ins)
                for c in range(C):
                    if c >= 2:
                        xsb_ready.need(pe, seq, c - 1)
                    for j in range(TAPS):
                        pe.matmul(bank[6 + c % 2][:, 0:XB], xnT[:, c * P + j:(c + 1) * P + j], w_conv[:, j, 0:XB],
                                  start=(j == 0), stop=False)
                    pe.matmul(bank[6 + c % 2][:, 0:XB], ones[0:1, :], conv_b_row[0:1, :], start=False, stop=True)
                    mm_xz.mark(pe.matmul(bank[c % 2][:, 0:DI + H], xnT[:, c * P + TAPS - 1:(c + 1) * P + TAPS - 1],
                                         w_zdt[:], start=True, stop=True))
                dt_ready.need(pe, seq, 1)
                bcT_ready.need(pe, seq, 4)
                flat = adt[:].rearrange("p c h -> p (c h)")
                pe.matmul(bank[2][:, 0:C * H], upper[:], flat, start=True, stop=True)
                mm_cs.mark(pe.matmul(bank[2][:, C * H:2 * C * H], ones[:], flat, start=True, stop=True))
                for c in range(C + 1):
                    if c < C:
                        if c >= 2:
                            decay_ready.need(pe, seq, c - 1)
                        pe.matmul(bank[3 + c % 2][:], ident_b[:], wide(mask[:], 1, [P, H, P]), start=True, stop=False)
                        for h in range(H):
                            ins = pe.matmul(bank[3 + c % 2][:, h * P:(h + 1) * P], adt[:, c, h:h + 1].to_broadcast([P, P]),
                                            upper[:], start=False, stop=(h == H - 1))
                        mm_decay.mark(ins)
                        if c >= 2:
                            gated_ready.need(pe, seq, c - 1)
                        mm_scores.mark(pe.matmul(bank[5 + c % 2][:, 0:P], bT[:, c * P:(c + 1) * P], cT[:, c * P:(c + 1) * P],
                                                 start=True, stop=True))
                    if c >= 1:
                        d = c - 1
                        gated_ready.need(pe, seq, d + 1)
                        xdec_ready.need(pe, seq, d + 1)
                        state_ready.need(pe, seq, d)
                        if d >= 2:
                            yg_ready.need(pe, seq, d - 1)
                        elif d == 0:
                            xsb_ready.need(pe, seq, C)
                        to = bank[(7, 0)[d % 2]]
                        for h in range(H):
                            pe.matmul(to[:, h * HD:(h + 1) * HD], gated[:, d % 2, h], xdt[:, d, h], start=True, stop=True)
                        pe.matmul(to[:, DI:2 * DI], cT[:, d * P:(d + 1) * P], state[:, d % 2].rearrange("p h e -> p (h e)"),
                                  start=True, stop=True)
                        mm_y.mark(pe.matmul(bank[(1, 2)[d % 2]][0:NS, 0:DI], xsb[:, d, DI:XB],
                                            xdec[:, d].rearrange("p h e -> p (h e)"), start=True, stop=True))
                for c in range(C + 1):
                    if c < C:
                        yg_ready.need(pe, seq, c + 1)
                        if c >= 2:
                            ygT_ready.need(pe, seq, c - 1)
                        else:
                            decay_ready.need(pe, seq, C)
                        for k in range(2):
                            ins = pe.transpose(bank[3 + c % 2][:, k * P:(k + 1) * P], yg[:, c, k * P:(k + 1) * P], ident[:])
                        t_yg.mark(ins)
                    if c >= 1:
                        ygT_ready.need(pe, seq, c)
                        if c >= 3:
                            out_sum.need(pe, seq, c - 2)
                        else:
                            gated_ready.need(pe, seq, C)
                        for k in range(2):
                            ins = pe.matmul(bank[5 + (c - 1) % 2][:, 0:D], ygT[:, (c - 1) % 2, k], w_out[:, k], start=(k == 0), stop=(k == 1))
                        mm_out.mark(ins)
            for s in (t_xn, mm_bc, mm_xz, mm_cs, mm_decay, mm_scores, mm_y, t_yg, mm_out):
                s.close()

        @block.vector
        def _(dve):
            for s in (vec, var_ready, xn_ready, dt_abs_ready, dt_ready, cs_ready, gated_ready,
                      state_ready, yg_ready, out_sum, out_ready):
                dve.sem_inc(s.sem, 1)
            dve.sem_inc(ready_w, 1)
            dve.wait_ge(loaded_w, W_LOADED)
            for j in range(TAPS):
                ins = dve.tensor_tensor(w_conv[:, j], w_in[:, DI:2 * DI + 2 * NS], taps[:, j], ALU.mult)
            ins.then_inc(ready_w, 1)
            dve.tensor_copy(w_zdt[:, 0:DI], w_in[:, 0:DI])
            dve.tensor_copy(w_zdt[:, DI:DI + H], w_in[:, 2 * DI + 2 * NS:]).then_inc(ready_w, 1)
            dve.memset(xnT[:, 0:TAPS - 1], 0.0)
            dve.memset(ones[:], 1.0)
            dve.tensor_copy(ident_b[:], ident[:]).then_inc(ready_w, 1)
            dve.wait_ge(a_exp, 1)
            dve.tensor_scalar(a_neg[:], a_neg[:], -1.0, None, ALU.mult).then_inc(ready_w, 1)
            dve.wait_ge(ready_w, 5)
            with dve.Fori(0, B) as seq:
                def own(ins):
                    vec.need(dve, seq, vec.mark(ins))

                rounds = [0]

                def normalise(to, of, eps, done=None, ready=None):
                    for c in range(C):
                        if ready:
                            ready(c)
                        ins = dve.bn_stats(stat[:, c], of(c))
                    own(ins)
                    dve.tensor_tensor(mean[:], stat[:, :, 1], stat[:, :, 4], ALU.add)
                    dve.tensor_tensor(apart[:], stat[:, :, 1], stat[:, :, 4], ALU.subtract)
                    own(dve.scalar_tensor_tensor(var[:], stat[:, :, 2], D * eps, stat[:, :, 5], ALU.add, ALU.add))
                    dve.tensor_scalar(mean[:], mean[:], 0.5, None, ALU.mult)
                    own(dve.scalar_tensor_tensor(apart[:], apart[:], 0.25, apart[:], ALU.mult, ALU.mult))
                    var_ready.mark(dve.scalar_tensor_tensor(var[:], var[:], 1.0 / D, apart[:], ALU.mult, ALU.add))
                    rounds[0] += 1
                    rstd_ready.need(dve, seq, rounds[0])
                    for c in range(C):
                        ins = dve.tensor_scalar(to[:, c], of(c), mean[:, c:c + 1], rstd[:, c:c + 1], ALU.subtract, ALU.mult)
                        if done:
                            done.mark(ins)
                    return ins

                dve.wait_ge(loaded, seq * 16 + 16)
                half = seq % 2
                own(normalise(xn0, lambda c: xt[:, bass.ds(half, 1), c].squeeze(1), 1e-5))
                normalise(xn, lambda c: xn0[:, c], 1e-5, done=xn_ready)
                xsb_ready.need(dve, seq, C)
                own(dve.tensor_tensor(dt_raw[:], dt_raw[:], wide(dt_bias[:], 1, [P, C, H]), ALU.add))
                dt_abs_ready.mark(dve.scalar_tensor_tensor(dt_abs[:], dt_raw[:], -1.0, dt_raw[:], ALU.mult, ALU.max))
                dt_log_ready.need(dve, seq, 1)
                own(dve.scalar_tensor_tensor(dt[:], dt_raw[:], 0.0, dt_exp[:], ALU.max, ALU.add))
                dt_ready.mark(dve.tensor_tensor(adt[:], dt[:], wide(a_neg[:], 1, [P, C, H]), ALU.mult))
                mm_cs.need(dve, seq, 1)
                cs = bank[2][:, 0:C * H].rearrange("p (c h) -> p c h", h=H)
                tot = bank[2][:, C * H:2 * C * H].rearrange("p (c h) -> p c h", h=H)
                own(dve.tensor_scalar(cs_neg[:], cs, -1.0, None, ALU.mult))
                own(dve.memset(state[:, 0], 0.0))
                cs_ready.mark(dve.tensor_tensor(rest[:], tot, cs_neg[:], ALU.add))
                decays_ready.need(dve, seq, 1)
                for c in range(C + 1):
                    if c < C:
                        decay_ready.need(dve, seq, c + 1)
                        mm_scores.need(dve, seq, c + 1)
                        if c >= 2:
                            mm_y.need(dve, seq, c - 1)
                        gated_ready.mark(dve.tensor_tensor(gated[:, c % 2], decay[:, c % 2],
                                                           wide(bank[5 + c % 2][:, 0:P], 1, [P, H, P]), ALU.mult))
                    if c >= 1:
                        d = c - 1
                        to = bank[(7, 0)[d % 2]]
                        mm_y.need(dve, seq, d + 1)
                        yg_ready.need(dve, seq, d)
                        own(dve.tensor_tensor(y1[:], to[:, DI:2 * DI].rearrange("p (h e) -> p h e", h=H),
                                              wide(e_cs[:, d], 2, [P, H, HD]), ALU.mult))
                        nxt = state[:, (d + 1) % 2]
                        own(dve.tensor_tensor(nxt, state[:, d % 2], wide(e_tot[0:NS, d], 2, [NS, H, HD]), ALU.mult))
                        own(dve.tensor_tensor(y2[:], to[:, 0:DI].rearrange("p (h e) -> p h e", h=H), y1[:], ALU.add))
                        state_ready.mark(dve.tensor_tensor(
                            nxt, bank[(1, 2)[d % 2]][0:NS, 0:DI].rearrange("p (h e) -> p h e", h=H), nxt, ALU.add))
                        xskip_ready.need(dve, seq, d + 1)
                        own(dve.tensor_tensor(y1[:], y2[:], xskip[:, d], ALU.add))
                        yg_ready.mark(dve.tensor_tensor(yg[:, d], y1[:].rearrange("p h e -> p (h e)"), zs[:, d], ALU.mult))
                        state_ready.need(dve, seq, d + 1)
                ss_ready.need(dve, seq, C)
                var_ready.mark(dve.tensor_scalar(var[:], ssum[:], 1.0 / DI, 1e-5, ALU.mult, ALU.add))
                rounds[0] += 1
                rstd_ready.need(dve, seq, rounds[0])
                for c in range(C):
                    mm_out.need(dve, seq, c + 1)
                    out_sum.mark(dve.scalar_tensor_tensor(ot[:, c], bank[5 + c % 2][:, 0:D], rstd[:, c:c + 1], xn0[:, c],
                                                          ALU.mult, ALU.add))
                out_sum.need(dve, seq, C)
                own(normalise(xn, lambda c: ot[:, c], 1e-5))
                dve.wait_ge(stored, seq * 16 + 1)
                for c in range(C):
                    out_ready.mark(dve.tensor_tensor(yo[:, c], xn[:, c], xt[:, bass.ds(half, 1), c].squeeze(1), ALU.add))
            for s in (vec, var_ready, xn_ready, dt_abs_ready, dt_ready, cs_ready, gated_ready,
                      state_ready, yg_ready, out_sum, out_ready):
                s.close()


def attention_layer(nc, x_in, x_out, w, const):
    DEPTH, H, HD, WIN = 2, 8, 64, 64
    INNER = H * HD
    HID = D * 4 * 2 // 3
    PAIRS = H // 2
    VW = HD + 1
    HALF = HD // 2
    UNITS = 2 * C
    NB1, NB2 = DEPTH * 2 * HID, DEPTH * D
    HID_TILES = [(0, P), (P, P), (2 * P, HID - 2 * P)]
    with ExitStack() as ctx:
        def sb(name, shape, dt=F32):
            return ctx.enter_context(nc.sbuf_tensor("b_" + name, shape, dt))

        def steps(name, per):
            return Steps(nc, "b_" + name, per)

        bank = [ctx.enter_context(nc.psum_tensor(f"b_bank{n}", [P, 512], F32)) for n in range(8)]
        w_qkv = sb("w_qkv", [D, DEPTH, 3, INNER])
        w_o = sb("w_o", [P, DEPTH, PAIRS, D])
        w1 = sb("w1", [D, DEPTH, 2, HID])
        bias_parts = sb("bias_parts", [2 * 32 + 1, NB1 + NB2], BF16)
        b1 = bias_parts[:, 0:NB1].rearrange("p (l a n) -> p l a n", l=DEPTH, a=2)
        b2 = bias_parts[:, NB1:NB1 + NB2].rearrange("p (l n) -> p l n", l=DEPTH)
        w2 = sb("w2", [P, DEPTH, 3, D])
        ln_gb = sb("ln_gb", [D, DEPTH, 2])
        ln_now = sb("ln_now", [D, 2])
        scales = sb("scales", [P, DEPTH, 4, HD])
        tab = sb("tab", [P, DEPTH, 4, C, HD])
        tab_now = sb("tab_now", [P, 4, C, HD])
        ident = sb("ident", [P, P])
        ident_b = sb("ident_b", [P, P], BF16)
        masks = sb("masks", [P, 3, P], BF16)
        ones = sb("ones", [2 * 32 + 1, P], BF16)
        minus_half = sb("minus_half", [P, 2 * H])
        xt = sb("xt", [P, 2, C, D])
        xr = sb("xr", [P, C, D])
        stat = sb("stat", [P, C, 6])
        mean = sb("mean", [P, C])
        apart = sb("apart", [P, C])
        var = sb("var", [P, C])
        rstd = sb("rstd", [P, C])
        hT = sb("hT", [D, L + 1])
        square = sb("square", [P, 2, 2, H, HD])
        ss = sb("ss", [P, 2, 2, H])
        inv = sb("inv", [P, 2, 2, H])
        rot_cos = sb("rot_cos", [P, 2, 2, H, HD])
        rot_sin = sb("rot_sin", [P, 2, 2, H, HD])
        rot = sb("rot", [P, 2, 2, H, HD])
        qT = sb("qT", [P, UNITS, PAIRS, P])
        rotary = qT[:].rearrange("p u j t -> p (u j t)")[:, 0:4 * C * HD].rearrange("p (a c e) -> p a c e", a=4, c=C)
        kT = sb("kT", [P, PAIRS, 2 * C + 1, WIN])
        v_own = sb("v_own", [P, C, H, VW])
        v_mix = sb("v_mix", [P, C + 1, H, VW])
        shifted_s = sb("shifted_s", [P, 2, PAIRS, P])
        k_raw = shifted_s[:].rearrange("p b j t -> p (b j t)").rearrange("p (b h e) -> p b h e", b=2, h=H)
        probs = sb("probs", [P, 2, PAIRS, P])
        row_max = sb("row_max", [P, 2, PAIRS])
        probsT = sb("probsT", [P, 2, PAIRS, P])
        inv_sum = sb("inv_sum", [P, 2, PAIRS])
        o_rows = sb("o_rows", [P, 2, 2, PAIRS, HD])
        spare = [t[:].rearrange("p a b h e -> p (a b h e)") for t in (rot, rot_cos, rot_sin)]
        oT = spare[0][:, 0:2 * PAIRS * P].rearrange("p (b f t) -> p b f t", b=2, f=PAIRS)
        sh = spare[1][:, 0:C * D].rearrange("p (c d) -> p c d", c=C)
        hn = spare[1][:, C * D:2 * C * D].rearrange("p (c d) -> p c d", c=C)
        x_next = spare[2][:, C * D:2 * C * D].rearrange("p (c d) -> p c d", c=C)
        last_rows = sb("last_rows", [P, C, D])
        hnT = hT[:, 1:L + 1]
        flat = square[:].rearrange("p a b h e -> p (a b h e)")
        gelu = flat[:, 0:2 * HID].rearrange("p (a n) -> p a n", a=2)
        prod = flat[:, 2 * HID:4 * HID].rearrange("p (a n) -> p a n", a=2)
        prodT = spare[2][:, 0:2 * 3 * P].rearrange("p (b j t) -> p b j t", b=2, j=3)
        bias_wide = flat[0:2 * 32 + 1, 0:NB1 + NB2]
        rounded = o_rows[:].rearrange("p b w j e -> p (b w j e)")[0:2 * 32 + 1, 0:(NB1 + NB2) // 2].bitcast(BF16)
        bias_rest = rot[:].rearrange("p a b h e -> p (a b h e)")[0:2 * 32 + 1, 0:NB1 + NB2]

        loaded_w = nc.alloc_semaphore("b_loaded_w")
        loaded = nc.alloc_semaphore("b_loaded")
        stored = nc.alloc_semaphore("b_stored")
        shifted = [nc.alloc_semaphore(f"b_shifted{g}") for g in range(2)]
        pool_own = nc.alloc_semaphore("b_pool_own")
        ready_w = nc.alloc_semaphore("b_ready_w")
        first_own = steps("first_own", 4)
        seq_own = steps("seq_own", 9)
        in_var = steps("in_var", 1)
        out_var = steps("out_var", 1)
        out_ready = steps("out_ready", C)
        seq_seen = steps("seq_seen", 1)
        vec = steps("vec", 56)
        block_ready = steps("block_ready", 1)
        ss_ready = steps("ss_ready", C)
        q_parts = steps("q_parts", C)
        rot_ready = steps("rot_ready", C)
        max_ready = steps("max_ready", UNITS)
        o_ready = steps("o_ready", UNITS)
        mid_ready = steps("mid_ready", C)
        var_ready = steps("var_ready", 2)
        hn_ready = steps("hn_ready", C)
        prod_ready = steps("prod_ready", C)
        end_ready = steps("end_ready", C)
        hT_ready = steps("hT_ready", 2)
        sq_ready = steps("sq_ready", C)
        k_ready = steps("k_ready", C)
        v_ready = steps("v_ready", C)
        qkT_ready = steps("qkT_ready", C)
        exp_ready = steps("exp_ready", UNITS)
        probsT_ready = steps("probsT_ready", UNITS)
        oT_ready = steps("oT_ready", C)
        hnT_ready = steps("hnT_ready", 2)
        gelu_ready = steps("gelu_ready", C)
        prodT_ready = steps("prodT_ready", C)
        t_x = steps("t_x", 2)
        mm_qkv = steps("mm_qkv", C)
        t_qk = steps("t_qk", C)
        mm_s = steps("mm_s", UNITS)
        t_p = steps("t_p", UNITS)
        mm_pv = steps("mm_pv", UNITS)
        t_o = steps("t_o", C)
        mm_o = steps("mm_o", C)
        t_h = steps("t_h", 2)
        mm_1 = steps("mm_1", C)
        t_prod = steps("t_prod", C)
        mm_2 = steps("mm_2", C)
        in_rstd = steps("in_rstd", 1)
        out_rstd = steps("out_rstd", 1)
        inv_ready = steps("inv_ready", C)
        k_parts = steps("k_parts", C)
        rstd_ready = steps("rstd_ready", 2)

        x_rows = x_in.rearrange("b (c p) d -> b p c d", p=P)
        y_rows = x_out.rearrange("b (c p) d -> b p c d", p=P)
        loads = [(w_qkv[:], w["wqkv"].rearrange("l d (j n) -> d l j n", j=3)),
                 (w1[:], w["w1"].rearrange("l d (j n) -> d l j n", j=2)),
                 (bias_wide[:, 0:NB1], w["b1"].rearrange("l n -> (l n)").partition_broadcast(2 * 32 + 1)),
                 (w2[:, :, 0], w["w2"][:, 0:P].rearrange("l p n -> p l n")),
                 (w2[:, :, 1], w["w2"][:, P:2 * P].rearrange("l p n -> p l n")),
                 (w2[0:HID - 2 * P, :, 2], w["w2"][:, 2 * P:HID].rearrange("l p n -> p l n")),
                 (bias_wide[:, NB1:NB1 + NB2], w["b2"].rearrange("l n -> (l n)").partition_broadcast(2 * 32 + 1)),
                 (ln_gb[:], w["ln_gb"]), (scales[:], w["qk_scales"].partition_broadcast(P)),
                 (rotary, const["rotary"]), (ident[:], const["ident"]), (masks[:], const["window_masks"])]
        for l in range(DEPTH):
            for i in range(2):
                for k in range(2):
                    rows = w["wo"][l].rearrange("(i k a d) n -> i k d a n", i=2, k=2, a=2)[i, k]
                    loads.append((w_o[k * HD:(k + 1) * HD, l, 2 * i:2 * i + 2], rows))
        W_LOADED = 16 * len(loads)
        SETUP = 8
        block = ctx.enter_context(nc.Block())

        @block.sync
        def _(sp):
            for to, of in loads:
                sp.dma_start(to, of).then_inc(loaded_w, 16)
            sp.sem_inc(stored, 1)
            sp.dma_start(xt[:, 0], x_rows[0]).then_inc(loaded, 16)

            def blocks(seq):
                with sp.Fori(0, DEPTH) as depth:
                    turn = seq * DEPTH + depth
                    for g in range(2):
                        mid_ready.need(sp, turn, 4 * (g + 1))
                        sp.dma_start(sh[1:P, 4 * g:4 * g + 4, HD:D], xr[0:P - 1, 4 * g:4 * g + 4, HD:D]).then_inc(shifted[g], 16)
                        sp.dma_start(sh[0:1, 1 + 3 * g:4 + 4 * g, HD:D],
                                     xr[P - 1:P, 3 * g:3 + 4 * g, HD:D]).then_inc(shifted[g], 16)

            def store(seq):
                out_ready.need(sp, seq, C)
                sp.dma_start(y_rows[bass.ds(seq, 1)].squeeze(0), last_rows[:]).then_inc(stored, 16)

            seq_seen.need(sp, 0, 1)
            sp.dma_start(xt[:, 1], x_rows[1]).then_inc(loaded, 16)
            with sp.Fori(0, B - 2) as seq:
                blocks(seq)
                store(seq)
                sp.dma_start(xt[:, bass.ds(seq % 2, 1)].squeeze(1), x_rows[bass.ds(seq + 2, 1)].squeeze(0)).then_inc(loaded, 16)
            for seq in (B - 2, B - 1):
                blocks(seq)
                store(seq)
            sp.wait_ge(stored, 16 * B + 1)

        @block.gpsimd
        def _(pool):
            marks = (in_rstd, out_rstd, inv_ready, k_parts, rstd_ready)
            for s in marks:
                pool.sem_inc(s.sem, 1)
            pool.memset(minus_half[:], -0.5).then_inc(pool_own, 1)
            pool.wait_ge(pool_own, 1)

            def inverse_root(var_ready, rstd_ready, turn):
                var_ready.need(pool, turn, 1)
                rstd_ready.mark(pool.tensor_tensor(rstd[:], var[:], minus_half[:, 0:C], ALU.pow))

            def sequence(seq, last):
                with pool.Fori(0, DEPTH) as depth:
                    turn = seq * DEPTH + depth
                    for c in range(C):
                        k = k_raw[:, c % 2]
                        k_ready.need(pool, turn, c + 1)
                        if c >= 2:
                            rot_ready.need(pool, turn, c - 1)
                        pool.tensor_tensor(rot_cos[:, c % 2, 1], k, wide(tab_now[:, 2, c], 1, [P, H, HD]), ALU.mult)
                        pool.tensor_tensor(rot_sin[:, c % 2, 1, :, 0:HALF], k[:, :, HALF:HD],
                                           wide(tab_now[:, 3, c, 0:HALF], 1, [P, H, HALF]), ALU.mult)
                        k_parts.mark(pool.tensor_tensor(rot_sin[:, c % 2, 1, :, HALF:HD], k[:, :, 0:HALF],
                                                        wide(tab_now[:, 3, c, HALF:HD], 1, [P, H, HALF]), ALU.mult))
                        ss_ready.need(pool, turn, c + 1)
                        inv_ready.mark(pool.tensor_tensor(
                            inv[:, c % 2].rearrange("p a h -> p (a h)"), ss[:, c % 2].rearrange("p a h -> p (a h)"),
                            minus_half[:], ALU.pow))
                    for g in range(2):
                        var_ready.need(pool, turn, g + 1)
                        rstd_ready.mark(pool.tensor_tensor(rstd[:, 4 * g:4 * g + 4], var[:, 4 * g:4 * g + 4],
                                                           minus_half[:, 0:4], ALU.pow))
                if not last:
                    inverse_root(in_var, in_rstd, seq + 1)
                inverse_root(out_var, out_rstd, seq)
                for s in marks:
                    s.n = 0

            inverse_root(in_var, in_rstd, 0)
            with pool.Fori(0, B - 1) as seq:
                sequence(seq, False)
            sequence(B - 1, True)

        @block.scalar
        def _(act):
            marks = (hT_ready, sq_ready, k_ready, v_ready, qkT_ready, exp_ready, probsT_ready, oT_ready, hnT_ready,
                     gelu_ready, prodT_ready)
            for s in marks:
                act.sem_inc(s.sem, 1)
            act.wait_ge(ready_w, SETUP)
            with act.Fori(0, B) as seq:
                with act.Fori(0, DEPTH) as depth:
                    turn = seq * DEPTH + depth
                    for g in range(2):
                        t_x.need(act, turn, g + 1)
                        act.activation(hT[0:HD, 512 * g:512 * (g + 1)], bank[g][0:HD, :], ACT.Copy)
                        hT_ready.mark(act.activation(hT[HD:D, 512 * g + 1:512 * (g + 1) + 1], bank[g][HD:D, :], ACT.Copy))

                    def transposed(c):
                        t_qk.need(act, turn, c + 1)
                        for a in range(2):
                            rows = slice(a * HD, (a + 1) * HD)
                            act.activation(qT[rows, 2 * c:2 * c + 2, :, rows],
                                           bank[6][rows].rearrange("p (j w t) -> p w j t", j=PAIRS, w=2), ACT.Copy)
                        qkT_ready.mark(act.activation(
                            kT[:, :, 2 * c + 1:2 * c + 3], bank[7][:].rearrange("p (j w t) -> p j w t", j=PAIRS, w=2), ACT.Copy))

                    for c in range(C):
                        q, k, v = (bank[3 * (c % 2) + j][:].rearrange("p (h e) -> p h e", h=H) for j in range(3))
                        mm_qkv.need(act, turn, c + 1)
                        if c >= 2:
                            ss_ready.need(act, turn, c - 1)
                            k_parts.need(act, turn, c - 1)
                        act.activation(square[:, c % 2, 0], q, ACT.Square)
                        sq_ready.mark(act.activation(square[:, c % 2, 1], k, ACT.Square))
                        k_ready.mark(act.activation(k_raw[:, c % 2], k, ACT.Copy))
                        act.activation(v_own[:, c, :, 0:HD], v, ACT.Copy)
                        act.activation(v_mix[0:WIN, c, :, 0:HD], v[0:WIN], ACT.Copy)
                        v_ready.mark(act.activation(v_mix[WIN:P, c + 1, :, 0:HD], v[WIN:P], ACT.Copy))
                        if c >= 2:
                            transposed(c - 2)

                    def copy_probs(u):
                        t_p.need(act, turn, u + 1)
                        if u >= 2:
                            mm_pv.need(act, turn, u - 1)
                        probsT_ready.mark(act.activation(
                            probsT[:, u % 2], bank[2 + u % 2][:].rearrange("p (j t) -> p j t", j=PAIRS), ACT.Copy))

                    def copy_o(c):
                        t_o.need(act, turn, c + 1)
                        if c >= 2:
                            mm_o.need(act, turn, c - 1)
                        oT_ready.mark(act.activation(
                            oT[:, c % 2].rearrange("p f (w t) -> p w f t", w=2),
                            bank[6][:].rearrange("p (w f t) -> p w f t", w=2, f=PAIRS), ACT.Copy))

                    for u in range(UNITS + 3):
                        if u < UNITS:
                            max_ready.need(act, turn, u + 1)
                            if u >= 2:
                                t_p.need(act, turn, u - 1)
                            exp_ready.mark(act.activation(probs[:, u % 2], shifted_s[:, u % 2], ACT.Exp))
                        if 1 <= u <= UNITS:
                            copy_probs(u - 1)
                        if u < 2:
                            transposed(C - 2 + u)
                        if u >= 4 and u % 2 == 0:
                            copy_o(u // 2 - 2)
                    def copy_h(g):
                        t_h.need(act, turn, g + 1)
                        hnT_ready.mark(act.activation(hnT[:, 512 * g:512 * (g + 1)], bank[4 + g][:], ACT.Identity,
                                                      bias=ln_now[:, 1:2], scale=ln_now[:, 0:1]))

                    copy_h(0)
                    for c in range(C + 1):
                        if c < C:
                            mm_1.need(act, turn, c + 1)
                            if c >= 2:
                                prod_ready.need(act, turn, c - 1)
                            gelu_ready.mark(act.activation(gelu[:, c % 2], bank[2 + c % 2][:, 0:HID], ACT.Gelu))
                        if c == 3:
                            copy_h(1)
                        if c >= 1:
                            d = c - 1
                            t_prod.need(act, turn, d + 1)
                            if d >= 2:
                                mm_2.need(act, turn, d - 1)
                            act.activation(prodT[:, d % 2, 0:2], bank[4 + d % 2][:, 0:2 * P].rearrange("p (j t) -> p j t", j=2), ACT.Copy)
                            prodT_ready.mark(act.activation(prodT[0:HID - 2 * P, d % 2, 2], bank[4 + d % 2][0:HID - 2 * P, 2 * P:3 * P], ACT.Copy))
            for s in marks:
                s.close()

        @block.tensor
        def _(pe):
            marks = (t_x, mm_qkv, t_qk, mm_s, t_p, mm_pv, t_o, mm_o, t_h, mm_1, t_prod, mm_2)
            for s in marks:
                pe.sem_inc(s.sem, 1)
            pe.wait_ge(loaded_w, W_LOADED)
            pe.wait_ge(ready_w, SETUP)
            with pe.Fori(0, B) as seq:
                with pe.Fori(0, DEPTH) as depth:
                    turn = seq * DEPTH + depth
                    block_ready.need(pe, turn, 1)
                    for g in range(2):
                        for j in range(4):
                            ins = pe.transpose(bank[g][:, j * P:(j + 1) * P], xr[:, 4 * g + j], ident[:])
                        t_x.mark(ins)
                    hT_ready.need(pe, turn, 2)

                    def transpose_qk(c):
                        if c >= 1:
                            qkT_ready.need(pe, turn, c)
                        rot_ready.need(pe, turn, c + 1)
                        for a in range(2):
                            for j in range(PAIRS):
                                ins = pe.transpose(bank[6 + a][:, j * P:(j + 1) * P],
                                                   rot[:, c % 2, a, 2 * j:2 * j + 2].rearrange("p h e -> p (h e)"), ident[:])
                        t_qk.mark(ins)

                    for c in range(C):
                        if c >= 2:
                            v_ready.need(pe, turn, c - 1)
                            q_parts.need(pe, turn, c - 1)
                        for j in range(3):
                            ins = pe.matmul(bank[3 * (c % 2) + j][:], hT[:, c * P:(c + 1) * P],
                                            w_qkv[:, bass.ds(depth, 1), j].squeeze(1), start=True, stop=True)
                        mm_qkv.mark(ins)
                        if c >= 2:
                            transpose_qk(c - 2)

                    def scores(u):
                        to = bank[u % 2]
                        if u >= 2:
                            max_ready.need(pe, turn, u - 1)
                        elif u == 0:
                            q_parts.need(pe, turn, C - 1)
                        else:
                            k_ready.need(pe, turn, C - 1)
                        qkT_ready.need(pe, turn, u // 2 + 1)
                        pe.matmul(to[:], ident_b[:], wide(masks[:, 0 if u == 0 else 1 + u % 2], 1, [P, PAIRS, P]), start=True, stop=False)
                        for j in range(PAIRS):
                            last = j == PAIRS - 1
                            if u % 2:
                                ins = pe.matmul(to[:, j * P:(j + 1) * P], qT[:, u, j],
                                                kT[:, j, u:u + 2].rearrange("p w t -> p (w t)"), start=False, stop=last)
                            else:
                                pe.matmul(to[:, j * P:j * P + WIN], qT[:, u, j], kT[:, j, u + 1], start=False, stop=False)
                                ins = pe.matmul(to[:, j * P + WIN:(j + 1) * P], qT[:, u, j], kT[:, j, u], start=False, stop=last)
                        mm_s.mark(ins)

                    def transpose_probs(u):
                        exp_ready.need(pe, turn, u + 1)
                        if u >= 2:
                            probsT_ready.need(pe, turn, u - 1)
                        elif u == 0:
                            v_ready.need(pe, turn, C - 1)
                        else:
                            q_parts.need(pe, turn, C)
                        for j in range(PAIRS):
                            ins = pe.transpose(bank[2 + u % 2][:, j * P:(j + 1) * P], probs[:, u % 2, j], ident[:])
                        t_p.mark(ins)

                    def values(u):
                        v = v_own if u % 2 else v_mix
                        probsT_ready.need(pe, turn, u + 1)
                        if u >= 2:
                            o_ready.need(pe, turn, u - 1)
                        elif u == 0:
                            v_ready.need(pe, turn, C)
                        for j in range(PAIRS):
                            for a in range(2):
                                rows = slice(a * WIN, (a + 1) * WIN)
                                ins = pe.matmul(bank[4 + u % 2][rows, j * VW:(j + 1) * VW], probsT[:, u % 2, j, rows],
                                                v[:, u // 2, 2 * j + a], start=True, stop=True)
                        mm_pv.mark(ins)

                    def transpose_o(c):
                        o_ready.need(pe, turn, 2 * c + 2)
                        if c >= 1:
                            oT_ready.need(pe, turn, c)
                        else:
                            qkT_ready.need(pe, turn, C)
                        for n in range(4):
                            i = n % 2
                            ins = pe.transpose(bank[6][:, n * P:(n + 1) * P],
                                               o_rows[:, c % 2, n // 2, 2 * i:2 * i + 2].rearrange("p j e -> p (j e)"), ident[:])
                        t_o.mark(ins)

                    def project(c):
                        oT_ready.need(pe, turn, c + 1)
                        if c >= 1:
                            mid_ready.need(pe, turn, c)
                        for j in range(PAIRS):
                            ins = pe.matmul(bank[7][:, 0:D], oT[:, c % 2, j], w_o[:, bass.ds(depth, 1), j].squeeze(1),
                                            start=(j == 0), stop=(j == PAIRS - 1))
                        mm_o.mark(ins)

                    for u in range(UNITS + 5):
                        if u < UNITS:
                            scores(u)
                        if 1 <= u <= UNITS:
                            transpose_probs(u - 1)
                        if u < 2:
                            transpose_qk(C - 2 + u)
                        if 2 <= u <= UNITS + 1:
                            values(u - 2)
                        if u >= 4 and u % 2 == 0 and u // 2 - 2 < C:
                            transpose_o(u // 2 - 2)
                        if u >= 5 and u % 2 == 1 and (u - 5) // 2 < C:
                            project((u - 5) // 2)

                    def transpose_h(g):
                        if g:
                            prodT_ready.need(pe, turn, 2)
                        for j in range(4):
                            hn_ready.need(pe, turn, 4 * g + j + 1)
                            ins = pe.transpose(bank[4 + g][:, j * P:(j + 1) * P], hn[:, 4 * g + j], ident[:])
                        t_h.mark(ins)

                    transpose_h(0)

                    def up(c):
                        if c >= 2:
                            prod_ready.need(pe, turn, c - 1)
                        hnT_ready.need(pe, turn, c // 4 + 1)
                        for j in range(2):
                            to = bank[2 * j + c % 2][:, 0:HID]
                            pe.matmul(to, hnT[:, c * P:(c + 1) * P], w1[:, bass.ds(depth, 1), j].squeeze(1), start=True, stop=False)
                            ins = pe.matmul(to, ones[:], b1[:, bass.ds(depth, 1), j].squeeze(1), start=False, stop=True)
                        mm_1.mark(ins)

                    def transpose_prod(c):
                        prod_ready.need(pe, turn, c + 1)
                        if c >= 2:
                            prodT_ready.need(pe, turn, c - 1)
                        if c == 3:
                            hnT_ready.need(pe, turn, 2)
                        for j, (a, n) in enumerate(HID_TILES):
                            ins = pe.transpose(bank[4 + c % 2][0:n, j * P:(j + 1) * P], prod[:, c % 2, a:a + n], ident[:])
                        t_prod.mark(ins)

                    def down(c):
                        prodT_ready.need(pe, turn, c + 1)
                        if c >= 2:
                            end_ready.need(pe, turn, c - 1)
                        to = bank[6 + c % 2][:, 0:D]
                        for j, (a, n) in enumerate(HID_TILES):
                            pe.matmul(to, prodT[0:n, c % 2, j], w2[0:n, bass.ds(depth, 1), j].squeeze(1), start=(j == 0), stop=False)
                        mm_2.mark(pe.matmul(to, ones[:], b2[:, bass.ds(depth, 1)].squeeze(1), start=False, stop=True))

                    for c in range(C + 2):
                        if c < C:
                            up(c)
                        if c == 3:
                            transpose_h(1)
                        if 1 <= c <= C:
                            transpose_prod(c - 1)
                        if c >= 2:
                            down(c - 2)
            for s in marks:
                s.close()

        @block.vector
        def _(dve):
            per_block = (vec, ss_ready, q_parts, rot_ready, max_ready, o_ready, mid_ready, var_ready, hn_ready,
                         prod_ready, end_ready)
            marks = (first_own, seq_own, in_var, out_var, out_ready, seq_seen, vec, block_ready, ss_ready, q_parts, rot_ready, max_ready,
                     o_ready, mid_ready, var_ready, hn_ready, prod_ready, end_ready)
            for s in marks:
                dve.sem_inc(s.sem, 1)
            dve.wait_ge(loaded_w, W_LOADED)
            dve.tensor_copy(ident_b[:], ident[:])
            dve.memset(ones[:], 1.0)
            dve.memset(hT[HD:D, 0:1], 0.0)
            dve.memset(kT[:, :, 0], 0.0)
            dve.memset(v_own[:, :, :, HD:VW], 1.0)
            dve.memset(v_mix[:, :, :, HD:VW], 1.0)
            dve.memset(v_mix[WIN:P, 0, :, 0:HD], 0.0)
            dve.memset(bias_parts[:], 0.0).then_inc(ready_w, 1)
            for l in range(DEPTH):
                for j in range(4):
                    ins = dve.tensor_tensor(tab[:, l, j], rotary[:, j], wide(scales[:, l, j], 1, [P, C, HD]), ALU.mult)
            ins.then_inc(ready_w, 1)
            dve.wait_ge(ready_w, 2)
            dve.tensor_scalar(tab[:, :, 0:2], tab[:, :, 0:2], 8.0, None, ALU.mult)
            dve.memset(qT[:], 0.0)
            rest = bias_wide
            for n in range(3):
                at = slice(32 * n, 32 * n + 1)
                dve.tensor_copy(rounded, rest).then_inc(ready_w, 1)
                dve.wait_ge(ready_w, 3 + 2 * n)
                dve.tensor_copy(bias_parts[at], rounded[at])
                dve.tensor_tensor(bias_rest, rest, rounded, ALU.subtract).then_inc(ready_w, 1)
                dve.wait_ge(ready_w, 4 + 2 * n)
                rest = bias_rest
            dve.wait_ge(ready_w, SETUP)
            def statistics(own, of, eps, var_mark, lo=0, hi=C):
                for c in range(lo, hi):
                    ins = dve.bn_stats(stat[:, c], of(c))
                own(ins)
                st, m, a, v = stat[:, lo:hi], mean[:, lo:hi], apart[:, lo:hi], var[:, lo:hi]
                dve.tensor_tensor(m, st[:, :, 1], st[:, :, 4], ALU.add)
                dve.tensor_tensor(a, st[:, :, 1], st[:, :, 4], ALU.subtract)
                own(dve.scalar_tensor_tensor(v, st[:, :, 2], D * eps, st[:, :, 5], ALU.add, ALU.add))
                dve.tensor_scalar(m, m, 0.5, None, ALU.mult)
                own(dve.scalar_tensor_tensor(a, a, 0.25, a, ALU.mult, ALU.mult))
                var_mark(dve.scalar_tensor_tensor(v, v, 1.0 / D, a, ALU.mult, ALU.add))

            def normalise(to, of, done=None, lo=0, hi=C):
                for c in range(lo, hi):
                    ins = dve.tensor_scalar(to[:, c], of(c), mean[:, c:c + 1], rstd[:, c:c + 1], ALU.subtract, ALU.mult)
                    if done:
                        done.mark(ins)
                return ins

            def tables(depth):
                dve.tensor_copy(ln_now[:], ln_gb[:, depth])
                block_ready.mark(dve.tensor_copy(tab_now[:], tab[:, depth]))
                block_ready.n = 0

            def transformer(turn, prefetch):
                block_ready.need(dve, turn, 1)

                def own(ins):
                    vec.need(dve, turn, vec.mark(ins))

                def rotate(c):
                    k_parts.need(dve, turn, c + 1)
                    own(dve.tensor_tensor(rot_sin[:, c % 2], rot_cos[:, c % 2], rot_sin[:, c % 2], ALU.add))
                    inv_ready.need(dve, turn, c + 1)
                    if c >= 2:
                        t_qk.need(dve, turn, c - 1)
                    rot_ready.mark(dve.tensor_tensor(
                        rot[:, c % 2].rearrange("p a h e -> p (a h) e"), rot_sin[:, c % 2].rearrange("p a h e -> p (a h) e"),
                        wide(inv[:, c % 2].rearrange("p a h -> p (a h)"), 2, [P, 2 * H, HD]), ALU.mult))
                    rot_ready.need(dve, turn, c + 1)

                for c in range(C):
                    sq_ready.need(dve, turn, c + 1)
                    own(dve.tensor_reduce(ss[:, c % 2], square[:, c % 2], AX_X, ALU.add))
                    ss_ready.mark(dve.tensor_scalar(ss[:, c % 2], ss[:, c % 2], 1e-24, None, ALU.max))
                    q = bank[3 * (c % 2)][:].rearrange("p (h e) -> p h e", h=H)
                    dve.tensor_tensor(rot_cos[:, c % 2, 0], q, wide(tab_now[:, 0, c], 1, [P, H, HD]), ALU.mult)
                    dve.tensor_tensor(rot_sin[:, c % 2, 0, :, 0:HALF], q[:, :, HALF:HD],
                                      wide(tab_now[:, 1, c, 0:HALF], 1, [P, H, HALF]), ALU.mult)
                    q_parts.mark(dve.tensor_tensor(rot_sin[:, c % 2, 0, :, HALF:HD], q[:, :, 0:HALF],
                                                   wide(tab_now[:, 1, c, HALF:HD], 1, [P, H, HALF]), ALU.mult))
                    if c >= 1:
                        rotate(c - 1)
                q_parts.need(dve, turn, C)
                def row_shift(u):
                    of = bank[u % 2][:].rearrange("p (j t) -> p j t", j=PAIRS)
                    mm_s.need(dve, turn, u + 1)
                    if u >= 2:
                        exp_ready.need(dve, turn, u - 1)
                    own(dve.tensor_reduce(row_max[:, u % 2], of, AX_X, ALU.max))
                    max_ready.mark(dve.tensor_tensor(shifted_s[:, u % 2], of, wide(row_max[:, u % 2], 2, [P, PAIRS, P]), ALU.subtract))

                def divide(u):
                    c = u // 2
                    of = bank[4 + u % 2][:, 0:PAIRS * VW].rearrange("p (j t) -> p j t", j=PAIRS)
                    mm_pv.need(dve, turn, u + 1)
                    if c >= 2:
                        t_o.need(dve, turn, c - 1)
                    own(dve.reciprocal(inv_sum[:, u % 2], of[:, :, HD]))
                    o_ready.mark(dve.tensor_tensor(o_rows[:, c % 2, u % 2], of[:, :, 0:HD], wide(inv_sum[:, u % 2], 2, [P, PAIRS, HD]), ALU.mult))

                def add_o(c):
                    mm_o.need(dve, turn, c + 1)
                    mid_ready.mark(dve.tensor_tensor(xr[:, c], bank[7][:, 0:D], xr[:, c], ALU.add))

                def shifted_rows(g):
                    half_tiles = slice(4 * g, 4 * g + 4)
                    mid_ready.need(dve, turn, 4 * g + 4)
                    if g == 0:
                        dve.memset(sh[0:1, 0, HD:D], 0.0)
                    dve.tensor_copy(sh[:, half_tiles, 0:HD], xr[:, half_tiles, 0:HD])
                    dve.wait_ge(shifted[g], turn * 32 + 32)
                    own(dve.memset(apart[:, half_tiles], 0.0))
                    statistics(own, lambda c: sh[:, c], 1e-5, var_ready.mark, 4 * g, 4 * g + 4)

                def normalised_rows(g):
                    rstd_ready.need(dve, turn, g + 1)
                    normalise(hn, lambda c: sh[:, c], hn_ready, 4 * g, 4 * g + 4)

                def product(c):
                    gelu_ready.need(dve, turn, c + 1)
                    if c >= 2:
                        t_prod.need(dve, turn, c - 1)
                    prod_ready.mark(dve.tensor_tensor(prod[:, c % 2], bank[c % 2][:, 0:HID], gelu[:, c % 2], ALU.mult))

                for u in range(UNITS + 5):
                    if u < UNITS:
                        row_shift(u)
                    if u == 0:
                        rotate(C - 1)
                    if 2 <= u <= UNITS + 1:
                        divide(u - 2)
                    if u >= 5 and u % 2 == 1 and (u - 5) // 2 < C:
                        add_o((u - 5) // 2)
                    if u == UNITS - 2:
                        shifted_rows(0)
                    if u == UNITS - 1:
                        normalised_rows(0)
                shifted_rows(1)
                product(0)
                normalised_rows(1)
                for c in range(1, C + 2):
                    if c < C:
                        product(c)
                    if prefetch and c == 3:
                        prefetch(0)
                    if prefetch and c == 5:
                        prefetch(1)
                    if c >= 2:
                        d = c - 2
                        mm_2.need(dve, turn, d + 1)
                        end_ready.mark(dve.tensor_tensor(xr[:, d], bank[6 + d % 2][:, 0:D], xr[:, d], ALU.add))
                end_ready.need(dve, turn, C)
                for s in per_block:
                    s.close()

            def sequence(seq, last):
                def own_seq(ins):
                    seq_own.need(dve, seq, seq_own.mark(ins))

                def x_tile(c, later=0):
                    return xt[:, bass.ds((seq + later) % 2, 1), c].squeeze(1)

                def prefetch(part):
                    if part == 0:
                        dve.wait_ge(loaded, seq * 16 + 32)
                        statistics(own_seq, lambda c: x_tile(c, 1), 1e-5, in_var.mark)
                    else:
                        in_rstd.need(dve, seq + 1, 1)
                        own_seq(normalise(x_next, lambda c: x_tile(c, 1)))

                transformer(seq * DEPTH, None)
                tables(1)
                transformer(seq * DEPTH + 1, None if last else prefetch)
                dve.wait_ge(stored, seq * 16 + 1)
                own_seq(dve.tensor_copy(last_rows[:], xr[:]))
                if not last:
                    dve.tensor_copy(xr[:], x_next)
                    tables(0)
                statistics(own_seq, lambda c: last_rows[:, c], 1e-5, out_var.mark)
                out_rstd.need(dve, seq, 1)
                own_seq(normalise(last_rows, lambda c: last_rows[:, c]))
                for c in range(C):
                    out_ready.mark(dve.tensor_tensor(last_rows[:, c], last_rows[:, c], x_tile(c), ALU.add))
                if not last:
                    for s in (seq_own, in_var, out_var, out_ready):
                        s.close()

            def first(ins):
                first_own.need(dve, 0, first_own.mark(ins))

            dve.wait_ge(loaded, 16)
            statistics(first, lambda c: xt[:, 0, c], 1e-5, lambda ins: ins.then_inc(in_var.sem, 1))
            in_rstd.need(dve, 0, 1)
            seq_seen.mark(normalise(xr, lambda c: xt[:, 0, c]))
            seq_seen.need(dve, 0, 1)
            tables(0)
            with dve.Fori(0, B - 1) as seq:
                sequence(seq, False)
            sequence(B - 1, True)


SEG = 10
BLK = 2 * SEG
PAD = SEG - 1
BLOCKS = -(-(L + PAD) // BLK)
T_ALL = BLOCKS * BLK
TAPS1 = 4
LEAD = TAPS1 - 1 + 1


def scan_layer_rows(nc, x_in, rows_out, xnT, w, const):
    with ExitStack() as ctx:
        def sb(name, shape, dt=F32):
            return ctx.enter_context(nc.sbuf_tensor("c0_" + name, shape, dt))

        def steps(name, per):
            return Steps(nc, "c0_" + name, per)

        bank = [ctx.enter_context(nc.psum_tensor(f"c0_bank{n}", [P, 512], F32)) for n in range(2)]
        ident = sb("ident", [P, P])
        norm_w = sb("norm_w", [P, 1])
        minus_half = sb("minus_half", [P, C])
        xt = sb("xt", [P, 2, C, D])
        xn0 = sb("xn0", [P, C, D])
        xn = sb("xn", [P, C, D])
        sq = sb("sq", [P, C, D])
        stat = sb("stat", [P, C, 6])
        mean = sb("mean", [P, C])
        apart = sb("apart", [P, C])
        var = sb("var", [P, C])
        rstd = sb("rstd", [P, C])
        ssum = sb("ssum", [P, C])
        loaded_w = nc.alloc_semaphore("c0_loaded_w")
        loaded = nc.alloc_semaphore("c0_loaded")
        stored = nc.alloc_semaphore("c0_stored")
        pool_own = nc.alloc_semaphore("c0_pool_own")
        zeroed = nc.alloc_semaphore("c0_zeroed")
        vec = steps("vec", 4)
        var_ready = steps("var_ready", 2)
        xn0_ready = steps("xn0_ready", C)
        xn_ready = steps("xn_ready", C)
        ss_ready = steps("ss_ready", C)
        xnT_ready = steps("xnT_ready", 2)
        t_xn = steps("t_xn", 2)
        rstd_ready = steps("rstd_ready", 2)
        x_rows = x_in.rearrange("b (c p) d -> b p c d", p=P)
        o_rows = rows_out.rearrange("b (c p) d -> b p c d", p=P)
        loads = [(ident, const["ident"]), (norm_w, w["norm_w"])]
        W_LOADED = 16 * len(loads)
        block = ctx.enter_context(nc.Block())

        @block.sync
        def _(sp):
            for to, of in loads:
                sp.dma_start(to[:], of).then_inc(loaded_w, 16)
            sp.sem_inc(stored, 1)
            sp.dma_start(xt[:, 0], x_rows[0]).then_inc(loaded, 16)
            with sp.Fori(0, B - 1) as seq:
                xn0_ready.need(sp, seq, 1)
                sp.dma_start(xt[:, bass.ds((seq + 1) % 2, 1)].squeeze(1),
                             x_rows[bass.ds(seq + 1, 1)].squeeze(0)).then_inc(loaded, 16)
                xn0_ready.need(sp, seq, C)
                sp.dma_start(o_rows[bass.ds(seq, 1)].squeeze(0), xn0[:]).then_inc(stored, 16)
            xn0_ready.need(sp, B - 1, C)
            sp.dma_start(o_rows[B - 1], xn0[:]).then_inc(stored, 16)
            sp.wait_ge(stored, 16 * B + 1)

        @block.gpsimd
        def _(pool):
            pool.sem_inc(rstd_ready.sem, 1)
            pool.memset(minus_half[:], -0.5).then_inc(pool_own, 1)
            pool.wait_ge(pool_own, 1)
            with pool.Fori(0, B) as seq:
                for n in (1, 2):
                    var_ready.need(pool, seq, n)
                    rstd_ready.mark(pool.tensor_tensor(rstd[:], var[:], minus_half[:], ALU.pow))
            rstd_ready.close()

        @block.scalar
        def _(act):
            act.sem_inc(ss_ready.sem, 1)
            with act.Fori(0, B) as seq:
                for c in range(C):
                    xn0_ready.need(act, seq, c + 1)
                    ss_ready.mark(act.activation(sq[:, c], xn0[:, c], ACT.Square, accum_out=ssum[:, c:c + 1]))
            ss_ready.close()

        @block.tensor
        def _(pe):
            pe.sem_inc(t_xn.sem, 1)
            pe.wait_ge(loaded_w, W_LOADED)
            with pe.Fori(0, B) as seq:
                for g in range(2):
                    for q in range(4):
                        xn_ready.need(pe, seq, 4 * g + q + 1)
                        ins = pe.transpose(bank[g][:, q * P:(q + 1) * P], xn[:, 4 * g + q], ident[:])
                    t_xn.mark(ins)
            t_xn.close()

        @block.vector
        def _(dve):
            marks = (vec, var_ready, xn0_ready, xn_ready, xnT_ready)
            for s in marks:
                dve.sem_inc(s.sem, 1)
            dve.memset(xnT[:], 0.0).then_inc(zeroed, 1)
            dve.wait_ge(zeroed, 1)
            dve.wait_ge(loaded_w, W_LOADED)
            with dve.Fori(0, B) as seq:
                def own(ins):
                    vec.need(dve, seq, vec.mark(ins))

                dve.wait_ge(loaded, seq * 16 + 16)
                half = seq % 2
                for c in range(C):
                    ins = dve.bn_stats(stat[:, c], xt[:, bass.ds(half, 1), c].squeeze(1))
                own(ins)
                dve.tensor_tensor(mean[:], stat[:, :, 1], stat[:, :, 4], ALU.add)
                dve.tensor_tensor(apart[:], stat[:, :, 1], stat[:, :, 4], ALU.subtract)
                own(dve.scalar_tensor_tensor(var[:], stat[:, :, 2], D * 1e-5, stat[:, :, 5], ALU.add, ALU.add))
                dve.tensor_scalar(mean[:], mean[:], 0.5, None, ALU.mult)
                own(dve.scalar_tensor_tensor(apart[:], apart[:], 0.25, apart[:], ALU.mult, ALU.mult))
                var_ready.mark(dve.scalar_tensor_tensor(var[:], var[:], 1.0 / D, apart[:], ALU.mult, ALU.add))
                rstd_ready.need(dve, seq, 1)
                dve.wait_ge(stored, seq * 16 + 1)
                for c in range(C):
                    xn0_ready.mark(dve.tensor_scalar(xn0[:, c], xt[:, bass.ds(half, 1), c].squeeze(1), mean[:, c:c + 1],
                                                     rstd[:, c:c + 1], ALU.subtract, ALU.mult))
                ss_ready.need(dve, seq, C)
                var_ready.mark(dve.tensor_scalar(var[:], ssum[:], 1.0 / D, 1e-6, ALU.mult, ALU.add))
                rstd_ready.need(dve, seq, 2)
                for c in range(C):
                    xn_ready.mark(dve.tensor_scalar(xn[:, c], xn0[:, c], rstd[:, c:c + 1], None, ALU.mult))
                for g in range(2):
                    t_xn.need(dve, seq, g + 1)
                    xnT_ready.mark(dve.tensor_scalar(
                        xnT[:, bass.ds(seq, 1), LEAD + PAD + 512 * g:LEAD + PAD + 512 * (g + 1)].squeeze(1),
                        bank[g][:], norm_w[:, 0:1], None, ALU.mult))
                own(dve.memset(apart[:], 0.0))
            for s in marks:
                s.close()


def scan_layer_blocks(nc, xnT, spread, out_rows, w, const):
    NS, K = 16, 2
    ROWS = K * B * NS
    GRP = B // 2
    RING = 4
    DT_MID, DT_RAD = (0.1 + 0.001) / 2.0, (0.1 - 0.001) / 2.0
    with ExitStack() as ctx:
        def sb(name, shape, dt=F32):
            return ctx.enter_context(nc.sbuf_tensor("c1_" + name, shape, dt))

        def steps(name, per):
            return Steps(nc, "c1_" + name, per)

        bank = [ctx.enter_context(nc.psum_tensor(f"c1_bank{n}", [P, 512], F32)) for n in range(8)]
        w_x = sb("w_x", [D, K, P])
        w_gate = sb("w_gate", [D, K, P])
        taps = sb("taps", [P, TAPS1, K, P])
        w_conv = sb("w_conv", [D, TAPS1, K, P])
        w_dt = sb("w_dt", [P, K, K, P])
        w_bc = sb("w_bc", [P, K, 2, NS])
        w_out = sb("w_out", [P, K, D])
        conv_b = sb("conv_b", [P, K])
        b_dt = sb("b_dt", [P, K])
        a_log = sb("a_log", [P, K, NS])
        a_scale = sb("a_scale", [P, K, NS])
        d_col = sb("d_col", [P, K])
        d_diag = sb("d_diag", [P, K, P])
        ident = sb("ident", [P, P])
        ones = sb("ones", [P, P])
        dt_shift = sb("dt_shift", [P, 1])
        dt_mid = sb("dt_mid", [P, 1])
        half_pow = sb("half_pow", [P, B])
        xc = sb("xc", [P, RING, K, B, 1 + BLK])
        sg = sb("sg", [P, RING, K, B, BLK])
        soft = sb("soft", [P, K, B, BLK])
        dt = sb("dt", [P, K, B, BLK])
        dtx = sb("dtx", [P, 2, K, B, BLK])
        bc = sb("bc", [NS, 2, B, 2, SEG])
        rep = sb("rep", [P, 2, 2, B, 2, NS, SEG])
        decay = sb("decay", [P, 2, 2, ROWS, 1 + SEG])
        state = sb("state", [P, 2, 2, ROWS, 1 + SEG])
        sq = sb("sq", [P, K, B, NS])
        ssq = sb("ssq", [P, B])
        ssum = sb("ssum", [P, B])
        norm = sb("norm", [P, B])
        fac = sb("fac", [P, B])
        yg = sb("yg", [P, K, B, BLK])
        rows = sb("rows", [GRP * BLK, 2, D])

        loaded_w = nc.alloc_semaphore("c1_loaded_w")
        ready_w = nc.alloc_semaphore("c1_ready_w")
        a_ready = nc.alloc_semaphore("c1_a_ready")
        pool_own = nc.alloc_semaphore("c1_pool_own")
        spread_out = nc.alloc_semaphore("c1_spread_out")
        spread_in = [nc.alloc_semaphore(f"c1_spread_in{k}") for k in range(2)]
        stored = nc.alloc_semaphore("c1_stored")
        mm_x = steps("mm_x", 1)
        mm_dt = steps("mm_dt", 1)
        mm_norm = steps("mm_norm", 2)
        mm_y = steps("mm_y", 2)
        mm_out = steps("mm_out", 1)
        act_own = steps("act_own", 4)
        xc_ready = steps("xc_ready", 1)
        bc_ready = steps("bc_ready", 1)
        dt_ready = steps("dt_ready", 1)
        decay_ready = steps("decay_ready", 2)
        rows_ready = steps("rows_ready", 1)
        first_own = steps("first_own", 3)
        vec = steps("vec", 10)
        arg_ready = steps("arg_ready", 1)
        dtx_ready = steps("dtx_ready", 1)
        scan_ready = steps("scan_ready", 2)
        ssq_ready = steps("ssq_ready", 2)
        ssum_ready = steps("ssum_ready", 2)
        carried = steps("carried", 2)
        yg_ready = steps("yg_ready", 1)
        norm_ready = steps("norm_ready", 2)
        hc_ready = steps("hc_ready", 2)

        loads = [(w_x, w["W_xT"]), (w_gate, w["W_gateT"]), (taps, w["conv_w"].partition_broadcast(P)),
                 (w_dt, w["W_dtT"]), (w_bc, w["W_bcT"]), (w_out, w["W_outT"]), (conv_b, w["conv_b"]), (b_dt, w["b_dt"]),
                 (a_log, w["A_log"]), (d_col, w["D_col"]), (ident, const["ident"])]
        W_LOADED = 16 * len(loads)
        block = ctx.enter_context(nc.Block())

        def turns(eng, step):
            head = 2
            tail = 6
            for n in range(head):
                step(n, n % RING)
            with eng.Fori(0, (BLOCKS - head - tail) // RING) as four:
                for j in range(RING):
                    step(four * RING + (head + j), (head + j) % RING)
            for n in range(BLOCKS - tail, BLOCKS):
                step(n, n % RING)

        def there(blk):
            return not isinstance(blk, int) or 0 <= blk < BLOCKS

        def from_(blk, first):
            return not isinstance(blk, int) or blk >= first

        @block.sync
        def _(sp):
            for to, of in loads:
                sp.dma_start(to[:], of).then_inc(loaded_w, 16)
            sp.sem_inc(stored, 1)
            sp.sem_inc(spread_out, 1)

            def spread_bc(blk, k):
                if not there(blk):
                    return
                bc_ready.need(sp, blk, 1)
                for j in range(2):
                    sp.dma_start(spread[bass.ds(blk, 1), j].squeeze(0).rearrange("x n t -> n x t"),
                                 bc[:, j].rearrange("n b s t -> n (b s) t")).then_inc(spread_out, 16)
                sp.wait_ge(spread_out, blk * 32 + 33)
                if from_(blk, 2):
                    hc_ready.before(sp, blk, 2, 2)
                sp.dma_start(rep[:, k].rearrange("p j b s n t -> p (j b s n t)"),
                             spread[bass.ds(blk, 1)].squeeze(0).rearrange("j x n t -> (j x n t)").partition_broadcast(P)
                             ).then_inc(spread_in[k], 16)

            def store(blk):
                if not there(blk):
                    return
                rows_ready.need(sp, blk, 1)
                for g in range(2):
                    sp.dma_start(out_rows[g * GRP:(g + 1) * GRP, bass.ds(blk * BLK, BLK)], rows[:, g]).then_inc(stored, 16)

            def step(blk, j):
                store(blk - 1)
                spread_bc(blk + 2, j % 2)

            spread_bc(0, 0)
            spread_bc(1, 1)
            turns(sp, step)
            store(BLOCKS - 1)
            sp.wait_ge(stored, BLOCKS * 32 + 1)

        @block.gpsimd
        def _(pool):
            for s in (norm_ready, hc_ready):
                pool.sem_inc(s.sem, 1)
            pool.memset(half_pow[:], 0.5).then_inc(pool_own, 1)
            pool.wait_ge(pool_own, 1)

            def step(blk, j):
                k = j % 2
                for seg in range(2):
                    ssum_ready.need(pool, blk, seg + 1)
                    norm_ready.mark(pool.tensor_tensor(norm[:], ssum[:], half_pow[:], ALU.pow))
                    for q in range(K):
                        h = state[:, k, seg, q * B * NS:(q + 1) * B * NS, 0:SEG].rearrange("p (b n) t -> p b n t", b=B)
                        ins = pool.tensor_tensor(h, h, rep[:, k, 1, :, seg], ALU.mult)
                    hc_ready.mark(ins)
                norm_ready.close()
                hc_ready.close()

            turns(pool, step)

        @block.scalar
        def _(act):
            for s in (act_own, xc_ready, bc_ready, dt_ready, decay_ready, rows_ready):
                act.sem_inc(s.sem, 1)
            act.wait_ge(loaded_w, W_LOADED)
            act.activation(a_log[:], a_log[:], ACT.Tanh, scale=0.5 / (5.0 + 1e-8)).then_inc(a_ready, 1)
            act.wait_ge(a_ready, 1)
            act.activation(a_log[:], a_log[:], ACT.Exp, scale=10.0).then_inc(a_ready, 1)
            act.wait_ge(ready_w, 4)

            def gates(blk, j):
                if not there(blk):
                    return
                mm_x.need(act, blk, 1)
                if from_(blk, RING):
                    mm_y.before(act, blk, RING, 2)
                    yg_ready.before(act, blk, RING, 1)
                for q in range(K):
                    act.activation(xc[:, j, q], bank[0][:, q * B * (1 + BLK):(q + 1) * B * (1 + BLK)].rearrange("p (b t) -> p b t", b=B),
                                   ACT.Silu, bias=conv_b[:, q:q + 1])
                xc_ready.mark(act.activation(sg[:, j], bank[1][:, 0:K * B * BLK].rearrange("p (q b t) -> p q b t", q=K, b=B), ACT.Silu))
                xc_ready.close()

            def decays(blk, k):
                if not there(blk):
                    return
                act_own.need(act, blk, 2)
                act_own.n = 2
                n = act_own.mark(act.activation(soft[:], soft[:], ACT.Tanh, scale=0.5 / (DT_RAD + 1e-8), bias=dt_shift[:, 0:1]))
                act_own.need(act, blk, n)
                if from_(blk, 1):
                    dtx_ready.before(act, blk, 1, 1)
                dt_ready.mark(act.activation(dt[:], soft[:], ACT.Identity, scale=2.0 * DT_RAD, bias=dt_mid[:, 0:1]))
                dt_ready.need(act, blk, 1)
                dt_ready.close()
                if from_(blk, 2):
                    scan_ready.before(act, blk, 2, 2)
                d6 = decay[:, k].rearrange("p s (q b n) t -> p s q b n t", q=K, b=B)
                for q in range(K):
                    for n in range(NS):
                        ins = act.activation(d6[:, :, q, :, n, 1:1 + SEG], dt[:, q].rearrange("p b (s t) -> p s b t", s=2),
                                             ACT.Tanh, scale=a_scale[:, q, n:n + 1])
                act_own.need(act, blk, act_own.mark(ins))
                act_own.close()
                for seg in range(2):
                    part = decay[:, k, seg, :, 1:1 + SEG]
                    decay_ready.mark(act.activation(part, part, ACT.Exp, scale=16.0))
                decay_ready.close()

            def softplus(blk):
                if not there(blk):
                    return
                mm_dt.need(act, blk, 1)
                act.wait_ge(spread_out, blk * 32 + 1)
                act.activation(bc[:, 0], bank[3][0:NS, 0:B * BLK].rearrange("n (b s t) -> n b s t", b=B, s=2), ACT.Copy)
                bc_ready.mark(act.activation(bc[:, 1], bank[3][0:NS, 256:256 + B * BLK].rearrange("n (b s t) -> n b s t", b=B, s=2), ACT.Copy))
                bc_ready.close()
                arg_ready.need(act, blk, 1)
                act_own.need(act, blk, act_own.mark(act.activation(soft[:], soft[:], ACT.Exp)))
                act_own.mark(act.activation(soft[:], soft[:], ACT.Ln, bias=1.0))
                act_own.n = 0

            def out(blk):
                if not there(blk):
                    return
                mm_out.need(act, blk, 1)
                act.wait_ge(stored, blk * 32 + 1)
                rows_ready.mark(act.activation(rows[:], bank[6][0:GRP * BLK, 0:2 * D].rearrange("p (g n) -> p g n", g=2), ACT.Copy))
                rows_ready.close()

            def step(blk, j):
                gates(blk + 2, (j + 2) % RING)
                decays(blk + 1, (j + 1) % 2)
                softplus(blk + 2)
                out(blk - 1)

            gates(0, 0)
            softplus(0)
            gates(1, 1)
            decays(0, 0)
            softplus(1)
            turns(act, step)
            out(BLOCKS - 1)

        @block.tensor
        def _(pe):
            for s in (mm_x, mm_dt, mm_norm, mm_y, mm_out):
                pe.sem_inc(s.sem, 1)
            pe.wait_ge(loaded_w, W_LOADED)
            pe.wait_ge(ready_w, 4)

            def project(blk):
                if not there(blk):
                    return
                if from_(blk, 1):
                    xc_ready.before(pe, blk, 1, 1)
                for q in range(K):
                    for j in range(TAPS1):
                        pe.matmul(bank[0][:, q * B * (1 + BLK):(q + 1) * B * (1 + BLK)], w_conv[:, j, q],
                                  xnT[:, :, bass.ds(blk * BLK + j, 1 + BLK)], start=(j == 0), stop=(j == TAPS1 - 1))
                for q in range(K):
                    ins = pe.matmul(bank[1][:, q * B * BLK:(q + 1) * B * BLK], w_gate[:, q],
                                    xnT[:, :, bass.ds(blk * BLK + LEAD - 1, BLK)], start=True, stop=True)
                mm_x.mark(ins)
                mm_x.close()

            def inner(blk, j):
                if not there(blk):
                    return
                xc_ready.need(pe, blk, 1)
                if from_(blk, 1):
                    arg_ready.before(pe, blk, 1, 1)
                    bc_ready.before(pe, blk, 1, 1)
                for m in range(K):
                    for q in range(K):
                        pe.matmul(bank[2][:, m * B * BLK:(m + 1) * B * BLK], w_dt[:, q, m], xc[:, j, q, :, 1:1 + BLK],
                                  start=(q == 0), stop=(q == K - 1))
                for i in range(2):
                    for q in range(K):
                        ins = pe.matmul(bank[3][0:NS, i * 256:i * 256 + B * BLK], w_bc[:, q, i], xc[:, j, q, :, 1 - i:1 - i + BLK],
                                        start=(q == 0), stop=(q == K - 1))
                mm_dt.mark(ins)
                mm_dt.close()

            def norms(blk, seg):
                ssq_ready.need(pe, blk, seg + 1)
                mm_norm.mark(pe.matmul(bank[4][:, 0:B], ones[:], ssq[:], start=True, stop=True))

            def outputs(blk, j, seg):
                if not there(blk):
                    return
                hc_ready.need(pe, blk, seg + 1)
                if seg == 0 and from_(blk, 1):
                    yg_ready.before(pe, blk, 1, 1)
                s6 = state[:, j % 2, seg].rearrange("p (q b n) t -> p q n b t", q=K, b=B)
                for q in range(K):
                    to = bank[5][:, (q * 2 + seg) * B * SEG:(q * 2 + seg + 1) * B * SEG]
                    for n in range(NS):
                        pe.matmul(to, ident[:], s6[:, q, n, :, 0:SEG], start=(n == 0), stop=False)
                    ins = pe.matmul(to, d_diag[:, q], xc[:, j, q, :, seg * SEG:(seg + 1) * SEG], start=False, stop=True)
                mm_y.mark(ins)

            def project_out(blk):
                if not there(blk):
                    return
                yg_ready.need(pe, blk, 1)
                if from_(blk, 1):
                    rows_ready.before(pe, blk, 1, 1)
                for g in range(2):
                    for q in range(K):
                        ins = pe.matmul(bank[6][0:GRP * BLK, g * D:(g + 1) * D],
                                        yg[:, q, g * GRP:(g + 1) * GRP].rearrange("p b t -> p (b t)"), w_out[:, q],
                                        start=(q == 0), stop=(q == K - 1))
                mm_out.mark(ins)
                mm_out.close()

            def step(blk, j):
                norms(blk, 0)
                inner(blk + 2, (j + 2) % RING)
                outputs(blk - 1, (j - 1) % RING, 1)
                norms(blk, 1)
                project(blk + 3)
                project_out(blk - 1)
                outputs(blk, j, 0)
                mm_y.n = mm_norm.n = 0

            project(0)
            inner(0, 0)
            project(1)
            inner(1, 1)
            project(2)
            turns(pe, step)
            outputs(BLOCKS - 1, (BLOCKS - 1) % RING, 1)
            project_out(BLOCKS - 1)

        @block.vector
        def _(dve):
            for s in (arg_ready, dtx_ready, scan_ready, ssq_ready, ssum_ready, carried, yg_ready, first_own, vec):
                dve.sem_inc(s.sem, 1)
            dve.wait_ge(loaded_w, W_LOADED)
            for j in range(TAPS1):
                dve.tensor_tensor(w_conv[:, j], w_x[:], taps[:, j], ALU.mult)
            dve.memset(ones[:], 1.0)
            dve.memset(dt_shift[:], -DT_MID * 0.5 / (DT_RAD + 1e-8))
            dve.memset(dt_mid[:], DT_MID)
            for q in range(K):
                ins = dve.tensor_scalar(d_diag[:, q], ident[:], d_col[:, q:q + 1], None, ALU.mult)
            ins.then_inc(ready_w, 1)
            dve.wait_ge(a_ready, 2)
            dve.tensor_scalar(a_scale[:], a_log[:], -0.5 / (8.0 + 1e-8), None, ALU.mult).then_inc(ready_w, 1)
            for k in range(2):
                ins = dve.memset(decay[:, k, :, :, 0:1], 0.0)
            ins.then_inc(ready_w, 1)
            dve.memset(state[:, 0, 0, :, 0:1], 0.0).then_inc(ready_w, 1)
            dve.wait_ge(ready_w, 4)

            def argument(blk):
                if not there(blk):
                    return
                mm_dt.need(dve, blk, 1)
                if from_(blk, 1):
                    dt_ready.before(dve, blk, 1, 1)
                for q in range(K):
                    ins = dve.tensor_scalar(soft[:, q], bank[2][:, q * B * BLK:(q + 1) * B * BLK].rearrange("p (b t) -> p b t", b=B),
                                            b_dt[:, q:q + 1], 80.0, ALU.add, ALU.min)
                arg_ready.mark(ins)
                arg_ready.close()

            def times_x(blk, j):
                if not there(blk):
                    return
                dt_ready.need(dve, blk, 1)
                dtx_ready.mark(dve.tensor_tensor(dtx[:, j % 2], dt[:], xc[:, j, :, :, 1:1 + BLK], ALU.mult))
                dtx_ready.need(dve, blk, 1)
                dtx_ready.close()

            def inputs(blk, k, seg, own):
                if not there(blk):
                    return
                if seg == 0:
                    dve.wait_ge(spread_in[k], (blk - k) * 8 + 16)
                    if from_(blk, 2):
                        mm_y.before(dve, blk, 2, 1)
                for q in range(K):
                    to = state[:, k, seg, q * B * NS:(q + 1) * B * NS, 1:1 + SEG].rearrange("p (b n) t -> p b n t", b=B)
                    ins = dve.tensor_tensor(to, rep[:, k, 0, :, seg],
                                            wide(dtx[:, k, q, :, seg * SEG:(seg + 1) * SEG], 2, [P, B, NS, SEG]), ALU.mult)
                own(ins)

            def sums(blk, seg):
                mm_norm.need(dve, blk, seg + 1)
                ssum_ready.mark(dve.tensor_copy(ssum[:], bank[4][:, 0:B]))

            def segment(blk, k, seg, own):
                decay_ready.need(dve, blk, seg + 1)
                h = state[:, k, seg].rearrange("p r t -> p (r t)")
                scan_ready.mark(dve.tensor_tensor_scan(h, decay[:, k, seg].rearrange("p r t -> p (r t)"), h, 0.0, ALU.mult, ALU.add))
                scan_ready.need(dve, blk, seg + 1)
                last = state[:, k, seg, :, SEG:SEG + 1].rearrange("p (q b n) t -> p q b (n t)", q=K, b=B)
                own(dve.tensor_tensor(sq[:], last, last, ALU.mult))
                ssq_ready.mark(dve.tensor_reduce(ssq[:], sq[:].rearrange("p q b n -> p b q n"), AX_XY, ALU.add))

            def carry(blk, k, seg, own):
                norm_ready.need(dve, blk, seg + 1)
                own(dve.tensor_scalar(fac[:], norm[:], 1e-8, None, ALU.add))
                own(dve.reciprocal(fac[:], fac[:]))
                own(dve.tensor_scalar(fac[:], fac[:], 20.0, 1.0, ALU.mult, ALU.min))
                to = state[:, k, 1] if seg == 0 else state[:, 1 - k, 0]
                last = state[:, k, seg, :, SEG:SEG + 1].rearrange("p (q b n) t -> p q b (n t)", q=K, b=B)
                carried.mark(dve.tensor_tensor(to[:, :, 0:1].rearrange("p (q b n) t -> p q b (n t)", q=K, b=B), last,
                                               fac[:].unsqueeze(1).unsqueeze(3).to_broadcast([P, K, B, NS]), ALU.mult))
                carried.need(dve, blk, seg + 1)

            def gate(blk, j):
                if not there(blk):
                    return
                mm_y.need(dve, blk, 2)
                if from_(blk, 1):
                    mm_out.before(dve, blk, 1, 1)
                for q in range(K):
                    y = bank[5][:, q * B * BLK:(q + 1) * B * BLK].rearrange("p (s b t) -> p b s t", s=2, b=B)
                    ins = dve.tensor_tensor(yg[:, q].rearrange("p b (s t) -> p b s t", s=2), y,
                                            sg[:, j, q].rearrange("p b (s t) -> p b s t", s=2), ALU.mult)
                yg_ready.mark(ins)
                yg_ready.close()

            def step(blk, j):
                def own(ins):
                    vec.need(dve, blk, vec.mark(ins))

                k = j % 2
                segment(blk, k, 0, own)
                sums(blk, 0)
                inputs(blk, k, 1, own)
                carry(blk, k, 0, own)
                segment(blk, k, 1, own)
                argument(blk + 2)
                sums(blk, 1)
                times_x(blk + 1, (j + 1) % RING)
                inputs(blk + 1, 1 - k, 0, own)
                gate(blk - 1, (j - 1) % RING)
                if there(blk + 1):
                    carry(blk, k, 1, own)
                    for s in (vec, scan_ready, ssq_ready, ssum_ready, carried):
                        s.close()

            def first(ins):
                first_own.need(dve, 0, first_own.mark(ins))

            argument(0)
            argument(1)
            times_x(0, 0)
            first(dve.memset(dtx[:, 0, :, :, 0:PAD], 0.0))
            inputs(0, 0, 0, first)
            turns(dve, step)
            gate(BLOCKS - 1, (BLOCKS - 1) % RING)


def scan_layer_end(nc, x_in, rows_in, out_rows, x_out, w, const):
    with ExitStack() as ctx:
        def sb(name, shape, dt=F32):
            return ctx.enter_context(nc.sbuf_tensor("c2_" + name, shape, dt))

        def steps(name, per):
            return Steps(nc, "c2_" + name, per)

        res = sb("res", [P, 1])
        minus_half = sb("minus_half", [P, C])
        xt = sb("xt", [P, 2, 3, C, D])
        os = sb("os", [P, C, D])
        on = sb("on", [P, C, D])
        stat = sb("stat", [P, C, 6])
        mean = sb("mean", [P, C])
        apart = sb("apart", [P, C])
        var = sb("var", [P, C])
        rstd = sb("rstd", [P, C])
        loaded_w = nc.alloc_semaphore("c2_loaded_w")
        loaded = nc.alloc_semaphore("c2_loaded")
        stored = nc.alloc_semaphore("c2_stored")
        own_w = nc.alloc_semaphore("c2_own_w")
        own_w2 = nc.alloc_semaphore("c2_own_w2")
        pool_own = nc.alloc_semaphore("c2_pool_own")
        vec = steps("vec", 5)
        seen = steps("seen", 1)
        var_ready = steps("var_ready", 1)
        out_ready = steps("out_ready", C)
        rstd_ready = steps("rstd_ready", 1)
        views = [x_in.rearrange("b (c p) d -> b p c d", p=P), rows_in.rearrange("b (c p) d -> b p c d", p=P),
                 out_rows[:, SEG:SEG + L].rearrange("b (c p) d -> b p c d", p=P)]
        o_rows = x_out.rearrange("b (c p) d -> b p c d", p=P)
        block = ctx.enter_context(nc.Block())

        @block.sync
        def _(sp):
            sp.dma_start(res[:], w["residual_scale"].partition_broadcast(P)).then_inc(loaded_w, 16)
            sp.sem_inc(stored, 1)
            for j in range(3):
                sp.dma_start(xt[:, 0, j], views[j][0]).then_inc(loaded, 16)
            with sp.Fori(0, B - 1) as seq:
                seen.need(sp, seq, 1)
                for j in range(3):
                    sp.dma_start(xt[:, bass.ds((seq + 1) % 2, 1), j].squeeze(1),
                                 views[j][bass.ds(seq + 1, 1)].squeeze(0)).then_inc(loaded, 16)
                out_ready.need(sp, seq, C)
                sp.dma_start(o_rows[bass.ds(seq, 1)].squeeze(0), on[:]).then_inc(stored, 16)
            out_ready.need(sp, B - 1, C)
            sp.dma_start(o_rows[B - 1], on[:]).then_inc(stored, 16)
            sp.wait_ge(stored, 16 * B + 1)

        @block.gpsimd
        def _(pool):
            pool.sem_inc(rstd_ready.sem, 1)
            pool.memset(minus_half[:], -0.5).then_inc(pool_own, 1)
            pool.wait_ge(pool_own, 1)
            with pool.Fori(0, B) as seq:
                var_ready.need(pool, seq, 1)
                rstd_ready.mark(pool.tensor_tensor(rstd[:], var[:], minus_half[:], ALU.pow))
            rstd_ready.close()

        @block.scalar
        def _(act):
            act.wait_ge(loaded_w, 16)
            act.activation(res[:], res[:], ACT.Sigmoid).then_inc(own_w, 1)

        @block.vector
        def _(dve):
            marks = (vec, seen, var_ready, out_ready)
            for s in marks:
                dve.sem_inc(s.sem, 1)
            dve.wait_ge(own_w, 1)
            dve.tensor_scalar(res[:], res[:], 0.5, None, ALU.mult).then_inc(own_w2, 1)
            dve.wait_ge(own_w2, 1)
            with dve.Fori(0, B) as seq:
                def own(ins):
                    vec.need(dve, seq, vec.mark(ins))

                dve.wait_ge(loaded, seq * 48 + 48)
                now = xt[:, bass.ds(seq % 2, 1)].squeeze(1)
                seen.mark(dve.scalar_tensor_tensor(os[:], now[:, 2], res[:, 0:1], now[:, 1], ALU.mult, ALU.add))
                seen.need(dve, seq, 1)
                for c in range(C):
                    ins = dve.bn_stats(stat[:, c], os[:, c])
                own(ins)
                dve.tensor_tensor(mean[:], stat[:, :, 1], stat[:, :, 4], ALU.add)
                dve.tensor_tensor(apart[:], stat[:, :, 1], stat[:, :, 4], ALU.subtract)
                own(dve.scalar_tensor_tensor(var[:], stat[:, :, 2], D * 1e-5, stat[:, :, 5], ALU.add, ALU.add))
                dve.tensor_scalar(mean[:], mean[:], 0.5, None, ALU.mult)
                own(dve.scalar_tensor_tensor(apart[:], apart[:], 0.25, apart[:], ALU.mult, ALU.mult))
                var_ready.mark(dve.scalar_tensor_tensor(var[:], var[:], 1.0 / D, apart[:], ALU.mult, ALU.add))
                rstd_ready.need(dve, seq, 1)
                for c in range(C):
                    ins = dve.tensor_scalar(os[:, c], os[:, c], mean[:, c:c + 1], rstd[:, c:c + 1], ALU.subtract, ALU.mult)
                own(ins)
                dve.wait_ge(stored, seq * 16 + 1)
                for c in range(C):
                    out_ready.mark(dve.tensor_tensor(on[:, c], os[:, c], now[:, 0, c], ALU.add))
                own(dve.memset(apart[:], 0.0))
            for s in marks:
                s.close()


def scan_layer(nc, x_in, rows, spread, out_rows, x_out, w, const):
    with ExitStack() as ctx:
        xnT = ctx.enter_context(nc.sbuf_tensor("c_xnT", [D, B, LEAD + T_ALL], F32))
        scan_layer_rows(nc, x_in, rows, xnT, w, const)
        scan_layer_blocks(nc, xnT, spread, out_rows, w, const)
    scan_layer_end(nc, x_in, rows, out_rows, x_out, w, const)


def expert_layer(nc, x_in, x_out, w, const):
    E, W = 8, 128
    with ExitStack() as ctx:
        def sb(name, shape, dt=F32):
            return ctx.enter_context(nc.sbuf_tensor("d_" + name, shape, dt))

        def steps(name, per):
            return Steps(nc, "d_" + name, per)

        bank = [ctx.enter_context(nc.psum_tensor(f"d_bank{n}", [P, 512], F32)) for n in range(8)]
        w1 = sb("w1", [D, E, W])
        w2 = sb("w2", [W, E, D])
        router = sb("router", [D, E])
        ident = sb("ident", [P, P])
        number = sb("number", [P, E])
        minus_half = sb("minus_half", [P, C])
        xt = sb("xt", [P, 2, C, D])
        xn0 = sb("xn0", [P, C, D])
        xn = sb("xn", [P, C, D])
        stat = sb("stat", [P, C, 6])
        mean = sb("mean", [P, C])
        apart = sb("apart", [P, C])
        var = sb("var", [P, C])
        rstd = sb("rstd", [P, C])
        xnT = sb("xnT", [D, L])
        probs = sb("probs", [P, C, E])
        top = sb("top", [P, C, E])
        top_at = sb("top_at", [P, C, E], U32)
        top_no = sb("top_no", [P, C, 2])
        total = sb("total", [P, C])
        share = sb("share", [P, C, 2])
        picked = sb("picked", [P, 2, C, E])
        gate = sb("gate", [P, C, E])
        relu = sb("relu", [W, 2, 512])
        hid = sb("hid", [W, 2, E, 512])
        acc = sb("acc", [P, C, D])
        yo = sb("yo", [P, C, D])

        loaded_w = nc.alloc_semaphore("d_loaded_w")
        loaded = nc.alloc_semaphore("d_loaded")
        stored = nc.alloc_semaphore("d_stored")
        pool_own = nc.alloc_semaphore("d_pool_own")
        vec = steps("vec", 71)
        var_ready = steps("var_ready", 2)
        xn_ready = steps("xn_ready", C)
        y_read = steps("y_read", C)
        out_ready = steps("out_ready", C)
        xnT_ready = steps("xnT_ready", 2)
        probs_ready = steps("probs_ready", 1)
        relu_ready = steps("relu_ready", 2 * E)
        t_xn = steps("t_xn", 2)
        mm_router = steps("mm_router", 1)
        mm_hid = steps("mm_hid", 2 * E)
        mm_y = steps("mm_y", C)
        rstd_ready = steps("rstd_ready", 2)
        hid_ready = steps("hid_ready", 2 * E)

        x_rows = x_in.rearrange("b (c p) d -> b p c d", p=P)
        o_rows = x_out.rearrange("b (c p) d -> b p c d", p=P)
        loads = [(w1, w["w1"].rearrange("d (e n) -> d e n", e=E)),
                 (w2, w["w2"].rearrange("(e n) d -> n e d", e=E)),
                 (router, w["routerT"]), (ident, const["ident"]),
                 (number, const["expert_no"].partition_broadcast(P))]
        W_LOADED = 16 * len(loads)
        block = ctx.enter_context(nc.Block())

        @block.sync
        def _(sp):
            for to, of in loads:
                sp.dma_start(to[:], of).then_inc(loaded_w, 16)
            sp.sem_inc(stored, 1)
            sp.dma_start(xt[:, 0], x_rows[0]).then_inc(loaded, 16)
            with sp.Fori(0, B - 1) as seq:
                xn_ready.need(sp, seq, 1)
                sp.dma_start(xt[:, bass.ds((seq + 1) % 2, 1)].squeeze(1),
                             x_rows[bass.ds(seq + 1, 1)].squeeze(0)).then_inc(loaded, 16)
                out_ready.need(sp, seq, C)
                sp.dma_start(o_rows[bass.ds(seq, 1)].squeeze(0), yo[:]).then_inc(stored, 16)
            out_ready.need(sp, B - 1, C)
            sp.dma_start(o_rows[B - 1], yo[:]).then_inc(stored, 16)
            sp.wait_ge(stored, 16 * B + 1)

        @block.gpsimd
        def _(pool):
            for s in (rstd_ready, hid_ready):
                pool.sem_inc(s.sem, 1)
            pool.memset(minus_half[:], -0.5).then_inc(pool_own, 1)
            pool.wait_ge(pool_own, 1)
            with pool.Fori(0, B) as seq:
                def inverse_root(n):
                    var_ready.need(pool, seq, n)
                    rstd_ready.mark(pool.tensor_tensor(rstd[:], var[:], minus_half[:], ALU.pow))

                inverse_root(1)
                for n in range(2 * E):
                    g, e = divmod(n, E)
                    relu_ready.need(pool, seq, n + 1)
                    hid_ready.mark(pool.tensor_tensor(hid[:, g, e], relu[:, n % 2], relu[:, n % 2], ALU.mult))
                inverse_root(2)
            for s in (rstd_ready, hid_ready):
                s.close()

        @block.scalar
        def _(act):
            own = (xnT_ready, probs_ready, relu_ready)
            for s in own:
                act.sem_inc(s.sem, 1)
            with act.Fori(0, B) as seq:
                for g in range(2):
                    t_xn.need(act, seq, g + 1)
                    xnT_ready.mark(act.activation(xnT[:, 512 * g:512 * (g + 1)], bank[g][:], ACT.Copy))
                mm_router.need(act, seq, 1)
                probs_ready.mark(act.activation(probs[:], bank[2][:, 0:C * E].rearrange("p (c e) -> p c e", e=E),
                                                ACT.Sigmoid))
                for n in range(2 * E):
                    mm_hid.need(act, seq, n + 1)
                    if n >= 2:
                        hid_ready.need(act, seq, n - 1)
                    relu_ready.mark(act.activation(relu[:, n % 2], bank[n % 2][:], ACT.Relu))
            for s in own:
                s.close()

        @block.tensor
        def _(pe):
            own = (t_xn, mm_router, mm_hid, mm_y)
            for s in own:
                pe.sem_inc(s.sem, 1)
            pe.wait_ge(loaded_w, W_LOADED)
            with pe.Fori(0, B) as seq:
                for g in range(2):
                    for q in range(4):
                        xn_ready.need(pe, seq, 4 * g + q + 1)
                        ins = pe.transpose(bank[g][:, q * P:(q + 1) * P], xn0[:, 4 * g + q], ident[:])
                    t_xn.mark(ins)
                xnT_ready.need(pe, seq, 2)
                for c in range(C):
                    ins = pe.matmul(bank[2][:, c * E:(c + 1) * E], xnT[:, c * P:(c + 1) * P], router[:], start=True, stop=True)
                mm_router.mark(ins)

                def hidden(n):
                    g, e = divmod(n, E)
                    if n >= 2:
                        relu_ready.need(pe, seq, n - 1)
                    mm_hid.mark(pe.matmul(bank[n % 2][:], w1[:, e], xnT[:, 512 * g:512 * (g + 1)], start=True, stop=True))

                def experts_out(c):
                    if c % 4 == 0:
                        hid_ready.need(pe, seq, E * (c // 4 + 1))
                    if c >= 2:
                        y_read.need(pe, seq, c - 1)
                    for e in range(E):
                        ins = pe.matmul(bank[3 + 2 * (c % 2) + e // 4][:, (e % 4) * D:(e % 4 + 1) * D],
                                        hid[:, c // 4, e, (c % 4) * P:(c % 4 + 1) * P], w2[:, e], start=True, stop=True)
                    mm_y.mark(ins)

                for n in range(E):
                    hidden(n)
                for c in range(4):
                    hidden(E + 2 * c)
                    hidden(E + 2 * c + 1)
                    experts_out(c)
                for c in range(4, C):
                    experts_out(c)
            for s in own:
                s.close()

        @block.vector
        def _(dve):
            marks = (vec, var_ready, xn_ready, y_read, out_ready)
            for s in marks:
                dve.sem_inc(s.sem, 1)
            dve.wait_ge(loaded_w, W_LOADED)
            with dve.Fori(0, B) as seq:
                def own(ins):
                    vec.need(dve, seq, vec.mark(ins))

                rounds = [0]

                def normalise(to, of, eps, done=None):
                    for c in range(C):
                        ins = dve.bn_stats(stat[:, c], of(c))
                    own(ins)
                    dve.tensor_tensor(mean[:], stat[:, :, 1], stat[:, :, 4], ALU.add)
                    dve.tensor_tensor(apart[:], stat[:, :, 1], stat[:, :, 4], ALU.subtract)
                    own(dve.scalar_tensor_tensor(var[:], stat[:, :, 2], D * eps, stat[:, :, 5], ALU.add, ALU.add))
                    dve.tensor_scalar(mean[:], mean[:], 0.5, None, ALU.mult)
                    own(dve.scalar_tensor_tensor(apart[:], apart[:], 0.25, apart[:], ALU.mult, ALU.mult))
                    var_ready.mark(dve.scalar_tensor_tensor(var[:], var[:], 1.0 / D, apart[:], ALU.mult, ALU.add))
                    rounds[0] += 1
                    rstd_ready.need(dve, seq, rounds[0])
                    for c in range(C):
                        ins = dve.tensor_scalar(to[:, c], of(c), mean[:, c:c + 1], rstd[:, c:c + 1], ALU.subtract, ALU.mult)
                        if done:
                            done.mark(ins)
                    return ins

                dve.wait_ge(loaded, seq * 16 + 16)
                half = seq % 2
                normalise(xn0, lambda c: xt[:, bass.ds(half, 1), c].squeeze(1), 1e-5, done=xn_ready)
                probs_ready.need(dve, seq, 1)
                dve.memset(gate[:], 0.0)
                for c in range(C):
                    ins = dve.max(top[:, c], probs[:, c])
                own(ins)
                dve.memset(total[:], 0.0)
                for c in range(C):
                    ins = dve.max_index(top_at[:, c], top[:, c], probs[:, c])
                own(ins)
                own(dve.scalar_tensor_tensor(total[:], top[:, :, 0], 1e-20, top[:, :, 1], ALU.add, ALU.add))
                dve.tensor_copy(top_no[:], top_at[:, :, 0:2])
                own(dve.reciprocal(total[:], total[:]))
                own(dve.tensor_tensor(share[:], top[:, :, 0:2], wide(total[:], 2, [P, C, 2]), ALU.mult))
                for k in range(2):
                    ins = dve.tensor_tensor(picked[:, k], wide(number[:], 1, [P, C, E]),
                                            top_no[:, :, k:k + 1].to_broadcast([P, C, E]), ALU.is_equal)
                own(ins)
                for k in range(2):
                    ins = dve.tensor_tensor(picked[:, k], picked[:, k], share[:, :, k:k + 1].to_broadcast([P, C, E]), ALU.mult)
                own(ins)
                own(dve.tensor_tensor(gate[:], picked[:, 0], picked[:, 1], ALU.add))
                for c in range(C):
                    mm_y.need(dve, seq, c + 1)
                    for e in range(E):
                        of = bank[3 + 2 * (c % 2) + e // 4][:, (e % 4) * D:(e % 4 + 1) * D]
                        if e == 0:
                            own(dve.tensor_scalar(acc[:, c], of, gate[:, c, e:e + 1], None, ALU.mult))
                        else:
                            ins = dve.scalar_tensor_tensor(acc[:, c], of, gate[:, c, e:e + 1], acc[:, c], ALU.mult, ALU.add)
                            if e < E - 1:
                                own(ins)
                    y_read.mark(ins)
                y_read.need(dve, seq, C)
                own(normalise(xn, lambda c: acc[:, c], 1e-5))
                dve.wait_ge(stored, seq * 16 + 1)
                for c in range(C):
                    out_ready.mark(dve.tensor_tensor(yo[:, c], xn[:, c], xt[:, bass.ds(half, 1), c].squeeze(1), ALU.add))
            for s in marks:
                s.close()



def sandwich(nc, inputs, y):
    def scratch(name, shape):
        return nc.dram_tensor(name, shape, F32, kind="Internal").ap()

    def weights(prefix):
        return {n[len(prefix):]: ap for n, ap in inputs.items() if n.startswith(prefix)}

    after_mamba2, after_attention, after_scan = (scratch(n, [B, L, D]) for n in ("after_mamba2", "after_attention", "after_scan"))
    const = weights("const_")
    with nc.cleanup_on_exit():
        mamba2_layer(nc, inputs["x"], after_mamba2, weights("mamba2_"), const)
    with nc.cleanup_on_exit():
        attention_layer(nc, after_mamba2, after_attention, weights("attention_"), const)
    with nc.cleanup_on_exit():
        scan_layer(nc, after_attention, scratch("scan_rows", [B, L, D]), scratch("scan_spread", [BLOCKS, 2, 2 * B, 16, SEG]),
                   scratch("scan_out", [B, T_ALL, D]), after_scan, weights("scan_"), const)
    expert_layer(nc, after_scan, y, weights("expert_"), const)



def rotary_tables():
    import numpy as np
    n, window, width = L, 64, 64
    half = np.arange(0, width, 2, dtype=np.float32)
    inv_freq = (1 / np.float32(10000) ** (half / np.float32(width))).astype(np.float32)
    t = np.arange(n, dtype=np.float32)
    freqs = (t[:, None] * inv_freq).astype(np.float32).astype(np.float64)
    base = ((half + np.float32(0.4 * width)) / np.float32(1.4 * width)).astype(np.float32)
    scale = base.astype(np.float64) ** ((t - n // 2) / (window // 2))[:, None]
    freqs, scale = np.concatenate([freqs, freqs], 1), np.concatenate([scale, scale], 1)
    sign = np.repeat([-1.0, 1.0], width // 2)
    cos, sin = np.cos(freqs), np.sin(freqs) * sign
    tables = np.stack([cos * scale, sin * scale, cos / scale, sin / scale])
    return tables.reshape(4, C, P, width).transpose(2, 0, 1, 3).astype(np.float32)


def window_masks():
    import numpy as np
    i, j = np.arange(64)[:, None], np.arange(64)[None]
    own, before = j <= i, j >= i
    seen = np.stack([np.hstack([own, 0 * before]), np.hstack([own, before]), np.hstack([before, own])], 1)
    return np.where(np.concatenate([seen, seen]), 0, MASKED).astype(mybir.dt.np(BF16))


def layout(given):
    import numpy as np

    def halves(v):
        return v.reshape(2, P).T

    m, a, s, e = ({n[len(p):]: v for n, v in given.items() if n.startswith(p)}
                  for p in ("L0_attn_", "L0_ffn_", "L1_attn_", "L1_ffn_"))
    upper = np.triu(np.ones((P, P), np.float32))

    def swapped(v):
        return np.concatenate([v[:, 32:], v[:, :32]], 1)

    w_in = s["W_in"].T
    out = {
        "x": m["x"],
        "const_ident": np.eye(P, dtype=np.float32),
        "const_upper": upper,
        "const_mask_upper": ((1 - upper) * MASKED).astype(mybir.dt.np(BF16)),
        "const_rotary": rotary_tables(),
        "const_window_masks": window_masks(),
        "const_expert_no": np.arange(8, dtype=np.float32),
        "mamba2_in_projT": m["in_proj_w"].T,
        "mamba2_conv_w": m["conv_w"][:, 0, :].T,
        "mamba2_conv_b": m["conv_b"].reshape(1, -1),
        "mamba2_conv_b_cols": m["conv_b"][256:].reshape(2, 64).T,
        "mamba2_ln_wb": np.stack([m["ln_w"], m["ln_b"]], 1),
        "mamba2_dt_bias": m["dt_bias"],
        "mamba2_A_log": m["A_log"],
        "mamba2_D_skip": m["D_skip"],
        "mamba2_norm_w": halves(m["norm_w"]),
        "mamba2_out_projT": m["out_proj_w"].T,
        "attention_wqkv": a["wqkv"],
        "attention_wo": a["wo"],
        "attention_w1": a["w1"],
        "attention_b1": a["b1"],
        "attention_w2": a["w2"],
        "attention_b2": a["b2"],
        "attention_ln_gb": np.stack([a["ln_g"], a["ln_b"]], -1).transpose(1, 0, 2),
        "attention_qk_scales": np.stack([a["q_scale"], swapped(a["q_scale"]), a["k_scale"], swapped(a["k_scale"])], 1),
        "scan_norm_w": s["norm_w"][:, None],
        "scan_W_xT": w_in[:, :256].reshape(P, 2, P),
        "scan_W_gateT": w_in[:, 256:].reshape(P, 2, P),
        "scan_conv_w": s["conv_w"][:, 0, :].T.reshape(4, 2, P),
        "scan_conv_b": halves(s["conv_b"]),
        "scan_b_dt": halves(s["b_dt"]),
        "scan_W_dtT": s["W_dt"].T.reshape(2, P, 2, P).transpose(1, 0, 2, 3),
        "scan_W_bcT": np.stack([s["W_B"].T.reshape(2, P, 16), s["W_C"].T.reshape(2, P, 16)], 2).transpose(1, 0, 2, 3),
        "scan_A_log": s["A_log"].reshape(2, P, 16).transpose(1, 0, 2),
        "scan_D_col": halves(s["D_param"]),
        "scan_W_outT": s["W_out"].T.reshape(2, P, P).transpose(1, 0, 2),
        "scan_residual_scale": s["residual_scale"].reshape(1),
        "expert_w1": e["w1"],
        "expert_w2": e["w2"],
        "expert_routerT": e["router_w"].T,
    }
    return {n: np.ascontiguousarray(v) for n, v in out.items()}


def kernel(**inputs):
    import concourse.bacc as bacc
    import numpy as np
    from concourse.bass_utils import run_bass_kernel_spmd

    nc = bacc.Bacc("TRN2", target_bir_lowering=False, num_devices=1)
    arrays = layout({n: np.asarray(v) for n, v in inputs.items()})
    aps = {n: nc.dram_tensor("in_" + n, v.shape, mybir.dt.from_np(v.dtype), kind="ExternalInput").ap() for n, v in arrays.items()}
    y = nc.dram_tensor("out_y", [B, L, D], F32, kind="ExternalOutput").ap()
    sandwich(nc, aps, y)
    got = run_bass_kernel_spmd(nc, [{"in_" + n: v for n, v in arrays.items()}], core_ids=[0])
    return got.results[0]["out_y"]
```
